# Optimizing a Trainium2 kernel written in Bass

```python
import numpy as np
import jax
import jax.numpy as jnp

def _softmax(x, axis=-1):
    return jax.nn.softmax(x, axis=axis)
def _gelu(x):
    return jax.nn.gelu(x, approximate=True)
def _silu(x):
    return jax.nn.silu(x)
def _sigmoid(x):
    return jax.nn.sigmoid(x)
def _layernorm(x, axis=-1, eps=1e-5):
    m = jnp.mean(x, axis=axis, keepdims=True)
    v = jnp.var(x, axis=axis, keepdims=True)
    return (x - m) / jnp.sqrt(v + eps)
def _scatter_add(tgt, idx, src, axis=0):
    return tgt.at[idx].add(src)
def _segment_sum(src, seg, n):
    return jax.ops.segment_sum(src, seg, n)

kernel_name = 'mk_metaformer_d2_conv_nchw128_4486f7'

def setup_inputs(seed: int = 0):
    np.random.seed(seed)
    _w = jnp.asarray
    def _rec_inputs():
        import jax
        import jax.numpy as jnp
        _gk = jax.random.key(seed)
        x = -0.000125 + 0.9999 * jax.random.normal(jax.random.fold_in(_gk, 1), (4, 128, 256, 256), jnp.float32)
        return x
    x = _rec_inputs()
    def _L0_conv_setup():
        import jax, jax.numpy as jnp
        import numpy as np
        DIM = 128
        HEADS = 8
        HDIM = DIM // HEADS
        KS = 4
        START = KS // 2
        EPS = 1e-06

        def _to_seq(t, head=HEADS, d=HDIM):
            b, c, h, w = t.shape
            return t.reshape(b, head, d, h * w).transpose(0, 3, 1, 2)

        def _feature_map(t):
            return jax.nn.elu(t) + 1.0
        key = jax.random.key(seed)
        ks = jax.random.split(key, 7)
        B, H, W = (4, 256, 256)
        x = jax.random.normal(ks[0], (B, DIM, H, W), dtype=jnp.float32)
        s = 0.05
        q_w = jax.random.normal(ks[1], (DIM, DIM), dtype=jnp.float32) * s
        q_b = jax.random.normal(ks[2], (DIM,), dtype=jnp.float32) * s
        kv_w = jax.random.normal(ks[3], (2 * DIM, DIM), dtype=jnp.float32) * s
        kv_b = jax.random.normal(ks[4], (2 * DIM,), dtype=jnp.float32) * s
        proj_w = jax.random.normal(ks[5], (DIM, DIM), dtype=jnp.float32) * s
        proj_b = jax.random.normal(ks[6], (DIM,), dtype=jnp.float32) * s
        return {'x': x, 'q_w': q_w, 'q_b': q_b, 'kv_w': kv_w, 'kv_b': kv_b, 'proj_w': proj_w, 'proj_b': proj_b}
    _L0_conv_all = _L0_conv_setup()
    _L0_conv_in = {k: v for k, v in _L0_conv_all.items() if k in ('q_w', 'q_b', 'kv_w', 'kv_b', 'proj_w', 'proj_b', )}
    del _L0_conv_all

    def _L0_ffn_setup():
        import jax, jax.numpy as jnp
        import numpy as np
        BN_EPS = 1e-05
        key = jax.random.key(seed)
        k1, k2, k3 = jax.random.split(key, 3)
        B, T, I, H = (64, 2048, 128, 128)
        x = jax.random.normal(k1, (B, T, I), dtype=jnp.float32)
        W = jax.random.normal(k2, (H, I), dtype=jnp.float32) * (1.0 / np.sqrt(I))
        V = jnp.linalg.qr(jax.random.normal(k3, (H, H), dtype=jnp.float32))[0]
        gamma = jnp.ones((H,), dtype=jnp.float32)
        beta = jnp.zeros((H,), dtype=jnp.float32)
        return {'x': x, 'W': W, 'V': V, 'gamma': gamma, 'beta': beta}
    _L0_ffn_all = _L0_ffn_setup()
    _L0_ffn_in = {k: v for k, v in _L0_ffn_all.items() if k in ('W', 'V', 'gamma', 'beta', )}
    del _L0_ffn_all

    def _L1_conv_setup():
        import jax, jax.numpy as jnp
        import numpy as np
        LAMBD = 0.01

        def softshrink(v, lambd):
            return jnp.sign(v) * jnp.maximum(jnp.abs(v) - lambd, 0.0)

        def spectral_gating(y, w1, b1, w2, b2):
            B, C, H2, W2 = y.shape
            nb, bs = (w1.shape[1], w1.shape[2])
            f = jnp.fft.rfft2(y, axes=(2, 3), norm='ortho')
            Hh, Wf = (f.shape[2], f.shape[3])
            xb = f.reshape(B, nb, bs, Hh, Wf)
            xr, xi = (xb.real, xb.imag)
            o1r = jnp.einsum('bkihw,kio->bkohw', xr, w1[0]) - jnp.einsum('bkihw,kio->bkohw', xi, w1[1]) + b1[0][None, :, :, None, None]
            o1i = jnp.einsum('bkihw,kio->bkohw', xi, w1[0]) + jnp.einsum('bkihw,kio->bkohw', xr, w1[1]) + b1[1][None, :, :, None, None]
            o2r = jnp.einsum('bkihw,kio->bkohw', o1r, w2[0]) - jnp.einsum('bkihw,kio->bkohw', o1i, w2[1]) + b2[0][None, :, :, None, None]
            o2i = jnp.einsum('bkihw,kio->bkohw', o1i, w2[0]) + jnp.einsum('bkihw,kio->bkohw', o1r, w2[1]) + b2[1][None, :, :, None, None]
            o2r = softshrink(o2r, LAMBD)
            o2i = softshrink(o2i, LAMBD)
            g = (o2r + 1j * o2i).reshape(B, C, Hh, Wf)
            z = g * f
            out = jnp.fft.irfft2(z, s=(H2, W2), axes=(2, 3), norm='ortho')
            return out + y
        key = jax.random.key(seed)
        ks = jax.random.split(key, 5)
        B, C, H, W = (8, 128, 256, 256)
        nb, bs = (8, 16)
        scale = 0.02
        return {'x': jax.random.normal(ks[0], (B, C, H, W), dtype=jnp.float32), 'w1': scale * jax.random.normal(ks[1], (2, nb, bs, bs), dtype=jnp.float32), 'b1': scale * jax.random.normal(ks[2], (2, nb, bs), dtype=jnp.float32), 'w2': scale * jax.random.normal(ks[3], (2, nb, bs, bs), dtype=jnp.float32), 'b2': scale * jax.random.normal(ks[4], (2, nb, bs), dtype=jnp.float32)}
    _L1_conv_all = _L1_conv_setup()
    _L1_conv_in = {k: v for k, v in _L1_conv_all.items() if k in ('w1', 'b1', 'w2', 'b2', )}
    del _L1_conv_all

    def _L1_ffn_setup():
        import jax, jax.numpy as jnp
        import numpy as np
        B, S, D, E, H, O, K = (512, 2048, 128, 64, 512, 128, 8)
        key = jax.random.key(seed)
        k0, k1, k2, k3 = jax.random.split(key, 4)
        x = jax.random.normal(k0, (B, S, D), dtype=jnp.float32)
        gate_w = jax.random.normal(k1, (E, D), dtype=jnp.float32) * (1.0 / np.sqrt(D))
        gate_b = jnp.zeros((E,), dtype=jnp.float32)
        weight1 = jax.random.uniform(k2, (E, D + 1, H), dtype=jnp.float32, minval=-1.0, maxval=1.0) * (1.0 / np.sqrt(D + 1))
        weight2 = jax.random.uniform(k3, (E, H + 1, O), dtype=jnp.float32, minval=-1.0, maxval=1.0) * (1.0 / np.sqrt(H + 1))
        return {'x': x, 'gate_w': gate_w, 'gate_b': gate_b, 'weight1': weight1, 'weight2': weight2}
    _L1_ffn_all = _L1_ffn_setup()
    _L1_ffn_in = {k: v for k, v in _L1_ffn_all.items() if k in ('gate_w', 'gate_b', 'weight1', 'weight2', )}
    del _L1_ffn_all

    return {
        "x": x,
        "L0_conv_q_w": _L0_conv_in["q_w"],
        "L0_conv_q_b": _L0_conv_in["q_b"],
        "L0_conv_kv_w": _L0_conv_in["kv_w"],
        "L0_conv_kv_b": _L0_conv_in["kv_b"],
        "L0_conv_proj_w": _L0_conv_in["proj_w"],
        "L0_conv_proj_b": _L0_conv_in["proj_b"],
        "L0_ffn_W": _L0_ffn_in["W"],
        "L0_ffn_V": _L0_ffn_in["V"],
        "L0_ffn_gamma": _L0_ffn_in["gamma"],
        "L0_ffn_beta": _L0_ffn_in["beta"],
        "L1_conv_w1": _L1_conv_in["w1"],
        "L1_conv_b1": _L1_conv_in["b1"],
        "L1_conv_w2": _L1_conv_in["w2"],
        "L1_conv_b2": _L1_conv_in["b2"],
        "L1_ffn_gate_w": _L1_ffn_in["gate_w"],
        "L1_ffn_gate_b": _L1_ffn_in["gate_b"],
        "L1_ffn_weight1": _L1_ffn_in["weight1"],
        "L1_ffn_weight2": _L1_ffn_in["weight2"],
    }

def reference(x, L0_conv_q_w, L0_conv_q_b, L0_conv_kv_w, L0_conv_kv_b, L0_conv_proj_w, L0_conv_proj_b, L0_ffn_W, L0_ffn_V, L0_ffn_gamma, L0_ffn_beta, L1_conv_w1, L1_conv_b1, L1_conv_w2, L1_conv_b2, L1_ffn_gate_w, L1_ffn_gate_b, L1_ffn_weight1, L1_ffn_weight2):
    import jax
    import jax.numpy as jnp
    def _L0_conv_ref(x, q_w, q_b, kv_w, kv_b, proj_w, proj_b):
        import jax, jax.numpy as jnp
        import numpy as np
        DIM = 128
        HEADS = 8
        HDIM = DIM // HEADS
        KS = 4
        START = KS // 2
        EPS = 1e-06

        def _to_seq(t, head=HEADS, d=HDIM):
            b, c, h, w = t.shape
            return t.reshape(b, head, d, h * w).transpose(0, 3, 1, 2)

        def _feature_map(t):
            return jax.nn.elu(t) + 1.0
        b, c, h, w = x.shape
        q = jnp.einsum('oc,bchw->bohw', q_w, x) + q_b[None, :, None, None]
        xs = x[:, :, START::KS, START::KS]
        kv = jnp.einsum('oc,bchw->bohw', kv_w, xs) + kv_b[None, :, None, None]
        k, v = (kv[:, :DIM], kv[:, DIM:])
        Q = _feature_map(_to_seq(q))
        K = _feature_map(_to_seq(k))
        V = _to_seq(v)
        S = V.shape[1]
        Vn = V / S
        KV = jnp.einsum('nshd,nshv->nhdv', K, Vn)
        Z = 1.0 / (jnp.einsum('nlhd,nhd->nlh', Q, K.sum(axis=1)) + EPS)
        out = jnp.einsum('nlhd,nhdv,nlh->nlhv', Q, KV, Z) * S
        out = out.transpose(0, 2, 3, 1).reshape(b, DIM, h, w)
        out = jnp.einsum('oc,bchw->bohw', proj_w, out) + proj_b[None, :, None, None]
        return out

    def _L0_ffn_ref(x, W, V, gamma, beta):
        import jax, jax.numpy as jnp
        import numpy as np
        BN_EPS = 1e-05
        B, T, H = (x.shape[0], x.shape[1], W.shape[0])
        Wx = jnp.einsum('bti,hi->bth', x, W)
        flat = Wx.reshape(B * T, H)
        mean = jnp.mean(flat, axis=0)
        var = jnp.var(flat, axis=0)
        Wx = ((flat - mean) * jax.lax.rsqrt(var + BN_EPS) * gamma + beta).reshape(B, T, H)
        Vt = V.T

        def step(yt, wx_t):
            yt = jax.nn.sigmoid(wx_t + yt @ Vt)
            return (yt, yt)
        y0 = jnp.zeros((B, H), dtype=Wx.dtype)
        _, ys = jax.lax.scan(step, y0, jnp.swapaxes(Wx, 0, 1))
        return jnp.swapaxes(ys, 0, 1)

    def _L1_conv_ref(x, w1, b1, w2, b2):
        import jax, jax.numpy as jnp
        import numpy as np
        LAMBD = 0.01

        def softshrink(v, lambd):
            return jnp.sign(v) * jnp.maximum(jnp.abs(v) - lambd, 0.0)

        def spectral_gating(y, w1, b1, w2, b2):
            B, C, H2, W2 = y.shape
            nb, bs = (w1.shape[1], w1.shape[2])
            f = jnp.fft.rfft2(y, axes=(2, 3), norm='ortho')
            Hh, Wf = (f.shape[2], f.shape[3])
            xb = f.reshape(B, nb, bs, Hh, Wf)
            xr, xi = (xb.real, xb.imag)
            o1r = jnp.einsum('bkihw,kio->bkohw', xr, w1[0]) - jnp.einsum('bkihw,kio->bkohw', xi, w1[1]) + b1[0][None, :, :, None, None]
            o1i = jnp.einsum('bkihw,kio->bkohw', xi, w1[0]) + jnp.einsum('bkihw,kio->bkohw', xr, w1[1]) + b1[1][None, :, :, None, None]
            o2r = jnp.einsum('bkihw,kio->bkohw', o1r, w2[0]) - jnp.einsum('bkihw,kio->bkohw', o1i, w2[1]) + b2[0][None, :, :, None, None]
            o2i = jnp.einsum('bkihw,kio->bkohw', o1i, w2[0]) + jnp.einsum('bkihw,kio->bkohw', o1r, w2[1]) + b2[1][None, :, :, None, None]
            o2r = softshrink(o2r, LAMBD)
            o2i = softshrink(o2i, LAMBD)
            g = (o2r + 1j * o2i).reshape(B, C, Hh, Wf)
            z = g * f
            out = jnp.fft.irfft2(z, s=(H2, W2), axes=(2, 3), norm='ortho')
            return out + y
        B, C, H, W = x.shape
        bias = x
        xr = x.reshape(B, C, H // 2, 2, W // 2, 2)
        y = xr.max(axis=(3, 5)) + xr.mean(axis=(3, 5))
        y = spectral_gating(y, w1, b1, w2, b2)
        y = jax.image.resize(y, (B, C, H, W), method='bilinear')
        return y + bias

    def _L1_ffn_ref(x, gate_w, gate_b, weight1, weight2):
        import jax, jax.numpy as jnp
        import numpy as np
        B, S, D, E, H, O, K = (512, 2048, 128, 64, 512, 128, 8)
        Bn, Sn, Dn = x.shape
        logits = jnp.einsum('bsd,ed->bse', x, gate_w) + gate_b
        probs = jax.nn.softmax(logits, axis=1)
        vals, idx = jax.lax.top_k(probs.transpose(0, 2, 1), K)
        topv = vals.transpose(0, 2, 1)
        topi = idx.transpose(0, 2, 1)
        flat_idx = topi.reshape(Bn, K * E)
        gathered = jnp.take_along_axis(x, flat_idx[:, :, None], axis=1)
        gathered = gathered.reshape(Bn, K, E, Dn)
        pooled = jnp.einsum('bked,bke->bed', gathered, topv)
        ones = jnp.ones((E, Bn, 1), dtype=x.dtype)
        h = jnp.concatenate([pooled.transpose(1, 0, 2), ones], axis=-1)
        h = jax.nn.gelu(jnp.einsum('ebd,edh->ebh', h, weight1), approximate=False)
        h = jnp.concatenate([h, ones], axis=-1)
        out = jnp.einsum('ebh,eho->ebo', h, weight2)
        out = out.transpose(1, 0, 2)
        weighted = jnp.einsum('beo,bke->bkeo', out, topv).reshape(Bn, K * E, O)
        outputs = jnp.zeros((Bn, Sn, O), dtype=x.dtype)
        outputs = outputs.at[jnp.arange(Bn)[:, None], flat_idx].add(weighted)
        return outputs

    def _gn(v, G=32, eps=1e-5):
        B_, C_, H_, W_ = v.shape
        g = v.reshape(B_, G, C_ // G, H_, W_)
        m = jnp.mean(g, axis=(2, 3, 4), keepdims=True)
        s = jnp.var(g, axis=(2, 3, 4), keepdims=True)
        return ((g - m) / jnp.sqrt(s + eps)).reshape(v.shape)

    def _ln_c(v, eps=1e-6):
        m = jnp.mean(v, axis=1, keepdims=True)
        s = jnp.var(v, axis=1, keepdims=True)
        return (v - m) / jnp.sqrt(s + eps)

    def _ln_t(v, eps=1e-5):
        m = jnp.mean(v, axis=-1, keepdims=True)
        s = jnp.var(v, axis=-1, keepdims=True)
        return (v - m) / jnp.sqrt(s + eps)

    def _to_tokens(v):
        B_, C_, H_, W_ = v.shape
        return v.reshape(B_, C_, H_ * W_).transpose(0, 2, 1)
    def _from_tokens(t, like):
        B_, C_, H_, W_ = like.shape
        return t.transpose(0, 2, 1).reshape(B_, C_, H_, W_)

    x = x + _L0_conv_ref(_ln_c(x), L0_conv_q_w, L0_conv_q_b, L0_conv_kv_w, L0_conv_kv_b, L0_conv_proj_w, L0_conv_proj_b)
    t = _to_tokens(x)
    t = t + _L0_ffn_ref(_ln_t(t), L0_ffn_W, L0_ffn_V, L0_ffn_gamma, L0_ffn_beta)
    x = _from_tokens(t, x)
    x = x + _L1_conv_ref(_ln_c(x), L1_conv_w1, L1_conv_b1, L1_conv_w2, L1_conv_b2)
    t = _to_tokens(x)
    t = t + _L1_ffn_ref(_ln_t(t), L1_ffn_gate_w, L1_ffn_gate_b, L1_ffn_weight1, L1_ffn_weight2)
    x = _from_tokens(t, x)
    return x


_drawn_inputs = setup_inputs


def setup_inputs(seed=0):
    import zlib

    import numpy as np

    out = dict(_drawn_inputs(seed))
    spreads = {'L0_ffn_gamma': (1.0, 0.584), 'L0_ffn_beta': (0.0, 0.1), 'L1_ffn_gate_b': (0.0, 0.8)}
    factors = {'L0_conv_q_w': 8.0,
     'L0_conv_q_b': 64.0,
     'L0_conv_kv_w': 5.283,
     'L1_conv_b1': 52.982,
     'L1_conv_b2': 7.692,
     'L1_ffn_gate_w': 8.0,
     'L1_ffn_weight1': 8.0,
     'L1_ffn_weight2': 8.0}
    for name, (base, spread) in spreads.items():
        noise = np.random.default_rng([zlib.crc32(name.encode()), seed]).standard_normal(out[name].shape)
        drawn = base * np.exp(spread * noise) if base else spread * noise
        out[name] = jnp.asarray(drawn.astype(out[name].dtype))
    for name, factor in factors.items():
        out[name] = (out[name] * factor).astype(out[name].dtype)
    return out
```

```python
from contextlib import ExitStack

import numpy as np

import concourse.bass as bass
from concourse import mybir

F32 = mybir.dt.float32
I32 = mybir.dt.int32
U32 = mybir.dt.uint32
ALU = mybir.AluOpType
ACT = mybir.ActivationFunctionType
AX = mybir.AxisListType

B, C, H, W = 4, 128, 256, 256
TOK = H * W
TILE = 512
SUP = 8
PERIOD = 2 * SUP
STOK = SUP * TILE
TILES = B * TOK // TILE
PAIRS = TILES // PERIOD
SUPERS = TILES // SUP
CHUNK = TILE
CHUNKS = TOK // CHUNK
COLS = B * CHUNKS
WIN = 16
WINDOWS = CHUNK // WIN
GROUPS = B
HEADS = 8
KS = 4
EXPERTS, TOPK, HID = 64, 8, 512
PH = H // 2
NK = PH // 2 + 1
LAMBD = 0.01
SEAM_TOL = 1e-6


def locate(r, k, lag, tiles):
    turn, slot = r + (k - lag) // PERIOD, (k - lag) % PERIOD
    t = turn * PERIOD + slot
    if isinstance(t, int) and not 0 <= t < tiles:
        return None
    return turn, slot, t


def run_steps(eng, tiles, last_lag, step, peel=2):
    for r in range(peel):
        for k in range(PERIOD):
            step(r, k)
    with eng.Fori(peel, tiles // PERIOD) as r:
        for k in range(PERIOD):
            step(r, k)
    for k in range(last_lag):
        step(tiles // PERIOD, k)


def wait(eng, sem, value):
    if not isinstance(value, int) or value > 0:
        eng.wait_ge(sem, value)


def wait_alone(eng, sem, value, passed):
    eng.wait_ge(sem, value)
    eng.sem_inc(passed, 1)


def load_ln_and_exp(act):
    act.preload_act_table_set("natural_log_exp_and_others")


class Scope(ExitStack):

    def __init__(self, nc, phase):
        super().__init__()
        self.nc, self.phase, self.used = nc, phase, []

    def sb(self, name, shape, dt=F32):
        return self.enter_context(self.nc.sbuf_tensor(f"{self.phase}_{name}", shape, dt))

    def ps(self, name, shape=(128, TILE)):
        return self.enter_context(self.nc.psum_tensor(f"{self.phase}_{name}", list(shape), F32))

    def sem(self, name):
        self.used.append(self.enter_context(self.nc.semaphore(f"{self.phase}_{name}")))
        return self.used[-1]

    def block(self):
        self.callback(self.clear)
        return self.enter_context(self.nc.Block())

    def clear(self):
        with self.nc.Block() as block:
            @block.sync
            def _(sp):
                for sem in self.used:
                    sp.sem_clear(sem)

    def sems(self, names):
        return [self.sem(n) for n in names.split()]


def setup_phase(nc, d, g):
    with Scope(nc, "su") as s:
        raw = s.sb("raw", [128, 2 * C + EXPERTS])
        p = s.ps("p")
        loaded, mixed, kept, eps_set = s.sems("loaded mixed kept eps_set")
        block = s.block()

        @block.sync
        def _(sp):
            for dst, src in ((g["cen"][:], d["cen"]), (g["ones"][:], d["ones"]), (raw[:, 0:C], d["qT"]),
                             (raw[:, C:2 * C], d["WT"]), (raw[:, 2 * C:], d["gateT"]), (g["kvT"][:], d["kvT"]),
                             (g["kvb"][:], d["kvb"].to_broadcast([128, 2 * C])), (g["projT"][:], d["projT"]),
                             (g["VT"][:], d["VT"]), (g["cols"][:], d["cols"]), (g["mask"][:], d["mask"]),
                             (g["gateb"][:], d["gateb"]), (g["iden"][:], d["iden"])):
                sp.dma_start(dst, src).then_inc(loaded, 16)

        @block.tensor
        def _(pe):
            pe.wait_ge(loaded, 16 * 13)
            nc.tensor.matmul(p[:, 0:2 * C + EXPERTS], g["cen"][:], raw[:], start=True, stop=True).then_inc(mixed, 1)

        @block.vector
        def _(dve):
            nc.vector.memset(g["eps"][:, 0:1], 1e-6).then_inc(eps_set, 1)
            nc.vector.memset(g["eps"][:, 1:2], 1e-5).then_inc(eps_set, 1)
            dve.wait_ge(mixed, 1)
            nc.vector.tensor_copy(g["qcWcGc"][:], p[:, 0:2 * C + EXPERTS]).then_inc(kept, 1)
            dve.wait_ge(kept, 1)


def attention_sums(nc, d, g):
    tiles = B * (H // KS) * (W // KS) // TILE
    rows = TILE // (W // KS)
    x_rows = d["x"].rearrange("b c (i k) w -> c b k i w", k=KS)[:, :, KS // 2]
    with Scope(nc, "at") as s:
        x = s.sb("x", [128, 2, rows, W])
        sq = s.sb("sq", [128, 2, TILE])
        lnv = s.sb("lnv", [128, 2, TILE])
        rstd = s.sb("rstd", [128, 2, TILE])
        xn = s.sb("xn", [128, 2, TILE])
        kv = s.sb("kv", [128, 2, 4, 2 * C + 1])
        km = s.sb("km", [128, 2, 4, C])
        ke = s.sb("ke", [128, 2, 4, C])
        kf = s.sb("kf", [128, 2, 4, C])
        pxc = [s.ps("pxc0"), s.ps("pxc1")]
        pvar = s.ps("pvar")
        pkv = [s.ps("pkv0"), s.ps("pkv1")]
        pKV = [s.ps("pKV0"), s.ps("pKV1")]
        ones_set, centered, squared, var_ready, ln_ready, rstd_ready, normed = s.sems(
            "ones_set centered squared var_ready ln_ready rstd_ready normed")
        kv_ready, biased, clipped, exped, mapped, summed, kept = s.sems(
            "kv_ready biased clipped exped mapped summed kept")
        x_in = s.sems("x_in0 x_in1")
        block = s.block()

        @block.sync
        def _(sp):
            def step(r, k):
                if at := locate(r, k, 0, tiles):
                    turn, slot, t = at
                    wait(sp, centered, t - 1)
                    b, j = turn * 2 + slot // SUP, slot % SUP
                    sp.dma_start(x[:, slot % 2], x_rows[:, bass.ds(b, 1), j * rows:(j + 1) * rows]
                                 ).then_inc(x_in[slot % 2], 16)
            run_steps(sp, tiles, 0, step, peel=1)

        @block.tensor
        def _(pe):
            pe.wait_ge(ones_set, 1)

            def step(r, k):
                if at := locate(r, k, 0, tiles):
                    turn, slot, t = at
                    pe.wait_ge(x_in[slot % 2], turn * (8 * 16) + 16 * (slot // 2 + 1))
                    wait(pe, normed, t - 1)
                    nc.tensor.matmul(pxc[slot % 2][:], g["cen"][:], x[:, slot % 2, :, KS // 2::KS],
                                     start=True, stop=True).then_inc(centered, 1)
                if at := locate(r, k, 1, tiles):
                    turn, slot, t = at
                    pe.wait_ge(squared, t + 1)
                    wait(pe, ln_ready, t)
                    nc.tensor.matmul(pvar[:], g["ones"][:], sq[:, slot % 2], start=True, stop=True
                                     ).then_inc(var_ready, 1)
                if at := locate(r, k, 3, tiles):
                    turn, slot, t = at
                    pe.wait_ge(normed, t + 1)
                    wait(pe, biased, 2 * t)
                    for h in range(2):
                        for c in range(2):
                            m = nc.tensor.matmul(pkv[h][:, c * 2 * C:(c + 1) * 2 * C],
                                                 xn[:, slot % 2, (2 * h + c) * 128:(2 * h + c + 1) * 128],
                                                 g["kvT"][:], start=True, stop=True)
                        m.then_inc(kv_ready, 1)
                if at := locate(r, k, 5, tiles):
                    turn, slot, t = at
                    pe.wait_ge(mapped, t + 1)
                    if slot % 8 == 0:
                        wait(pe, kept, turn * 2 + slot // 8 - 1)
                    for c in range(4):
                        m = nc.tensor.matmul(pKV[slot // 8][:, 0:C + 1], kf[:, slot % 2, c],
                                             kv[:, slot % 2, c, C:2 * C + 1],
                                             start=(slot % 8 == 0 and c == 0), stop=(slot % 8 == 7 and c == 3))
                    m.then_inc(summed, 1)
            run_steps(pe, tiles, 6, step, peel=1)

        @block.scalar
        def _(act):
            load_ln_and_exp(act)
            def step(r, k):
                if at := locate(r, k, 0, tiles):
                    turn, slot, t = at
                    act.wait_ge(centered, t + 1)
                    wait(act, var_ready, t - 1)
                    nc.scalar.activation(sq[:, slot % 2], pxc[slot % 2][:], ACT.Square).then_inc(squared, 1)
                if at := locate(r, k, 1, tiles):
                    turn, slot, t = at
                    act.wait_ge(var_ready, t + 1)
                    nc.scalar.activation(lnv[:, slot % 2], pvar[:], ACT.Ln, bias=g["eps"][:, 0:1]).then_inc(ln_ready, 1)
                    act.wait_ge(ln_ready, t + 1)
                    wait(act, normed, t - 1)
                    nc.scalar.activation(rstd[:, slot % 2], lnv[:, slot % 2], ACT.Exp, scale=-0.5
                                         ).then_inc(rstd_ready, 1)
                if at := locate(r, k, 4, tiles):
                    turn, slot, t = at
                    act.wait_ge(clipped, t + 1)
                    wait(act, mapped, t - 1)
                    nc.scalar.activation(ke[:, slot % 2], km[:, slot % 2], ACT.Exp).then_inc(exped, 1)
            run_steps(act, tiles, 5, step, peel=1)

        @block.vector
        def _(dve):
            nc.vector.memset(kv[:, :, :, 2 * C:2 * C + 1], 1.0).then_inc(ones_set, 1)

            def step(r, k):
                if at := locate(r, k, 2, tiles):
                    turn, slot, t = at
                    dve.wait_ge(rstd_ready, t + 1)
                    wait(dve, kv_ready, 2 * t - 2)
                    nc.vector.tensor_tensor(xn[:, slot % 2], pxc[slot % 2][:], rstd[:, slot % 2], ALU.mult
                                            ).then_inc(normed, 1)
                if at := locate(r, k, 5, tiles):
                    turn, slot, t = at
                    dve.wait_ge(exped, t + 1)
                    wait(dve, summed, t - 1)
                    nc.vector.scalar_tensor_tensor(kf[:, slot % 2], kv[:, slot % 2, :, 0:C], 0.0, ke[:, slot % 2],
                                                   ALU.max, ALU.add).then_inc(mapped, 1)
                if at := locate(r, k, 3, tiles):
                    turn, slot, t = at
                    wait(dve, summed, t - 1)
                    for h in range(2):
                        dve.wait_ge(kv_ready, 2 * t + 1 + h)
                        for c in range(2):
                            m = nc.vector.tensor_tensor(kv[:, slot % 2, 2 * h + c, 0:2 * C],
                                                        pkv[h][:, c * 2 * C:(c + 1) * 2 * C], g["kvb"][:], ALU.add)
                        m.then_inc(biased, 1)
                    dve.wait_ge(biased, 2 * t + 2)
                    wait(dve, exped, t - 1)
                    nc.vector.tensor_scalar(km[:, slot % 2], kv[:, slot % 2, :, 0:C], 0.0, None, ALU.min
                                            ).then_inc(clipped, 1)
                at = locate(r, k, 6, tiles)
                if at and at[1] % 8 == 7:
                    turn, slot, t = at
                    dve.wait_ge(summed, t + 1)
                    for i in range(PAIRS // B):
                        at_turn = turn * (2 * PAIRS // B) + (slot // 8) * (PAIRS // B) + i
                        nc.vector.tensor_tensor(g["kvden"][:, bass.ds(at_turn * 2 * C, C)],
                                                pKV[slot // 8][:, 0:C], g["mask"][:], ALU.mult)
                        m = nc.vector.tensor_scalar(g["kvden"][:, bass.ds(at_turn * 2 * C + C, C)], g["mask"][:],
                                                    pKV[slot // 8][:, C:C + 1], None, ALU.mult)
                    m.then_inc(kept, 1)
            run_steps(dve, tiles, 7, step, peel=1)


def attention_pass(nc, d, g):
    x_t = d["x"].rearrange("b c h w -> c b (h w)")
    x1_s, wx_s = (d[n].rearrange("w p c -> p w c") for n in ("x1s", "wxs"))
    sup_cols = SUP * WIN
    with Scope(nc, "ap") as s:
        x = s.sb("x", [128, 2, STOK])
        x1 = s.sb("x1", [128, 2, WINDOWS, SUP, WIN])
        wx = s.sb("wx", [128, 2, WINDOWS, SUP, WIN])
        two = lambda n: s.sb(n, [128, 2, TILE])
        sq, lnv, rstd, qs, qe, qr, qf, lnd, zr, att, sq1, lnv1, rstd1 = map(
            two, "sq lnv rstd qs qe qr qf lnd zr att sq1 lnv1 rstd1".split())
        kvd = s.sb("kvd", [128, 2 * C])
        pc, pvar, pq, pden, pnum, ppr, pvar1, pw = map(s.ps, "pc pvar pq pden pnum ppr pvar1 pw".split())
        centered, squared, var_ready, ln_ready, rstd_ready = s.sems("centered squared var_ready ln_ready rstd_ready")
        q_ready, q_scaled, q_exped, q_mapped, kvd_ready = s.sems("q_ready q_scaled q_exped q_mapped kvd_ready")
        den_ready, num_ready, lnd_ready, z_ready, att_ready = s.sems(
            "den_ready num_ready lnd_ready z_ready att_ready")
        proj_ready, x1_ready, centered1, squared1, var1_ready = s.sems(
            "proj_ready x1_ready centered1 squared1 var1_ready")
        ln1_ready, rstd1_ready, w_ready, wx_ready, bn_done = s.sems(
            "ln1_ready rstd1_ready w_ready wx_ready bn_done")
        x_in, x1_out, wx_out = s.sems("x_in0 x_in1"), s.sems("x1_out0 x1_out1"), s.sems("wx_out0 wx_out1")
        bn_sums, bn_sq, bn_rs = s.sb("bn_ag", [128, 2]), s.sb("bn_sq", [128, 1]), s.sb("bn_rs", [128, 1])
        fold = s.sem("fold")
        block = s.block()

        def tile_of(buf, slot):
            return buf[:, slot // SUP, :, slot % SUP, :]

        @block.sync
        def _(sp):
            def load(turn, half):
                st = turn * 2 + half
                sp.dma_start(x[:, half], d["xflat"][:, bass.ds(st // (SUPERS // B), 1),
                                                    bass.ds(st % (SUPERS // B) * STOK, STOK)]
                             ).then_inc(x_in[half], 16)

            load(0, 0)
            load(0, 1)

            def turn_body(turn, more):
                for half in range(2):
                    st = turn * 2 + half
                    sp.wait_ge(x1_ready, SUP * (st + 1))
                    if more:
                        load(turn + 1, half)
                    sp.dma_start(x1_s[:, :, bass.ds(st * sup_cols, sup_cols)],
                                 x1[:, half].rearrange("p w j i -> p w (j i)")).then_inc(x1_out[half], 16)
                    sp.wait_ge(wx_ready, SUP * (st + 1))
                    sp.dma_start(wx_s[:, :, bass.ds(st * sup_cols, sup_cols)],
                                 wx[:, half].rearrange("p w j i -> p w (j i)")).then_inc(wx_out[half], 16)
            with sp.Fori(0, PAIRS - 1) as r:
                turn_body(r, True)
            turn_body(PAIRS - 1, False)
            for out in (*x1_out, *wx_out):
                sp.wait_ge(out, 16 * PAIRS)

        @block.gpsimd
        def _(pool):
            def body(turn):
                wait(pool, num_ready, turn * PERIOD)
                nc.gpsimd.tensor_copy(kvd[:], g["kvden"][:, bass.ds(turn * 2 * C, 2 * C)]).then_inc(kvd_ready, 1)
            body(0)
            with pool.Fori(1, PAIRS) as r:
                body(r)

        @block.tensor
        def _(pe):
            def step(r, k):
                mm = nc.tensor.matmul
                if at := locate(r, k, 0, TILES):
                    turn, slot, t = at
                    if slot % SUP == 0:
                        pe.wait_ge(x_in[slot // SUP], 16 * (turn + 1))
                    wait(pe, squared1, t - 6)
                    wait(pe, squared, t)
                    mm(pc[:], g["cen"][:], x[:, slot // SUP, (slot % SUP) * TILE:(slot % SUP + 1) * TILE],
                       start=True, stop=True).then_inc(centered, 1)
                if at := locate(r, k, 5, TILES):
                    turn, slot, t = at
                    pe.wait_ge(att_ready, t + 1)
                    wait(pe, x1_ready, t)
                    mm(ppr[:], g["projT"][:], att[:, slot % 2], start=True, stop=True).then_inc(proj_ready, 1)
                if at := locate(r, k, 1, TILES):
                    turn, slot, t = at
                    pe.wait_ge(squared, t + 1)
                    wait(pe, ln_ready, t)
                    mm(pvar[:], g["ones"][:], sq[:, slot % 2], start=True, stop=True).then_inc(var_ready, 1)
                if at := locate(r, k, 7, TILES):
                    turn, slot, t = at
                    pe.wait_ge(squared1, t + 1)
                    wait(pe, ln1_ready, t)
                    mm(pvar1[:], g["ones"][:], sq1[:, slot % 2], start=True, stop=True).then_inc(var1_ready, 1)
                if at := locate(r, k, 6, TILES):
                    turn, slot, t = at
                    pe.wait_ge(x1_ready, t + 1)
                    if locate(r, k, 0, TILES):
                        pe.wait_ge(squared, t + 7)
                    else:
                        pe.wait_ge(squared, TILES)
                    wait(pe, squared1, t)
                    mm(pc[:], g["cen"][:], tile_of(x1, slot), start=True, stop=True).then_inc(centered1, 1)
                if at := locate(r, k, 1, TILES):
                    turn, slot, t = at
                    wait(pe, q_scaled, t)
                    mm(pq[:], g["qcWcGc"][:, 0:C], x[:, slot // SUP, (slot % SUP) * TILE:(slot % SUP + 1) * TILE],
                       start=True, stop=True).then_inc(q_ready, 1)
                if at := locate(r, k, 7, TILES):
                    turn, slot, t = at
                    wait(pe, wx_ready, t)
                    mm(pw[:], g["qcWcGc"][:, C:2 * C], tile_of(x1, slot), start=True, stop=True).then_inc(w_ready, 1)
                if at := locate(r, k, 3, TILES):
                    turn, slot, t = at
                    if slot == 0:
                        pe.wait_ge(kvd_ready, turn + 1)
                    pe.wait_ge(q_mapped, t + 1)
                    wait(pe, lnd_ready, t)
                    mm(pden[:], kvd[:, C:2 * C], qf[:, slot % 2], start=True, stop=True).then_inc(den_ready, 1)
                    wait(pe, att_ready, t)
                    mm(pnum[:], kvd[:, 0:C], qf[:, slot % 2], start=True, stop=True).then_inc(num_ready, 1)
            run_steps(pe, TILES, 8, step)

        @block.scalar
        def _(act):
            load_ln_and_exp(act)
            a = nc.scalar.activation

            def step(r, k):
                if at := locate(r, k, 4, TILES):
                    turn, slot, t = at
                    act.wait_ge(den_ready, t + 1)
                    a(lnd[:, slot % 2], pden[:], ACT.Ln, bias=g["eps"][:, 0:1]).then_inc(lnd_ready, 1)
                    act.wait_ge(lnd_ready, t + 1)
                    wait(act, att_ready, t - 1)
                    a(zr[:, slot % 2], lnd[:, slot % 2], ACT.Exp, scale=-1.0).then_inc(z_ready, 1)
                if at := locate(r, k, 2, TILES):
                    turn, slot, t = at
                    act.wait_ge(q_scaled, t + 1)
                    wait(act, q_mapped, t - 1)
                    a(qe[:, slot % 2], qs[:, slot % 2], ACT.Exp, bias=g["cols"][:, 0:1])
                    a(qr[:, slot % 2], qs[:, slot % 2], ACT.Relu, bias=g["cols"][:, 0:1]).then_inc(q_exped, 1)
                if at := locate(r, k, 0, TILES):
                    turn, slot, t = at
                    act.wait_ge(centered, t + 1)
                    wait(act, var_ready, t - 1)
                    a(sq[:, slot % 2], pc[:], ACT.Square).then_inc(squared, 1)
                if at := locate(r, k, 1, TILES):
                    turn, slot, t = at
                    act.wait_ge(var_ready, t + 1)
                    a(lnv[:, slot % 2], pvar[:], ACT.Ln, bias=g["eps"][:, 0:1]).then_inc(ln_ready, 1)
                    act.wait_ge(ln_ready, t + 1)
                    wait(act, q_scaled, t - 1)
                    a(rstd[:, slot % 2], lnv[:, slot % 2], ACT.Exp, scale=-0.5).then_inc(rstd_ready, 1)
                if at := locate(r, k, 7, TILES):
                    turn, slot, t = at
                    act.wait_ge(var1_ready, t + 1)
                    a(lnv1[:, slot % 2], pvar1[:], ACT.Ln, bias=g["eps"][:, 1:2]).then_inc(ln1_ready, 1)
                    act.wait_ge(ln1_ready, t + 1)
                    wait(act, wx_ready, t - 1)
                    a(rstd1[:, slot % 2], lnv1[:, slot % 2], ACT.Exp, scale=-0.5).then_inc(rstd1_ready, 1)
                if at := locate(r, k, 6, TILES):
                    turn, slot, t = at
                    act.wait_ge(centered1, t + 1)
                    wait(act, var1_ready, t - 1)
                    a(sq1[:, slot % 2], pc[:], ACT.Square).then_inc(squared1, 1)
            run_steps(act, TILES, 8, step)
            act.wait_ge(fold, 1)
            a(bn_sq[:], bn_sums[:, 1:2], ACT.Ln, bias=g["eps"][:, 1:2]).then_inc(fold, 1)
            act.wait_ge(fold, 2)
            a(bn_rs[:], bn_sq[:], ACT.Exp, scale=-0.5).then_inc(fold, 1)

        @block.vector
        def _(dve):
            v = nc.vector

            def step(r, k):
                if at := locate(r, k, 2, TILES):
                    turn, slot, t = at
                    dve.wait_ge(rstd_ready, t + 1)
                    dve.wait_ge(q_ready, t + 1)
                    wait(dve, q_exped, t - 1)
                    v.tensor_tensor(qs[:, slot % 2], pq[:], rstd[:, slot % 2], ALU.mult).then_inc(q_scaled, 1)
                if at := locate(r, k, 3, TILES):
                    turn, slot, t = at
                    dve.wait_ge(q_exped, t + 1)
                    wait(dve, num_ready, t - 1)
                    v.scalar_tensor_tensor(qf[:, slot % 2], qe[:, slot % 2], 1.0, qr[:, slot % 2], ALU.min, ALU.add
                                           ).then_inc(q_mapped, 1)
                if at := locate(r, k, 4, TILES):
                    turn, slot, t = at
                    dve.wait_ge(z_ready, t + 1)
                    dve.wait_ge(num_ready, t + 1)
                    wait(dve, proj_ready, t - 1)
                    v.tensor_tensor(att[:, slot % 2], pnum[:], zr[:, slot % 2], ALU.mult).then_inc(att_ready, 1)
                if at := locate(r, k, 5, TILES):
                    turn, slot, t = at
                    dve.wait_ge(proj_ready, t + 1)
                    if slot % SUP == 0:
                        wait(dve, x1_out[slot // SUP], 16 * turn)
                        wait(dve, w_ready, t - SUP)
                    j = slot % SUP
                    v.scalar_tensor_tensor(
                        tile_of(x1, slot), ppr[:].rearrange("p (w i) -> p w i", i=WIN), g["cols"][:, 1:2],
                        x[:, slot // SUP, j * TILE:(j + 1) * TILE].rearrange("p (w i) -> p w i", i=WIN),
                        ALU.add, ALU.add).then_inc(x1_ready, 1)
                if at := locate(r, k, 8, TILES):
                    turn, slot, t = at
                    dve.wait_ge(rstd1_ready, t + 1)
                    dve.wait_ge(w_ready, t + 1)
                    if slot % SUP == 0:
                        wait(dve, wx_out[slot // SUP], 16 * turn)
                    v.tensor_tensor(tile_of(wx, slot), pw[:].rearrange("p (w i) -> p w i", i=WIN),
                                    rstd1[:, slot % 2].rearrange("p (w i) -> p w i", i=WIN), ALU.mult
                                    ).then_inc(wx_ready, 1)
                    dve.wait_ge(wx_ready, t + 1)
                    v.bn_stats(g["bn"][:, bass.ds(t * 6, 6)], tile_of(wx, slot)).then_inc(bn_done, 1)
            run_steps(dve, TILES, 9, step)
            dve.wait_ge(bn_done, TILES)
            v.bn_aggr(bn_sums[:], g["bn"][:]).then_inc(fold, 1)
            dve.wait_ge(fold, 3)
            v.tensor_tensor(g["bnss"][:, 0:1], bn_rs[:], g["cols"][:, 2:3], ALU.mult).then_inc(fold, 1)
            dve.wait_ge(fold, 4)
            v.tensor_tensor(g["bnss"][:, 2:3], bn_sums[:, 0:1], g["bnss"][:, 0:1], ALU.mult).then_inc(fold, 1)
            dve.wait_ge(fold, 5)
            v.tensor_tensor(g["bnss"][:, 1:2], g["cols"][:, 3:4], g["bnss"][:, 2:3], ALU.subtract).then_inc(fold, 1)
            dve.wait_ge(fold, 6)


def recurrence(nc, d, g):
    x1_w = d["x1s"]
    with Scope(nc, "rc") as s:
        wx = s.sb("wx", [128, 2, COLS, WIN])
        y = s.sb("y", [128, 2, COLS, WIN])
        x1 = s.sb("x1", [128, 2, COLS, WIN])
        seed = s.sb("seed", [128, B, CHUNKS])
        gap = s.sb("gap", [128, B, CHUNKS - 1])
        gmax, gall = s.sb("gmax", [128, 1]), s.sb("gall", [128, 1])
        again = s.sb("again", [128, 1], I32)
        pv = [s.ps(f"pv{i}") for i in range(GROUPS)]
        product_ready = s.sems(" ".join(f"product_ready{i}" for i in range(GROUPS)))
        sum_ready = s.sems(" ".join(f"sum_ready{i}" for i in range(GROUPS)))
        y_ready = s.sems(" ".join(f"y_ready{i}" for i in range(GROUPS)))
        wx_in, x1_in, x2_out = s.sems("wx_in0 wx_in1"), s.sems("x1_in0 x1_in1"), s.sems("x2_out0 x2_out1")
        warm_in, x2_ready, seeded, gap_ready, gmax_ready, gall_ready, again_ready = s.sems(
            "warm_in x2_ready seeded gap_ready gmax_ready gall_ready again_ready")
        passed = s.sem("passed")
        block = s.block()
        gcols = COLS // GROUPS
        half_windows = WINDOWS // 2
        seed_flat = seed[:].rearrange("p b c -> p (b c)")

        def reruns(eng, run):
            reg = eng.alloc_register("again_" + eng.engine.name)
            eng.wait_ge(again_ready, 1)
            eng.reg_load(reg, again[0:1, 0:1])
            with eng.Fori(1, CHUNKS) as p:
                with eng.If_ne(reg, 0):
                    run(p)
                    wait_alone(eng, again_ready, p + 1, passed)
                    eng.reg_load(reg, again[0:1, 0:1])
                with eng.Else():
                    eng.nop()

        def windows(eng, body):
            for half in range(2):
                body(0, half)
            with eng.Fori(1, half_windows) as q:
                for half in range(2):
                    body(q, half)

        def first_step(p, q, half):
            return WIN + p * CHUNK + q * (2 * WIN) + half * WIN

        @block.sync
        def _(sp):
            sp.dma_start(wx[:, 1].rearrange("p c i -> p (c i)"), d["wxs"][WINDOWS - 1]).then_inc(warm_in, 16)

            def load(dst, src, q, half, sem):
                sp.dma_start(dst[:, half].rearrange("p c i -> p (c i)"),
                             src[bass.ds(2 * q + half, 1)].rearrange("o p c -> (o p) c")).then_inc(sem[half], 16)

            def run(p):
                if isinstance(p, int):
                    load(wx, d["wxs"], 0, 0, wx_in)
                    load(x1, x1_w, 0, 0, x1_in)
                    load(x1, x1_w, 0, 1, x1_in)
                    for i in range(GROUPS):
                        sp.wait_ge(sum_ready[i], WIN)
                    load(wx, d["wxs"], 0, 1, wx_in)
                else:
                    for half in range(2):
                        sp.wait_ge(x2_out[half], 16 * half_windows * p)
                        load(wx, d["wxs"], 0, half, wx_in)
                        load(x1, x1_w, 0, half, x1_in)

                def body(q, half):
                    for i in range(GROUPS):
                        sp.wait_ge(sum_ready[i], first_step(p, q, half) + WIN)
                    load(wx, d["wxs"], q + 1, half, wx_in)
                    sp.wait_ge(x2_out[half], 16 * (half_windows * p + q + 1))
                    load(x1, x1_w, q + 1, half, x1_in)
                for half in range(2):
                    body(0, half)
                with sp.Fori(1, half_windows - 1) as q:
                    for half in range(2):
                        body(q, half)
            run(0)
            reruns(sp, run)

        @block.tensor
        def _(pe):
            def step(rhs, i, n):
                pe.wait_ge(y_ready[i], n) if not isinstance(n, int) or n else None
                nc.tensor.matmul(pv[i][:, 0:gcols], g["VT"][:], rhs, start=True, stop=True
                                 ).then_inc(product_ready[i], 1)

            def cols(i):
                return slice(i * gcols, (i + 1) * gcols)

            pe.wait_ge(seeded, 1)
            for k in range(WIN):
                for i in range(GROUPS):
                    step(y[:, 1, cols(i), k - 1] if k else seed_flat[:, cols(i)], i, k)

            def run(p):
                def body(q, half):
                    for k in range(WIN):
                        for i in range(GROUPS):
                            if k:
                                rhs = y[:, half, cols(i), k - 1]
                            elif half:
                                rhs = y[:, 0, cols(i), WIN - 1]
                            else:
                                rhs = seed_flat[:, cols(i)] if isinstance(q, int) else y[:, 1, cols(i), WIN - 1]
                            step(rhs, i, first_step(p, q, half) + k)
                pe.wait_ge(seeded, p + 2)
                windows(pe, body)
            run(0)
            reruns(pe, run)

        @block.vector
        def _(dve):
            v = nc.vector

            def step(half, k, i, n):
                dve.wait_ge(product_ready[i], n + 1)
                c = slice(i * gcols, (i + 1) * gcols)
                v.scalar_tensor_tensor(pv[i][:, 0:gcols], wx[:, half, c, k], g["bnss"][:, 0:1], pv[i][:, 0:gcols],
                                       ALU.mult, ALU.add).then_inc(sum_ready[i], 1)

            v.memset(seed[:], 0.0).then_inc(seeded, 1)
            dve.wait_ge(warm_in, 16)
            for k in range(WIN):
                for i in range(GROUPS):
                    step(1, k, i, k)
            ends = y[:, 1, :, WIN - 1].rearrange("p (b c) -> p b c", b=B)
            for i in range(GROUPS):
                dve.wait_ge(y_ready[i], WIN)
            v.tensor_copy(seed[:, :, 1:CHUNKS], ends[:, :, 0:CHUNKS - 1]).then_inc(seeded, 1)

            def run(p):
                def body(q, half):
                    dve.wait_ge(wx_in[half], 16 * (half_windows * p + q + 1))
                    for k in range(WIN):
                        for i in range(GROUPS):
                            step(half, k, i, first_step(p, q, half) + k)
                windows(dve, body)
                for i in range(GROUPS):
                    dve.wait_ge(y_ready[i], WIN + (p + 1) * CHUNK)
                v.tensor_tensor(gap[:], ends[:, :, 0:CHUNKS - 1], seed[:, :, 1:CHUNKS], ALU.subtract
                                ).then_inc(gap_ready, 1)
                dve.wait_ge(gap_ready, p + 1)
                v.tensor_reduce(gmax[:], gap[:], AX.XY, ALU.max, apply_absolute_value=True).then_inc(gmax_ready, 1)
                v.tensor_copy(seed[:, :, 1:CHUNKS], ends[:, :, 0:CHUNKS - 1]).then_inc(seeded, 1)
                dve.wait_ge(gall_ready, p + 1)
                v.tensor_scalar(again[:], gall[:], SEAM_TOL, None, ALU.is_gt).then_inc(again_ready, 1)
            run(0)
            reruns(dve, run)

        @block.scalar
        def _(act):
            def step(half, k, i, n):
                act.wait_ge(sum_ready[i], n + 1)
                nc.scalar.activation(y[:, half, i * gcols:(i + 1) * gcols, k], pv[i][:, 0:gcols], ACT.Sigmoid,
                                     bias=g["bnss"][:, 1:2]).then_inc(y_ready[i], 1)

            for k in range(WIN):
                for i in range(GROUPS):
                    step(1, k, i, k)

            def run(p):
                act.wait_ge(seeded, p + 2)

                def body(q, half):
                    wait(act, x2_ready, p * WINDOWS + 2 * q + half - 1)
                    for k in range(WIN):
                        for i in range(GROUPS):
                            step(half, k, i, first_step(p, q, half) + k)
                windows(act, body)
            run(0)
            reruns(act, run)

        @block.gpsimd
        def _(pool):
            def run(p):
                def body(q, half):
                    pool.wait_ge(x1_in[half], 16 * (half_windows * p + q + 1))
                    for i in range(GROUPS):
                        pool.wait_ge(y_ready[i], first_step(p, q, half) + WIN)
                    nc.gpsimd.tensor_tensor(x1[:, half], x1[:, half], y[:, half], ALU.add).then_inc(x2_ready, 1)
                    wait_alone(pool, x2_ready, p * WINDOWS + 2 * q + half + 1, passed)
                    pool.dma_start(d["x2s"][bass.ds(2 * q + half, 1)].rearrange("o p c -> (o p) c"),
                                   x1[:, half].rearrange("p c i -> p (c i)")).then_inc(x2_out[half], 16)
                windows(pool, body)
                wait_alone(pool, gmax_ready, p + 1, passed)
                nc.gpsimd.partition_all_reduce(gall[:], gmax[:], 128, bass.bass_isa.ReduceOp.max
                                               ).then_inc(gall_ready, 1)
                for half in range(2):
                    pool.wait_ge(x2_out[half], 16 * half_windows * (p + 1))
            run(0)
            reruns(pool, run)


def norm_and_pool(nc, d, g):
    x2_s = d["x2s"].rearrange("w p c -> p w c")
    sup_cols = SUP * WIN
    with Scope(nc, "np") as s:
        x2 = s.sb("x2", [128, 2, WINDOWS, SUP, WIN])
        xn = s.sb("xn", [128, 2, STOK])
        rr = s.sb("rr", [128, 2, STOK])
        sq, lnv, rstd = (s.sb(n, [128, 2, TILE]) for n in ("sq", "lnv", "rstd"))
        hmax, hsum = s.sb("hmax", [128, 2, SUP, W]), s.sb("hsum", [128, 2, SUP, W])
        pmax, psum_, yp = (s.sb(n, [128, 2, SUP, PH]) for n in ("pmax", "psum", "yp"))
        pc = [s.ps(f"pc{i}") for i in range(4)]
        pvar = [s.ps(f"pvar{i}") for i in range(2)]
        centered, squared, var_ready, ln_ready, rstd_ready, normed, r_ready = s.sems(
            "centered squared var_ready ln_ready rstd_ready normed r_ready")
        hmax_ready, hsum_ready, pooled, y_ready = s.sems("hmax_ready hsum_ready pooled y_ready")
        x2_in, r_out, y_out = s.sems("x2_in0 x2_in1"), s.sems("r_out0 r_out1"), s.sems("y_out0 y_out1")
        block = s.block()

        def tile_of(buf, slot):
            return buf[:, slot // SUP, :, slot % SUP, :]

        def line(buf, slot):
            return buf[:, slot // SUP, (slot % SUP) * TILE:(slot % SUP + 1) * TILE]

        @block.sync
        def _(sp):
            def load(st, half):
                sp.dma_start(x2[:, half].rearrange("p w j i -> p w (j i)"),
                             x2_s[:, :, bass.ds(st * sup_cols, sup_cols)]).then_inc(x2_in[half], 16)
            load(0, 0)
            load(1, 1)

            def turn_body(turn, more):
                for half in range(2):
                    st = turn * 2 + half
                    sp.wait_ge(r_ready, SUP * (st + 1))
                    sp.wait_ge(centered, SUP * (st + 1))
                    if more:
                        load(st + 2, half)
                    sp.dma_start(d["rs"][:, bass.ds(st * STOK, STOK)], rr[:, half]).then_inc(r_out[half], 16)
                    sp.wait_ge(y_ready, st + 1)
                    sp.dma_start(d["ys"][:, bass.ds(st * SUP * PH, SUP * PH)],
                                 yp[:, half].rearrange("p h w -> p (h w)")).then_inc(y_out[half], 16)
            with sp.Fori(0, PAIRS - 1) as r:
                turn_body(r, True)
            turn_body(PAIRS - 1, False)
            for out in (*r_out, *y_out):
                sp.wait_ge(out, 16 * PAIRS)

        @block.tensor
        def _(pe):
            def step(r, k):
                if at := locate(r, k, 0, TILES):
                    turn, slot, t = at
                    if slot % SUP == 0:
                        pe.wait_ge(x2_in[slot // SUP], 16 * (turn + 1))
                    wait(pe, normed, t - 3)
                    nc.tensor.matmul(pc[slot % 4][:], g["cen"][:], tile_of(x2, slot), start=True, stop=True
                                     ).then_inc(centered, 1)
                if at := locate(r, k, 1, TILES):
                    turn, slot, t = at
                    pe.wait_ge(squared, t + 1)
                    wait(pe, ln_ready, t - 1)
                    nc.tensor.matmul(pvar[slot % 2][:], g["ones"][:], sq[:, slot % 2], start=True, stop=True
                                     ).then_inc(var_ready, 1)
            run_steps(pe, TILES, 2, step)

        @block.scalar
        def _(act):
            load_ln_and_exp(act)
            a = nc.scalar.activation

            def step(r, k):
                if at := locate(r, k, 2, TILES):
                    turn, slot, t = at
                    act.wait_ge(var_ready, t + 1)
                    a(lnv[:, slot % 2], pvar[slot % 2][:], ACT.Ln, bias=g["eps"][:, 0:1]).then_inc(ln_ready, 1)
                if at := locate(r, k, 0, TILES):
                    turn, slot, t = at
                    act.wait_ge(centered, t + 1)
                    wait(act, var_ready, t - 1)
                    a(sq[:, slot % 2], pc[slot % 4][:], ACT.Square).then_inc(squared, 1)
                if at := locate(r, k, 2, TILES):
                    turn, slot, t = at
                    act.wait_ge(ln_ready, t + 1)
                    wait(act, normed, t - 1)
                    a(rstd[:, slot % 2], lnv[:, slot % 2], ACT.Exp, scale=-0.5).then_inc(rstd_ready, 1)
            run_steps(act, TILES, 3, step)

        @block.vector
        def _(dve):
            v = nc.vector

            def step(r, k):
                if at := locate(r, k, 3, TILES):
                    turn, slot, t = at
                    st = turn * 2 + slot // SUP
                    if slot % SUP == 0:
                        wait(dve, r_ready, t - SUP)
                        wait(dve, hsum_ready, st - 1)
                    dve.wait_ge(rstd_ready, t + 1)
                    v.tensor_tensor(line(xn, slot), pc[slot % 4][:], rstd[:, slot % 2], ALU.mult).then_inc(normed, 1)
                at = locate(r, k, 4, TILES)
                if at and at[1] % SUP == SUP - 1:
                    turn, slot, t = at
                    half, st = slot // SUP, turn * 2 + slot // SUP
                    rows = xn[:, half].rearrange("p (i two w) -> p i two w", two=2, w=W)
                    dve.wait_ge(normed, t + 1)
                    v.tensor_tensor(hmax[:, half], rows[:, :, 0], rows[:, :, 1], ALU.max).then_inc(hmax_ready, 1)
                at = locate(r, k, 6, TILES)
                if at and at[1] % SUP == SUP - 1:
                    turn, slot, t = at
                    half, st = slot // SUP, turn * 2 + slot // SUP
                    dve.wait_ge(hmax_ready, st + 1)
                    v.tensor_tensor(pmax[:, half], hmax[:, half, :, 0::2], hmax[:, half, :, 1::2], ALU.max
                                    ).then_inc(pooled, 1)
                    dve.wait_ge(hsum_ready, st + 1)
                    v.tensor_tensor(psum_[:, half], hsum[:, half, :, 0::2], hsum[:, half, :, 1::2], ALU.add
                                    ).then_inc(pooled, 1)
                    dve.wait_ge(pooled, 2 * st + 2)
                    wait(dve, y_out[half], 16 * turn)
                    v.scalar_tensor_tensor(yp[:, half], psum_[:, half], 0.25, pmax[:, half], ALU.mult, ALU.add
                                           ).then_inc(y_ready, 1)
            run_steps(dve, TILES, 7, step)

        @block.gpsimd
        def _(pool):
            def step(r, k):
                if at := locate(r, k, 3, TILES):
                    turn, slot, t = at
                    st = turn * 2 + slot // SUP
                    if slot % SUP == 0:
                        wait(pool, r_out[slot // SUP], 16 * turn)
                    pool.wait_ge(normed, t + 1)
                    nc.gpsimd.tensor_tensor(line(rr, slot).rearrange("p (w i) -> p w i", i=WIN),
                                            line(xn, slot).rearrange("p (w i) -> p w i", i=WIN),
                                            tile_of(x2, slot), ALU.add).then_inc(r_ready, 1)
                at = locate(r, k, 4, TILES)
                if at and at[1] % SUP == SUP - 1:
                    turn, slot, t = at
                    half, st = slot // SUP, turn * 2 + slot // SUP
                    rows = xn[:, half].rearrange("p (i two w) -> p i two w", two=2, w=W)
                    wait(pool, pooled, 2 * st - 2)
                    nc.gpsimd.tensor_tensor(hsum[:, half], rows[:, :, 0], rows[:, :, 1], ALU.add
                                            ).then_inc(hsum_ready, 1)
            run_steps(pool, TILES, 5, step)


def spectral(nc, d, g):
    n = PH
    last = n // 2
    fours = n // 4
    fpairs = (NK + 1) // 2
    with Scope(nc, "sg") as s:
        ya = s.sb("ya", [128, n * n])
        yb = s.sb("yb", [128, 2 * NK * n])
        q = s.sb("q", [128, n * n])
        work = s.sb("work", [128, 32 * n + 16])
        f = work[:, 0:8 * n].rearrange("p (j a) -> p j a", j=2)
        ge, gc = work[:, 8 * n:12 * n], work[:, 12 * n:16 * n]
        m1 = work[:, 16 * n + 16:24 * n + 16].rearrange("p (j u r k) -> p j u r k", j=2, u=2, r=2)
        m2 = work[:, 24 * n + 16:32 * n + 16].rearrange("p (j u r k) -> p j u r k", j=2, u=2, r=2)
        side = work[:, 0:8 * n].rearrange("p (j h w) -> p j h w", j=2, h=4)
        out = work[:, 8 * n:16 * n + 16].rearrange("p (j h w) -> p j h w", j=2, h=4)
        w12 = work[:, 16 * n + 16:24 * n + 16]
        dft = s.sb("dft", [128, 7 * n])
        mixm = s.sb("mixm", [128, 4 * n])
        bias = s.sb("bias", [128, 2, 2, n])
        pb = [s.ps(f"pb{i}") for i in range(8)]
        w_in, mix_ready, mix_kept, y_in = s.sems("w_in mix_ready mix_kept y_in")
        t_ready, rows_ready, f_ready, f_kept, mixed = s.sems("t_ready rows_ready f_ready f_kept mixed")
        t_kept, rows_kept, inv_kept = (s.sems(f"{x}_by_act {x}_by_dve") for x in ("t_kept", "rows_kept", "inv_kept"))
        g_done, prod_ready, z_ready, inv_ready, fin_ready, fin_kept, fin_done = s.sems(
            "g_done prod_ready z_ready inv_ready fin_ready fin_kept fin_done")
        side_in, y_out = s.sems("side_in0 side_in1"), s.sems("y_out0 y_out1")
        edge_out, passed, batch_free = s.sems("edge_out passed batch_free")
        block = s.block()
        RW, CS, SC, C_, S_, B1, B2 = (dft[:, a * n:b * n] for a, b in
                                      ((0, 1), (1, 3), (3, 5), (1, 2), (3, 4), (5, 6), (6, 7)))

        def re_slot(freq):
            return {0: 0, last: 1}.get(freq, 1 + freq)

        def im_slot(freq):
            return {0: 2 * last, last: 2 * last + 1}.get(freq, last + freq)

        @block.sync
        def _(sp):
            for dst, src in ((dft[:], d["dft"]), (w12, d["w12"])):
                sp.dma_start(dst, src).then_inc(w_in, 16)
            sp.wait_ge(mix_kept, 11)

            with sp.Fori(0, B) as b:
                sp.wait_ge(batch_free, b + 1)
                sp.dma_start(ya[:], d["ys"][:, bass.ds(b * (n * n), n * n)]).then_inc(y_in, 16)
                for i in range(fours + 2):
                    half = i % 2
                    if i >= 2:
                        sp.wait_ge(fin_done, b * fours + i - 1)
                        sp.dma_start(d["y2s"][:, bass.ds(b * (n + 2) + 4 * (i - 2) + 1, 4), :], out[:, half]
                                     ).then_inc(y_out[half], 16)
                        if i == 2:
                            sp.dma_start(d["y2s"][:, bass.ds(b * (n + 2), 1), :], out[:, 0, 0:1]
                                         ).then_inc(edge_out, 16)
                            wait_alone(sp, edge_out, b * 32 + 16, passed)
                        if i == fours + 1:
                            sp.dma_start(d["y2s"][:, bass.ds(b * (n + 2) + n + 1, 1), :], out[:, 1, 3:4]
                                         ).then_inc(edge_out, 16)
                            wait_alone(sp, edge_out, b * 32 + 32, passed)
                    if i < fours:
                        if i < 2:
                            sp.wait_ge(inv_ready, b * fours + 1)
                        else:
                            sp.wait_ge(fin_kept, b * fours + i - 1)
                        sp.dma_start(side[:, half], d["ys"][:, bass.ds(b * (n * n) + i * 4 * n, 4 * n)].rearrange(
                            "p (h w) -> p h w", h=4)).then_inc(side_in[half], 16)
                for half in range(2):
                    wait_alone(sp, y_out[half], b * (8 * fours) + 8 * fours, passed)

        @block.tensor
        def _(pe):
            mm = nc.tensor.matmul
            pe.wait_ge(w_in, 32)
            w1r, w1i, w2r, w2i, b1r, b1i = (w12[:, i * n:(i + 1) * n] for i in range(6))
            for j, (lr, li) in enumerate(((w1r, w1i), (b1r, b1i))):
                mm(pb[4 * j][:, 0:n], lr, w2r, start=True, stop=True)
                mm(pb[4 * j + 1][:, 0:n], li, w2i, start=True, stop=True)
                mm(pb[4 * j + 2][:, 0:n], lr, w2i, start=True, stop=False)
                mm(pb[4 * j + 2][:, 0:n], li, w2r, start=False, stop=True).then_inc(mix_ready, 1)
            pe.wait_ge(mix_kept, 11)

            with pe.Fori(0, B) as b:
                pe.wait_ge(y_in, b * 16 + 16)
                for i in range(fours):
                    if i >= 4:
                        pe.wait_ge(t_kept[i % 2], b * (fours // 2) + i // 2 - 1)
                    for h in range(4):
                        at = (4 * i + h) * n
                        m = nc.tensor.transpose(pb[i % 4][:, h * n:(h + 1) * n], ya[:, at:at + n], g["iden"][:])
                    m.then_inc(t_ready, 1)
                for e in range(2):
                    pe.wait_ge(t_kept[e], b * (fours // 2) + fours // 2)
                for i in range(fours):
                    if i >= 4:
                        pe.wait_ge(rows_kept[i % 2], b * (fours // 2) + i // 2 - 1)
                    for c in range(4):
                        m = mm(pb[4 + i % 4][:, c * n:(c + 1) * n], yb[:, 4 * i + c:n * n:n], RW, start=True, stop=True)
                    m.then_inc(rows_ready, 1)
                for e in range(2):
                    pe.wait_ge(rows_kept[e], b * (fours // 2) + fours // 2)
                for j in range(fpairs + 1):
                    if j < fpairs:
                        if j >= 2:
                            pe.wait_ge(f_kept, b * fpairs + j - 1)
                        for u, freq in enumerate(range(2 * j, min(2 * j + 2, NK))):
                            o = pb[j % 2][:, u * 2 * n:(u + 1) * 2 * n]
                            both = 0 < freq < last
                            m = mm(o, q[:, re_slot(freq):n * n:n], CS, start=True, stop=not both)
                            if both:
                                m = mm(o, q[:, im_slot(freq):n * n:n], SC, start=False, stop=True)
                        m.then_inc(f_ready, 1)
                    if j:
                        i = j - 1
                        pe.wait_ge(f_kept, b * fpairs + i + 1)
                        if i >= 2:
                            pe.wait_ge(prod_ready, b * fpairs + i - 1)
                        live = min(2, NK - 2 * i)
                        for u in range(2 * live):
                            nc.tensor.transpose(pb[2 + i % 2][:, u * n:(u + 1) * n], f[:, i % 2, u * n:(u + 1) * n], g["iden"][:])
                        for u in range(live):
                            o = pb[4 + i % 2][:, u * 2 * n:(u + 1) * 2 * n]
                            mm(o, f[:, i % 2, 2 * u * n:(2 * u + 1) * n], mixm[:, 0:2 * n], start=True, stop=False)
                            m = mm(o, f[:, i % 2, (2 * u + 1) * n:(2 * u + 2) * n], mixm[:, 2 * n:4 * n],
                                   start=False, stop=True)
                        m.then_inc(mixed, 1)
                pe.wait_ge(z_ready, b * fpairs + fpairs)
                for i in range(fours):
                    if i >= 2:
                        for e in range(2):
                            pe.wait_ge(inv_kept[e], b * fours + i - 1)
                    for c in range(4):
                        ch = 4 * i + c
                        mm(pb[i % 2][:, c * n:(c + 1) * n], yb[:, ch:n * n:n], C_, start=True, stop=True)
                    for c in range(4):
                        ch = 4 * i + c
                        m = mm(pb[2 + i % 2][:, c * n:(c + 1) * n], yb[:, 2 * n + ch:n * n + 2 * n:n], S_,
                               start=True, stop=True)
                    m.then_inc(inv_ready, 1)
                for e in range(2):
                    pe.wait_ge(inv_kept[e], b * fours + fours)
                for i in range(fours):
                    if i >= 2:
                        pe.wait_ge(fin_kept, b * fours + i - 1)
                    for h in range(4):
                        row = 4 * i + h
                        o = pb[4 + i % 2][:, h * n:(h + 1) * n]
                        mm(o, ya[:, row:n * n:n], B1, start=True, stop=False)
                        m = mm(o, q[:, row:n * n:n], B2, start=False, stop=True)
                    m.then_inc(fin_ready, 1)

        def evacuate(eng, copy, e, b):
            for i in range(e, fours, 2):
                eng.wait_ge(t_ready, b * fours + i + 1)
                copy(yb[:, 4 * i * n:4 * (i + 1) * n], pb[i % 4][:]).then_inc(t_kept[e], 1)
            for i in range(e, fours, 2):
                eng.wait_ge(rows_ready, b * fours + i + 1)
                copy(q[:, 4 * i * n:4 * (i + 1) * n], pb[4 + i % 4][:]).then_inc(rows_kept[e], 1)

        @block.scalar
        def _(act):
            with act.Fori(0, B) as b:
                evacuate(act, nc.scalar.copy, 0, b)
                for j in range(fpairs):
                    act.wait_ge(f_ready, b * fpairs + j + 1)
                    if j >= 2:
                        act.wait_ge(mixed, b * fpairs + j - 1)
                    w = min(2, NK - 2 * j) * 2 * n
                    nc.scalar.copy(f[:, j % 2, 0:w], pb[j % 2][:, 0:w]).then_inc(f_kept, 1)
                for i in range(fours):
                    act.wait_ge(inv_ready, b * fours + i + 1)
                    nc.scalar.copy(ya[:, 4 * i * n:4 * (i + 1) * n], pb[i % 2][:]).then_inc(inv_kept[0], 1)

        @block.vector
        def _(dve):
            v = nc.vector
            kept = [0]

            def chain(ins):
                ins.then_inc(mix_kept, 1)
                kept[0] += 1
                dve.wait_ge(mix_kept, kept[0])
            dve.wait_ge(mix_ready, 2)
            chain(v.tensor_copy(gc[:, 0:n], pb[1][:, 0:n]))
            chain(v.tensor_copy(gc[:, n:2 * n], pb[5][:, 0:n]))
            chain(v.tensor_tensor(mixm[:, 0:n], pb[0][:, 0:n], gc[:, 0:n], ALU.subtract))
            chain(v.tensor_copy(mixm[:, 3 * n:4 * n], mixm[:, 0:n]))
            chain(v.tensor_copy(mixm[:, n:2 * n], pb[2][:, 0:n]))
            chain(v.tensor_scalar(mixm[:, 2 * n:3 * n], pb[2][:, 0:n], -1.0, None, ALU.mult))
            chain(v.tensor_tensor(gc[:, 2 * n:3 * n], pb[4][:, 0:n], gc[:, n:2 * n], ALU.subtract))
            chain(v.tensor_tensor(bias[:, 0, 0], gc[:, 2 * n:3 * n], w12[:, 6 * n:7 * n], ALU.add))
            chain(v.tensor_tensor(bias[:, 0, 1], pb[6][:, 0:n], w12[:, 7 * n:8 * n], ALU.add))
            chain(v.tensor_copy(bias[:, 1, 0], bias[:, 0, 0]))
            chain(v.tensor_copy(bias[:, 1, 1], bias[:, 0, 1]))

            dve.sem_inc(batch_free, 1)
            with dve.Fori(0, B) as b:
                evacuate(dve, v.tensor_copy, 1, b)
                for j in range(fpairs):
                    live = min(2, NK - 2 * j)
                    w = live * 2 * n
                    done = b * (3 * fpairs) + 3 * j
                    pT = pb[2 + j % 2][:].rearrange("p (u r k) -> p u r k", u=2, r=2)
                    gv = ge.rearrange("p (u r k) -> p u r k", u=2, r=2)
                    dve.wait_ge(mixed, b * fpairs + j + 1)
                    if j:
                        dve.wait_ge(prod_ready, b * fpairs + j)
                    v.tensor_tensor(ge[:, 0:w], pb[4 + j % 2][:, 0:w], bias[:].rearrange("p u r k -> p (u r k)")[:, 0:w],
                                    ALU.add).then_inc(g_done, 1)
                    dve.wait_ge(g_done, done + 1)
                    v.tensor_scalar(gc[:, 0:w], ge[:, 0:w], LAMBD, -LAMBD, ALU.min, ALU.max).then_inc(g_done, 1)
                    dve.wait_ge(g_done, done + 2)
                    v.tensor_tensor(ge[:, 0:w], ge[:, 0:w], gc[:, 0:w], ALU.subtract).then_inc(g_done, 1)
                    dve.wait_ge(g_done, done + 3)
                    if j >= 2:
                        dve.wait_ge(z_ready, b * fpairs + j - 1)
                    v.tensor_tensor(m1[:, j % 2, 0:live], gv[:, 0:live], pT[:, 0:live], ALU.mult)
                    v.tensor_tensor(m2[:, j % 2, 0:live, 0], gv[:, 0:live, 0], pT[:, 0:live, 1], ALU.mult)
                    m = v.tensor_tensor(m2[:, j % 2, 0:live, 1], gv[:, 0:live, 1], pT[:, 0:live, 0], ALU.mult)
                    m.then_inc(prod_ready, 1)
                for i in range(fours):
                    dve.wait_ge(inv_ready, b * fours + i + 1)
                    v.tensor_copy(q[:, 4 * i * n:4 * (i + 1) * n], pb[2 + i % 2][:]).then_inc(inv_kept[1], 1)
                for i in range(fours):
                    half = i % 2
                    dve.wait_ge(fin_ready, b * fours + i + 1)
                    dve.wait_ge(side_in[half], b * (8 * fours) + 16 * (i // 2 + 1))
                    if i >= 2:
                        dve.wait_ge(y_out[half], b * (8 * fours) + 16 * (i // 2))
                    v.tensor_tensor(out[:, half, :, 1:n + 1], pb[4 + half][:].rearrange("p (h w) -> p h w", h=4),
                                    side[:, half], ALU.add).then_inc(fin_kept, 1)
                    dve.wait_ge(fin_kept, b * fours + i + 1)
                    if i == 2:
                        dve.wait_ge(edge_out, b * 32 + 16)
                    v.tensor_copy(out[:, half, :, 0:n + 2:n + 1], out[:, half, :, 1:n + 1:n - 1]).then_inc(fin_done, 1)
                wait_alone(dve, fin_done, b * fours + fours, batch_free)

        @block.gpsimd
        def _(pool):
            t = nc.gpsimd.tensor_tensor
            z = yb[:].rearrange("p (s c) -> p s c", c=n)
            with pool.Fori(0, B) as b:
                for j in range(fpairs):
                    pool.wait_ge(prod_ready, b * fpairs + j + 1)
                    runs = [(0, 1), (1, 1)] if j == 0 else [(0, min(2, NK - 2 * j))]
                    for u, k in runs:
                        freq = 2 * j + u
                        zr, zi = re_slot(freq), im_slot(freq)
                        t(z[:, zr:zr + k], m1[:, j % 2, u:u + k, 0], m1[:, j % 2, u:u + k, 1], ALU.subtract)
                        m = t(z[:, zi:zi + k], m2[:, j % 2, u:u + k, 0], m2[:, j % 2, u:u + k, 1], ALU.add)
                    m.then_inc(z_ready, 1)


def experts_scan(nc, d, g):
    n = PH
    with Scope(nc, "es") as s:
        rr = s.sb("rr", [128, 2, STOK])
        y2 = s.sb("y2", [128, 2, SUP + 2, n + 2])
        y25 = s.sb("y25", [128, 2, SUP + 2, n + 2])
        vv, v25 = s.sb("vv", [128, 2, 2, n + 2]), s.sb("v25", [128, 2, 2, n + 2])
        up = s.sb("up", [128, 2, 2, n, 2])
        x3 = s.sb("x3", [128, 2, STOK])
        xt = s.sb("xt", [128, 2, SUP, 4, C])
        sq, lnv, rstd = (s.sb(nm, [128, 2, TILE]) for nm in ("sq", "lnv", "rstd"))
        lg = s.sb("lg", [128, 2, STOK // 2])
        le = s.sb("le", [128, STOK // 2])
        top, topi = s.sb("top", [128, 2, TOPK]), s.sb("topi", [128, 2, TOPK], U32)
        ntop, es = s.sb("ntop", [128, 2, 1]), s.sb("es", [128, 2, 1])
        junk = s.sb("junk", [128, 2])
        pc = [s.ps(f"pc{i}") for i in range(2)]
        pvar = [s.ps(f"pvar{i}") for i in range(2)]
        pg = [s.ps(f"pg{i}") for i in range(2)]
        pt = [s.ps(f"pt{i}") for i in range(2)]
        turned, xt_ready = s.sems("turned xt_ready")
        xt_out = s.sems("xt_out0 xt_out1")
        r_in, y_in, x3_out = s.sems("r_in0 r_in1"), s.sems("y_in0 y_in1"), s.sems("x3_out0 x3_out1")
        y25_ready, v_ready, v25_ready, up_ready, x3_ready = s.sems("y25_ready v_ready v25_ready up_ready x3_ready")
        centered, squared, var_ready, ln_ready, rstd_ready, gate_ready, scaled = s.sems(
            "centered squared var_ready ln_ready rstd_ready gate_ready scaled")
        biased, top_ready, topi_ready, ntop_ready, sum_ready, exped, noted = s.sems(
            "biased top_ready topi_ready ntop_ready sum_ready exped noted")
        block = s.block()

        def line(buf, slot):
            return buf[:, slot // SUP, (slot % SUP) * TILE:(slot % SUP + 1) * TILE]

        @block.sync
        def _(sp):
            def load(st, half):
                b = st // (SUPERS // B)
                sp.dma_start(rr[:, half], d["rs"][:, bass.ds(st * STOK, STOK)]).then_inc(r_in[half], 16)
                sp.dma_start(y2[:, half], d["y2s"][:, bass.ds(b * (n + 2) + st % (SUPERS // B) * SUP, SUP + 2), :]
                             ).then_inc(y_in[half], 16)
            load(0, 0)
            load(1, 1)

            def turn_body(turn, more):
                for half in range(2):
                    st = turn * 2 + half
                    sp.wait_ge(x3_ready, SUP * (st + 1))
                    if more:
                        load(st + 2, half)
                    b = st // (SUPERS // B)
                    sp.dma_start(d["outflat"][:, bass.ds(b, 1), bass.ds(st % (SUPERS // B) * STOK, STOK)],
                                 x3[:, half]).then_inc(x3_out[half], 16)
                    sp.wait_ge(xt_ready, SUP * (st + 1))
                    sp.dma_start(d["x3t"][bass.ds(st, 1)].rearrange("o (j p) c -> (o p) j c", p=128),
                                 xt[:, half].rearrange("p j q c -> p (j q) c")).then_inc(xt_out[half], 16)
            with sp.Fori(0, PAIRS - 1) as r:
                turn_body(r, True)
            turn_body(PAIRS - 1, False)
            for half in range(2):
                sp.wait_ge(x3_out[half], 16 * PAIRS)
                sp.wait_ge(xt_out[half], 16 * PAIRS)

        @block.tensor
        def _(pe):
            mm = nc.tensor.matmul

            def step(r, k):
                if at := locate(r, k, 3, TILES):
                    turn, slot, t = at
                    pe.wait_ge(x3_ready, t + 1)
                    wait(pe, squared, t - 1)
                    mm(pc[slot % 2][:], g["cen"][:], line(x3, slot), start=True, stop=True).then_inc(centered, 1)
                if at := locate(r, k, 4, TILES):
                    turn, slot, t = at
                    pe.wait_ge(squared, t + 1)
                    wait(pe, ln_ready, t - 1)
                    mm(pvar[slot % 2][:], g["ones"][:], sq[:, slot % 2], start=True, stop=True).then_inc(var_ready, 1)
                    rows = slice(64 * (slot % SUP // 4), 64 * (slot % SUP // 4) + 64)
                    wait(pe, scaled, t - 1)
                    mm(pg[slot % 2][rows, :], g["qcWcGc"][:, 2 * C:2 * C + EXPERTS], line(x3, slot),
                       start=True, stop=True).then_inc(gate_ready, 1)
                    wait(pe, xt_ready, t - 1)
                    for q in range(4):
                        m = nc.tensor.transpose(pt[slot % 2][:, q * 128:(q + 1) * 128],
                                                line(x3, slot)[:, q * 128:(q + 1) * 128], g["iden"][:])
                    m.then_inc(turned, 1)
            run_steps(pe, TILES, 5, step)

        @block.scalar
        def _(act):
            load_ln_and_exp(act)
            a = nc.scalar.activation

            def step(r, k):
                at = locate(r, k, 0, TILES)
                if at and at[1] % SUP == 0:
                    turn, slot, t = at
                    st, half = turn * 2 + slot // SUP, slot // SUP
                    act.wait_ge(y_in[half], 16 * (turn + 1))
                    wait(act, v_ready, t - SUP)
                    a(y25[:, half], y2[:, half], ACT.Copy, scale=0.25).then_inc(y25_ready, 1)
                if at := locate(r, k, 5, TILES):
                    turn, slot, t = at
                    act.wait_ge(var_ready, t + 1)
                    a(lnv[:, slot % 2], pvar[slot % 2][:], ACT.Ln, bias=g["eps"][:, 1:2]).then_inc(ln_ready, 1)
                if at := locate(r, k, 1, TILES):
                    turn, slot, t = at
                    act.wait_ge(v_ready, t + 1)
                    wait(act, up_ready, t - 1)
                    a(v25[:, slot % 2], vv[:, slot % 2], ACT.Copy, scale=0.25).then_inc(v25_ready, 1)
                if at := locate(r, k, 3, TILES):
                    turn, slot, t = at
                    act.wait_ge(centered, t + 1)
                    wait(act, var_ready, t - 1)
                    a(sq[:, slot % 2], pc[slot % 2][:], ACT.Square).then_inc(squared, 1)
                if at := locate(r, k, 5, TILES):
                    turn, slot, t = at
                    act.wait_ge(ln_ready, t + 1)
                    wait(act, scaled, t - 1)
                    a(rstd[:, slot % 2], lnv[:, slot % 2], ACT.Exp, scale=-0.5).then_inc(rstd_ready, 1)
                if at := locate(r, k, 5, TILES):
                    turn, slot, t = at
                    act.wait_ge(turned, t + 1)
                    if slot % SUP == 0:
                        wait(act, xt_out[slot // SUP], 16 * turn)
                    a(xt[:, slot // SUP, slot % SUP].rearrange("p q c -> p (q c)"), pt[slot % 2][:], ACT.Copy
                      ).then_inc(xt_ready, 1)
                at = locate(r, k, 9, TILES)
                if at and at[1] % SUP == SUP - 1:
                    turn, slot, t = at
                    st, half = turn * 2 + slot // SUP, slot // SUP
                    act.wait_ge(ntop_ready, st + 1)
                    wait(act, sum_ready, st)
                    wait(act, exped, st)
                    a(le[:], lg[:, half], ACT.Exp, bias=ntop[:, half], accum_out=es[:, half]).then_inc(exped, 1)
            run_steps(act, TILES, 10, step)

        @block.vector
        def _(dve):
            v = nc.vector

            def step(r, k):
                if at := locate(r, k, 2, TILES):
                    turn, slot, t = at
                    dve.wait_ge(v25_ready, t + 1)
                    wait(dve, x3_ready, t - 1)
                    for odd in range(2):
                        m = v.scalar_tensor_tensor(up[:, slot % 2, :, :, odd], vv[:, slot % 2, :, 1:n + 1], 0.75,
                                                   v25[:, slot % 2, :, 2 * odd:2 * odd + n], ALU.mult, ALU.add)
                    m.then_inc(up_ready, 1)
                if at := locate(r, k, 0, TILES):
                    turn, slot, t = at
                    st, half, i = turn * 2 + slot // SUP, slot // SUP, slot % SUP
                    dve.wait_ge(y25_ready, st + 1)
                    wait(dve, up_ready, t - 1)
                    wait(dve, v25_ready, t - 1)
                    v.scalar_tensor_tensor(vv[:, slot % 2], y2[:, half, i + 1:i + 2].to_broadcast([128, 2, n + 2]),
                                           0.75, y25[:, half, i:i + 3:2], ALU.mult, ALU.add).then_inc(v_ready, 1)
                if at := locate(r, k, 6, TILES):
                    turn, slot, t = at
                    rows = slice(64 * (slot % SUP // 4), 64 * (slot % SUP // 4) + 64)
                    cols = slice((slot % 4) * TILE, (slot % 4 + 1) * TILE)
                    dve.wait_ge(rstd_ready, t + 1)
                    dve.wait_ge(gate_ready, t + 1)
                    if slot % SUP == 0:
                        wait(dve, exped, turn * 2 + slot // SUP - 1)
                    v.tensor_tensor(lg[rows, slot // SUP, cols], pg[slot % 2][rows, :], rstd[rows, slot % 2], ALU.mult
                                    ).then_inc(scaled, 1)
                at = locate(r, k, 7, TILES)
                if at and at[1] % SUP == SUP - 1:
                    turn, slot, t = at
                    st, half = turn * 2 + slot // SUP, slot // SUP
                    dve.wait_ge(scaled, t + 1)
                    v.tensor_scalar(lg[:, half], lg[:, half], g["gateb"][:], None, ALU.add).then_inc(biased, 1)
                    dve.wait_ge(biased, st + 1)
                    v.tensor_copy(junk[:, 0:1], lg[:, half, 0:1])
                    v.max(top[:, half], lg[:, half]).then_inc(top_ready, 1)
                    dve.wait_ge(top_ready, st + 1)
                    v.tensor_scalar(ntop[:, half], top[:, half, 0:1], -1.0, None, ALU.mult).then_inc(ntop_ready, 1)
                    v.max_index(topi[:, half], top[:, half], lg[:, half]).then_inc(topi_ready, 1)
                    dve.wait_ge(topi_ready, st + 1)
                    v.tensor_copy(g["cand"][:, bass.ds(st * TOPK, TOPK)], top[:, half])
                    v.tensor_copy(g["candi"][:, bass.ds(st * TOPK, TOPK)], topi[:, half]).then_inc(noted, 1)
                at = locate(r, k, 10, TILES)
                if at and at[1] % SUP == SUP - 1:
                    turn, slot, t = at
                    st, half = turn * 2 + slot // SUP, slot // SUP
                    dve.wait_ge(exped, st + 1)
                    v.tensor_copy(g["cands"][:, bass.ds(st, 1)], es[:, half]).then_inc(sum_ready, 1)
            run_steps(dve, TILES, 11, step)
            dve.wait_ge(noted, SUPERS)
            dve.wait_ge(sum_ready, SUPERS)

        @block.gpsimd
        def _(pool):
            def step(r, k):
                if at := locate(r, k, 2, TILES):
                    turn, slot, t = at
                    half = slot // SUP
                    if slot % SUP == 0:
                        pool.wait_ge(r_in[half], 16 * (turn + 1))
                        wait(pool, x3_out[half], 16 * turn)
                        wait(pool, turned, t - SUP)
                    pool.wait_ge(up_ready, t + 1)
                    nc.gpsimd.tensor_tensor(line(x3, slot), line(rr, slot),
                                            up[:, slot % 2].rearrange("p a j o -> p (a j o)"), ALU.add
                                            ).then_inc(x3_ready, 1)
            run_steps(pool, TILES, 3, step)


def experts_apply(nc, d, g):
    BK = B * TOPK
    J = BK * EXPERTS
    NCAND = SUPERS // B * 2 * TOPK
    HC = HID // 128
    EB = EXPERTS * B
    EK = EXPERTS * TOPK
    PER = 8
    TURNS = EXPERTS // (2 * PER)
    with Scope(nc, "ea") as s:
        V, TK = s.sb("V", [EXPERTS, SUPERS, 2, TOPK]), s.sb("TK", [EXPERTS, SUPERS, 2, TOPK])
        SM = s.sb("SM", [EXPERTS, SUPERS, 2])
        off, iota = s.sb("off", [EXPERTS, SUPERS * 2 * TOPK]), s.sb("iota", [EXPERTS, NCAND])
        junk = s.sb("junk", [EXPERTS, NCAND])
        tv, tok, pk = (s.sb(nm, [EXPERTS, B, TOPK]) for nm in ("tv", "tok", "pk"))
        pos, posf = s.sb("pos", [EXPERTS, B, TOPK], U32), s.sb("posf", [EXPERTS, B, TOPK])
        toki, rowi = s.sb("toki", [EXPERTS, B, TOPK], I32), s.sb("rowi", [EXPERTS, B, TOPK], U32)
        ntop, zs, rz = (s.sb(nm, [EXPERTS, B]) for nm in ("ntop", "zs", "rz"))
        em = s.sb("em", [EXPERTS, B, SUPERS // B * 2])
        tokrow = s.sb("tokrow", [1, J], I32)
        tokall = s.sb("tokall", [EXPERTS, B, TOPK, EXPERTS])
        xg, xh, sq = (s.sb(nm, [EXPERTS, BK, C]) for nm in ("xg", "xh", "sq"))
        mean, var, rstd = (s.sb(nm, [EXPERTS, BK]) for nm in ("mean", "var", "rstd"))
        pooled_e = s.sb("pooled_e", [EXPERTS, B, C])
        pooled = s.sb("pooled", [128, B, EXPERTS])
        wbuf = s.sb("wbuf", [128, 2, PER, HID])
        wb1, wb2 = s.sb("wb1", [128, EXPERTS, HC]), s.sb("wb2", [128, EXPERTS])
        hb, hh = (s.sb(nm, [128, EXPERTS * HC, B]) for nm in ("hb", "hh"))
        ob = s.sb("ob", [128, B, EXPERTS])
        oe = s.sb("oe", [EXPERTS, B, C])
        wt = s.sb("wt", [EXPERTS, 2, C])
        same = s.sb("same", [EXPERTS, 2, EK])
        new = s.sb("new", [128, B, TOPK, EXPERTS])
        ptr, pA, pB, pN = s.ps("ptr"), s.ps("pA"), s.ps("pB", (128, 2 * TILE)), s.ps("pN", (128, B * TILE))
        c_in, merged, em_ready, rows_out, rows_in, got = s.sems("c_in merged em_ready rows_out rows_in got")
        centered, squared, var_ready, ln_ready, rstd_ready, pooled_ready, turned = s.sems(
            "centered squared var_ready ln_ready rstd_ready pooled_ready turned")
        w_in = s.sems("w_in0 w_in1")
        hid_ready, hb_ready, act_ready, o_ready, out_steps, same_ready, summed, new_ready = s.sems(
            "hid_ready hb_ready act_ready o_ready out_steps same_ready summed new_ready")
        put_by_sp, put_by_act, put_by_pool, put_rest, passed = s.sems("put_by_sp put_by_act put_by_pool put_rest passed")
        block = s.block()
        xt = d["outflat"]
        MERGES = 4 + B * (3 + TOPK)

        def put(eng, e, b, ranks, sem):
            for k in ranks:
                t = eng.value_load(tokrow[0:1, bass.ds(e * BK + (b * TOPK + k), 1)], min_val=0, max_val=TOK - 1)
                eng.dma_start(xt[:, b, bass.ds(t, 1)], new[:, b, k, bass.ds(e, 1)], allow_slow_non_contiguous=True
                              ).then_inc(sem, 16)

        MINE = 5

        @block.sync
        def _(sp):
            for half in range(2):
                rows = slice(64 * half, 64 * half + 64)
                sp.dma_start(V[:, :, half], g["cand"][rows].rearrange("p (s k) -> p s k", k=TOPK)).then_inc(c_in, 16)
                sp.dma_start(TK[:, :, half], g["candi"][rows].rearrange("p (s k) -> p s k", k=TOPK)).then_inc(c_in, 16)
                sp.dma_start(SM[:, :, half], g["cands"][rows], allow_slow_non_contiguous=True).then_inc(c_in, 16)
            sp.dma_start(off[:], d["tokoff"].to_broadcast([EXPERTS, SUPERS * 2 * TOPK])).then_inc(c_in, 16)
            sp.dma_start(iota[:], d["iota"].to_broadcast([EXPERTS, NCAND])).then_inc(c_in, 16)
            sp.dma_start(wb1[:], d["wb1"]).then_inc(c_in, 16)
            sp.dma_start(wb2[:], d["wb2"]).then_inc(c_in, 16)

            def load1(turn, half):
                sp.dma_start(wbuf[:, half], d["w1"][bass.ds((2 * turn + half) * PER, PER), 0:C].rearrange("e c h -> c e h")
                             ).then_inc(w_in[half], 16)

            def load2(turn, half):
                for q in range(HC):
                    sp.dma_start(wbuf[:, half].rearrange("p e (q o) -> p e q o", q=HC)[:, :, q],
                                 d["w2"][bass.ds((2 * turn + half) * PER, PER), q * 128:(q + 1) * 128].rearrange(
                                     "e p o -> p e o")).then_inc(w_in[half], 16)
            for half in range(2):
                load1(0, half)
            sp.wait_ge(merged, MERGES)
            sp.dma_start(d["toks"].rearrange("o (e j) -> (o e) j", e=EXPERTS), toki[:].rearrange("p b k -> p (b k)")
                         ).then_inc(rows_out, 16)
            sp.dma_start(d["tokf"].rearrange("o (b k e) -> (o e) b k", b=B, k=TOPK), tok[:],
                         allow_slow_non_contiguous=True).then_inc(rows_out, 16)
            sp.wait_ge(rows_out, 32)
            sp.dma_start(tokrow[:], d["toks"]).then_inc(rows_in, 16)
            sp.dma_start(tokall[:].rearrange("p b k e -> p (b k e)"), d["tokf"].to_broadcast([EXPERTS, J])
                         ).then_inc(rows_in, 16)
            with sp.Fori(1, TURNS) as t:
                for half in range(2):
                    sp.wait_ge(hid_ready, 2 * t + half - 1)
                    load1(t, half)
            for half in range(2):
                sp.wait_ge(hid_ready, 2 * TURNS + half - 1)
                load2(0, half)
            with sp.Fori(1, TURNS) as t:
                for half in range(2):
                    sp.wait_ge(o_ready, 2 * t + half - 1)
                    load2(t, half)
            sp.wait_ge(new_ready, B)
            with sp.Fori(0, EXPERTS) as e:
                put(sp, e, 0, range(TOPK), put_by_sp)
                wait_alone(sp, put_by_sp, 16 * TOPK * (e + 1), passed)

        @block.tensor
        def _(pe):
            mm = nc.tensor.matmul
            pe.wait_ge(pooled_ready, 1)
            for b in range(B):
                m = nc.tensor.transpose(ptr[:, b * EXPERTS:(b + 1) * EXPERTS], pooled_e[:, b], g["iden"][0:EXPERTS, 0:EXPERTS])
            m.then_inc(turned, 1)
            pe.wait_ge(pooled_ready, 2)

            with pe.Fori(0, TURNS) as t:
                for half in range(2):
                    pe.wait_ge(w_in[half], 16 * (t + 1))
                    for e in range(PER):
                        for q in range(HC):
                            ex = (2 * t + half) * PER + e
                            m = mm(pB[:, bass.ds((ex * HC + q) * B, B)], wbuf[:, half, e, q * 128:(q + 1) * 128],
                                   pooled[:, :, bass.ds(ex, 1)], start=True, stop=True)
                    m.then_inc(hid_ready, 1)
            pe.wait_ge(act_ready, 1)
            with pe.Fori(0, TURNS) as t:
                for half in range(2):
                    pe.wait_ge(w_in[half], 16 * (TURNS + HC * t + HC))
                    for e in range(PER):
                        ex = (2 * t + half) * PER + e
                        for q in range(HC):
                            m = mm(pA[:, bass.ds(ex * B, B)], wbuf[:, half, e, q * 128:(q + 1) * 128],
                                   hh[:, bass.ds(ex * HC + q, 1), :], start=(q == 0), stop=(q == HC - 1))
                    m.then_inc(o_ready, 1)
            pe.wait_ge(out_steps, 1)
            for b in range(B):
                m = nc.tensor.transpose(pB[0:EXPERTS, b * C:(b + 1) * C], ob[:, b], g["iden"][:])
            m.then_inc(turned, 1)
            for b in range(B):
                o = pN[:, b * TILE:(b + 1) * TILE]
                for k in range(TOPK):
                    pe.wait_ge(same_ready, b * TOPK + k + 1)
                    mm(o, wt[:, k % 2], same[:, k % 2], start=(k == 0), stop=False).then_inc(summed, 1)
                for k in range(TOPK):
                    m = mm(o[:, k * EXPERTS:(k + 1) * EXPERTS], xg[:, b * TOPK + k], g["iden"][0:EXPERTS, 0:EXPERTS],
                           start=False, stop=(k == TOPK - 1))
                m.then_inc(o_ready, 1)

        @block.scalar
        def _(act):
            load_ln_and_exp(act)
            a = nc.scalar.activation
            for b in range(B):
                act.wait_ge(merged, 2 + b * (3 + TOPK) + 3)
                heads = V[:].rearrange("p (b s) h k -> p b (s h) k", b=B)[:, b, :, 0]
                a(em[:, b], heads, ACT.Exp, bias=ntop[:, b:b + 1])
                a(pk[:, b], tv[:, b], ACT.Exp, bias=ntop[:, b:b + 1]).then_inc(em_ready, 1)
            act.wait_ge(centered, 1)
            a(sq[:], xh[:], ACT.Square).then_inc(squared, 1)
            act.wait_ge(var_ready, 1)
            a(var[:], var[:], ACT.Ln, bias=g["eps"][0:EXPERTS, 1:2], scale=1.0 / C).then_inc(ln_ready, 1)
            act.wait_ge(ln_ready, 1)
            a(rstd[:], var[:], ACT.Exp, scale=-0.5).then_inc(rstd_ready, 1)
            act.wait_ge(hb_ready, 1)
            a(hh[:], hb[:], ACT.Gelu).then_inc(act_ready, 1)
            act.wait_ge(new_ready, B)
            with act.Fori(0, EXPERTS) as e:
                put(act, e, 1, range(TOPK), put_by_act)
                put(act, e, 2, range(MINE), put_rest)
                act.wait_ge(put_by_act, 16 * TOPK * (e + 1))
                act.wait_ge(put_rest, 16 * MINE * (e + 1))
                act.wait_ge(put_by_pool, 16 * (2 * TOPK - MINE) * (e + 1))

        @block.vector
        def _(dve):
            v = nc.vector
            n = [0]

            def chain(ins):
                ins.then_inc(merged, 1)
                n[0] += 1
                dve.wait_ge(merged, n[0])
            dve.wait_ge(c_in, 16 * 10)
            chain(v.tensor_tensor(TK[:].rearrange("p s h k -> p (s h k)"), TK[:].rearrange("p s h k -> p (s h k)"),
                                  off[:], ALU.add))
            for b in range(B):
                vb = V[:].rearrange("p (b s) h k -> p b (s h k)", b=B)[:, b]
                tb = TK[:].rearrange("p (b s) h k -> p b (s h k)", b=B)[:, b]
                chain(v.max(tv[:, b], vb))
                v.tensor_scalar(ntop[:, b:b + 1], tv[:, b, 0:1], -1.0, None, ALU.mult)
                chain(v.max_index(pos[:, b], tv[:, b], vb))
                chain(v.tensor_copy(posf[:, b], pos[:, b]))
                for k in range(TOPK):
                    chain(v.scalar_tensor_tensor(junk[:], iota[:], posf[:, b, k:k + 1], tb, ALU.is_equal, ALU.mult,
                                                 accum_out=tok[:, b, k:k + 1]))
            chain(v.tensor_copy(toki[:], tok[:]))
            chain(v.scalar_tensor_tensor(
                rowi[:], iota[:, 0:B].rearrange("p (b o) -> p b o", o=1).to_broadcast([EXPERTS, B, TOPK]), float(TOK),
                tok[:], ALU.mult, ALU.add))
            chain(v.memset(junk[:], 0.0))
            assert n[0] == MERGES
            dve.wait_ge(em_ready, B)
            chain(v.tensor_tensor(em[:], em[:], SM[:].rearrange("p (b s) h -> p b (s h)", b=B), ALU.mult))
            chain(v.tensor_reduce(zs[:], em[:], AX.X, ALU.add))
            chain(v.reciprocal(rz[:], zs[:]))
            chain(v.tensor_tensor(pk[:], pk[:], rz[:].rearrange("p (b o) -> p b o", o=1).to_broadcast([EXPERTS, B, TOPK]),
                                  ALU.mult))
            over_c = lambda x: x[:].rearrange("p (j o) -> p j o", o=1).to_broadcast([EXPERTS, BK, C])
            dve.wait_ge(got, 16 * BK)
            chain(v.tensor_reduce(mean[:], xg[:], AX.X, ALU.add))
            chain(v.tensor_scalar(mean[:], mean[:], 1.0 / C, None, ALU.mult))
            v.tensor_tensor(xh[:], xg[:], over_c(mean), ALU.subtract).then_inc(centered, 1)
            dve.wait_ge(squared, 1)
            v.tensor_reduce(var[:], sq[:], AX.X, ALU.add).then_inc(var_ready, 1)
            dve.wait_ge(rstd_ready, 1)
            chain(v.tensor_tensor(rstd[:], rstd[:], pk[:].rearrange("p b k -> p (b k)"), ALU.mult))
            chain(v.tensor_tensor(xh[:], xh[:], over_c(rstd), ALU.mult))
            v.tensor_reduce(pooled_e[:], xh[:].rearrange("p (b k) c -> p b c k", b=B), AX.X, ALU.add
                            ).then_inc(pooled_ready, 1)
            dve.wait_ge(turned, 1)
            v.tensor_copy(pooled[:].rearrange("p b e -> p (b e)"), ptr[:, 0:EB]).then_inc(pooled_ready, 1)
            dve.wait_ge(hid_ready, 2 * TURNS)
            v.tensor_tensor(hb[:], pB[:, 0:EB * HC].rearrange("p (h b) -> p h b", b=B),
                            wb1[:].rearrange("p e q -> p (e q)").rearrange("p (h o) -> p h o", o=1).to_broadcast(
                                [128, EXPERTS * HC, B]), ALU.add).then_inc(hb_ready, 1)
            dve.wait_ge(o_ready, 2 * TURNS)
            v.tensor_tensor(ob[:].rearrange("p b e -> p e b"), pA[:, 0:EB].rearrange("p (e b) -> p e b", b=B),
                            wb2[:].rearrange("p (e o) -> p e o", o=1).to_broadcast([128, EXPERTS, B]), ALU.add
                            ).then_inc(out_steps, 1)
            dve.wait_ge(turned, 2)
            v.tensor_copy(oe[:].rearrange("p b c -> p (b c)"), pB[0:EXPERTS, 0:B * C]).then_inc(out_steps, 1)
            dve.wait_ge(rows_in, 32)
            dve.wait_ge(out_steps, 2)
            for b in range(B):
                for k in range(TOPK):
                    wait(dve, summed, b * TOPK + k - 1)
                    v.tensor_scalar(same[:, k % 2], tokall[:, b].rearrange("p k e -> p (k e)"), tok[:, b, k:k + 1], None,
                                    ALU.is_equal)
                    v.tensor_scalar(wt[:, k % 2], oe[:, b], pk[:, b, k:k + 1], None, ALU.mult).then_inc(same_ready, 1)
                dve.wait_ge(o_ready, 2 * TURNS + b + 1)
                v.tensor_copy(new[:, b].rearrange("p k e -> p (k e)"), pN[:, b * TILE:(b + 1) * TILE]
                              ).then_inc(new_ready, 1)

        @block.gpsimd
        def _(pool):
            pool.wait_ge(merged, MERGES)
            for b in range(B):
                for k in range(TOPK):
                    pool.indirect_dma_start(xg[:, b * TOPK + k], None, d["x3t"].rearrange("s t c -> (s t) c"),
                                            bass.IndirectOffsetOnAxis(ap=rowi[:, b, k:k + 1], axis=0)).then_inc(got, 16)
            pool.wait_ge(rows_in, 32)
            pool.wait_ge(new_ready, B)
            with pool.Fori(0, EXPERTS) as e:
                put(pool, e, 3, range(TOPK), put_by_pool)
                put(pool, e, 2, range(MINE, TOPK), put_by_pool)
                pool.wait_ge(put_by_pool, 16 * (2 * TOPK - MINE) * (e + 1))
                pool.wait_ge(put_rest, 16 * MINE * (e + 1))


SCRATCH = {
    "x1s": ((WINDOWS, C, COLS * WIN), F32), "wxs": ((WINDOWS, C, COLS * WIN), F32),
    "x2s": ((WINDOWS, C, COLS * WIN), F32), "rs": ((C, B * TOK), F32), "ys": ((C, B * PH * PH), F32),
    "y2s": ((C, B * (PH + 2), PH + 2), F32), "toks": ((1, B * EXPERTS * TOPK), I32),
    "tokf": ((1, B * EXPERTS * TOPK), F32), "x3t": ((SUPERS, STOK, C), F32),
}
EARLY = {"kvT": 2 * C, "kvb": 2 * C, "mask": C, "kvden": PAIRS * 2 * C, "bn": TILES * 6}
GLOBALS = {
    "cen": 128, "ones": 128, "projT": C, "VT": C, "cols": 4, "gateb": 1,
    "eps": 2, "qcWcGc": 2 * C + EXPERTS, "bnss": 3, "iden": 128,
}


def build(nc, d, phases=None):
    todo = (setup_phase, attention_sums, attention_pass, recurrence, norm_and_pool, spectral, experts_scan,
            experts_apply)
    phases = phases or [f.__name__ for f in todo]
    d["xflat"] = d["x"].rearrange("b c h w -> c b (h w)")
    d["outflat"] = d["out"].rearrange("b c h w -> c b (h w)")
    with ExitStack() as ctx:
        def sb(name, cols):
            return ctx.enter_context(nc.sbuf_tensor("g_" + name, [128, cols], F32))
        g = {k: sb(k, v) for k, v in GLOBALS.items()}
        with ExitStack() as early:
            for k, v in EARLY.items():
                g[k] = early.enter_context(nc.sbuf_tensor("g_" + k, [128, v], F32))
            setup_phase(nc, d, g)
            for f in todo[1:3]:
                if f.__name__ in phases:
                    f(nc, d, g)
        for f in (recurrence, norm_and_pool):
            if f.__name__ in phases:
                f(nc, d, g)
        if "spectral" in phases:
            spectral(nc, d, g)
        for k, v in (("cand", SUPERS * TOPK), ("candi", SUPERS * TOPK), ("cands", SUPERS)):
            g[k] = sb(k, v)
        for f in todo[6:]:
            if f.__name__ in phases:
                f(nc, d, g)


def constants():
    n = PH
    cen = np.eye(C) - 1.0 / C
    ones = np.full((C, C), 1.0 / C)
    mask = np.kron(np.eye(HEADS), np.ones((C // HEADS, C // HEADS)))
    k = np.arange(1, n // 2)
    i = np.arange(n)
    ang = 2 * np.pi * np.outer(i, i) / n
    cs, sn = np.cos(ang), np.sin(ang)
    rw = np.concatenate([cs[:, :1], cs[:, n // 2:n // 2 + 1], cs[:, k], -sn[:, k]], 1) / n
    b1 = np.concatenate([cs[:1], cs[n // 2:n // 2 + 1], 2 * cs[k], -2 * sn[k]], 0) / n
    b2 = np.concatenate([-2 * sn[k], -2 * cs[k], -cs[:1], -cs[n // 2:n // 2 + 1]], 0) / n
    dft = np.concatenate([rw, cs, -sn, sn, cs, b1, b2], 1)
    sups = SUPERS // B
    off = (np.arange(SUPERS)[:, None, None] % sups) * STOK + np.arange(2)[None, :, None] * (STOK // 2) + np.zeros((1, 1, TOPK))
    return {k: np.ascontiguousarray(v, dtype=np.float32) for k, v in dict(
        cen=cen, ones=ones, mask=mask, dft=dft, iden=np.eye(n), tokoff=off.reshape(1, -1),
        iota=np.arange(sups * 2 * TOPK)[None]).items()}


def lay_out(v):
    a = {k: np.asarray(x) for k, x in v.items()}
    w12 = np.zeros((128, 8, 128), np.float32)
    nb, bs = 8, 16
    for c in range(2):
        for k in range(nb):
            o = slice(k * bs, (k + 1) * bs)
            w12[o, c, o] = a["L1_conv_w1"][c, k].T
            w12[o, 2 + c, o] = a["L1_conv_w2"][c, k]
        w12[:, 4 + c] = a["L1_conv_b1"][c].reshape(-1)[:, None]
        w12[:, 6 + c] = a["L1_conv_b2"][c].reshape(-1)[None]
    w1, w2 = a["L1_ffn_weight1"], a["L1_ffn_weight2"]
    got = {
        "x": a["x"], "qT": a["L0_conv_q_w"].T, "kvT": a["L0_conv_kv_w"].T, "kvb": a["L0_conv_kv_b"][None],
        "projT": a["L0_conv_proj_w"].T, "WT": a["L0_ffn_W"].T, "VT": a["L0_ffn_V"].T,
        "gateT": a["L1_ffn_gate_w"].T, "gateb": np.concatenate([a["L1_ffn_gate_b"]] * 2)[:, None],
        "cols": np.stack([a["L0_conv_q_b"], a["L0_conv_proj_b"], a["L0_ffn_gamma"], a["L0_ffn_beta"]], 1),
        "w12": w12.reshape(128, -1), "w1": w1, "w2": w2,
        "wb1": w1[:, C].reshape(EXPERTS, HID // 128, 128).transpose(2, 0, 1), "wb2": w2[:, HID].T,
    }
    got = {k: np.ascontiguousarray(x) for k, x in got.items()}
    return {**got, **constants()}


def declare(nc, arrays, kinds=()):
    d = {k: nc.dram_tensor("in_" + k, list(a.shape), mybir.dt.from_np(a.dtype), kind="ExternalInput").ap()
         for k, a in arrays.items()}
    kinds = dict(kinds)
    for k, (shape, dt) in SCRATCH.items():
        d[k] = nc.dram_tensor("s_" + k, list(shape), dt, kind=kinds.get(k, "Internal")).ap()
    d["out"] = nc.dram_tensor("out_0_dram", [B, C, H, W], F32, kind=kinds.get("out", "ExternalOutput")).ap()
    return d


def kernel(**inputs):
    import concourse.bacc as bacc
    from concourse.bass_utils import run_bass_kernel_spmd

    arrays = lay_out(inputs)
    nc = bacc.Bacc("TRN2", target_bir_lowering=False, num_devices=1, dynamic_dma_scratch_size=2048)
    build(nc, declare(nc, arrays))
    r = run_bass_kernel_spmd(nc, [{"in_" + k: a for k, a in arrays.items()}], core_ids=[0])
    return r.results[0]["out_0_dram"]
```

```python
from contextlib import ExitStack

import numpy as np

import concourse.bass as bass
from concourse import mybir

F32 = mybir.dt.float32
I32 = mybir.dt.int32
U32 = mybir.dt.uint32
F32R = mybir.dt.float32r
ALU = mybir.AluOpType
ACT = mybir.ActivationFunctionType
AX = mybir.AxisListType

B, C, H, W = 4, 128, 256, 256
TOK = H * W
TILE = 512
SUP = 8
PERIOD = 2 * SUP
STOK = SUP * TILE
TILES = B * TOK // TILE
PAIRS = TILES // PERIOD
SUPERS = TILES // SUP
CHUNK = W
CHUNKS = TOK // CHUNK
COLS = B * CHUNKS
WIN = 8
WINDOWS = CHUNK // WIN
RUN = TILE // CHUNK * WIN
GROUPS = B
HEADS = 8
KS = 4
EXPERTS, TOPK, HID = 64, 8, 512
PH = H // 2
NK = PH // 2 + 1
LAMBD = 0.01
SEAM_TOL = 1e-6


def locate(r, k, lag, tiles):
    turn, slot = r + (k - lag) // PERIOD, (k - lag) % PERIOD
    t = turn * PERIOD + slot
    if isinstance(t, int) and not 0 <= t < tiles:
        return None
    return turn, slot, t


def run_steps(eng, tiles, last_lag, step, peel=2):
    for r in range(peel):
        for k in range(PERIOD):
            step(r, k)
    with eng.Fori(peel, tiles // PERIOD) as r:
        for k in range(PERIOD):
            step(r, k)
    for k in range(last_lag):
        step(tiles // PERIOD, k)


def wait(eng, sem, value):
    if not isinstance(value, int) or value > 0:
        eng.wait_ge(sem, value)


def wait_alone(eng, sem, value, passed):
    eng.wait_ge(sem, value)
    eng.sem_inc(passed, 1)


def high_part(eng, out, x):
    return eng.tensor_copy(out, x)


def split_product(nc, out, w_high, w_low, high, low):
    parts = [(w_high, low), (w_high, high)] + ([(w_low, high)] if w_low is not None else [])
    for i, (w, x) in enumerate(parts):
        m = nc.tensor.matmul(out, w, x, start=(i == 0), stop=(i == len(parts) - 1))
    return m


def load_ln_and_exp(act):
    act.preload_act_table_set("natural_log_exp_and_others")


class Scope(ExitStack):

    def __init__(self, nc, phase):
        super().__init__()
        self.nc, self.phase, self.used = nc, phase, []

    def sb(self, name, shape, dt=F32):
        return self.enter_context(self.nc.sbuf_tensor(f"{self.phase}_{name}", shape, dt))

    def ps(self, name, shape=(128, TILE)):
        return self.enter_context(self.nc.psum_tensor(f"{self.phase}_{name}", list(shape), F32))

    def sem(self, name):
        self.used.append(self.enter_context(self.nc.semaphore(f"{self.phase}_{name}")))
        return self.used[-1]

    def block(self):
        self.callback(self.clear)
        return self.enter_context(self.nc.Block())

    def clear(self):
        with self.nc.Block() as block:
            @block.sync
            def _(sp):
                for sem in self.used:
                    sp.sem_clear(sem)

    def sems(self, names):
        return [self.sem(n) for n in names.split()]


def setup_phase(nc, d, g):
    with Scope(nc, "su") as s:
        raw = s.sb("raw", [128, 2 * C + EXPERTS])
        p = s.ps("p")
        loaded, mixed, kept, eps_set = s.sems("loaded mixed kept eps_set")
        block = s.block()

        @block.sync
        def _(sp):
            for dst, src in ((g["cen"][:], d["cen"]), (g["ones"][:], d["ones"]), (raw[:, 0:C], d["qT"]),
                             (raw[:, C:2 * C], d["WT"]), (raw[:, 2 * C:], d["gateT"]), (g["kvT"][:], d["kvT"]),
                             (g["kvb"][:], d["kvb"].to_broadcast([128, 2 * C])), (g["projT"][:], d["projT"]),
                             (g["VT"][:], d["VT"]), (g["cols"][:], d["cols"]), (g["mask"][:], d["mask"]),
                             (g["gateb"][:], d["gateb"]), (g["iden"][:], d["iden"])):
                sp.dma_start(dst, src).then_inc(loaded, 16)

        @block.tensor
        def _(pe):
            pe.wait_ge(loaded, 16 * 13)
            nc.tensor.matmul(p[:, 0:2 * C + EXPERTS], g["cen"][:], raw[:], start=True, stop=True).then_inc(mixed, 1)

        @block.vector
        def _(dve):
            nc.vector.memset(g["eps"][:, 0:1], 1e-6).then_inc(eps_set, 1)
            nc.vector.memset(g["eps"][:, 1:2], 1e-5).then_inc(eps_set, 1)
            dve.wait_ge(mixed, 1)
            nc.vector.tensor_copy(g["qcWcGc"][:], p[:, 0:2 * C + EXPERTS]).then_inc(kept, 1)
            dve.wait_ge(kept, 1)
            high_part(nc.vector, g["qcWc_high"][:], g["qcWcGc"][:, 0:2 * C]).then_inc(kept, 1)
            dve.wait_ge(kept, 2)
            nc.vector.tensor_tensor(g["qcWc_low"][:], g["qcWcGc"][:, 0:2 * C], g["qcWc_high"][:], ALU.subtract
                                    ).then_inc(kept, 1)
            dve.wait_ge(loaded, 16 * 13)
            nc.vector.tensor_copy(g["cen_high"][:], g["cen"][:]).then_inc(kept, 1)
            nc.vector.tensor_copy(g["ones_high"][:], g["ones"][:]).then_inc(kept, 1)
            dve.wait_ge(kept, 5)


def attention_sums(nc, d, g):
    tiles = B * (H // KS) * (W // KS) // TILE
    rows = TILE // (W // KS)
    x_rows = d["x"].rearrange("b c (i k) w -> c b k i w", k=KS)[:, :, KS // 2]
    with Scope(nc, "at") as s:
        x = s.sb("x", [128, 2, rows, W])
        sq = s.sb("sq", [128, 2, TILE])
        lnv = s.sb("lnv", [128, 2, TILE])
        rstd = s.sb("rstd", [128, 2, TILE])
        xn = s.sb("xn", [128, 2, TILE])
        kv = s.sb("kv", [128, 2, 4, 2 * C + 1])
        km = s.sb("km", [128, 2, 4, C])
        ke = s.sb("ke", [128, 2, 4, C])
        kf = s.sb("kf", [128, 2, 4, C])
        pxc = [s.ps("pxc0"), s.ps("pxc1")]
        pvar = s.ps("pvar")
        pkv = [s.ps("pkv0"), s.ps("pkv1")]
        pKV = [s.ps("pKV0"), s.ps("pKV1")]
        ones_set, centered, squared, var_ready, ln_ready, rstd_ready, normed = s.sems(
            "ones_set centered squared var_ready ln_ready rstd_ready normed")
        kv_ready, biased, clipped, exped, mapped, summed, kept = s.sems(
            "kv_ready biased clipped exped mapped summed kept")
        x_in = s.sems("x_in0 x_in1")
        block = s.block()

        @block.sync
        def _(sp):
            def step(r, k):
                if at := locate(r, k, 0, tiles):
                    turn, slot, t = at
                    wait(sp, centered, t - 1)
                    b, j = turn * 2 + slot // SUP, slot % SUP
                    sp.dma_start(x[:, slot % 2], x_rows[:, bass.ds(b, 1), j * rows:(j + 1) * rows]
                                 ).then_inc(x_in[slot % 2], 16)
            run_steps(sp, tiles, 0, step, peel=1)

        @block.tensor
        def _(pe):
            pe.wait_ge(ones_set, 1)

            def step(r, k):
                if at := locate(r, k, 0, tiles):
                    turn, slot, t = at
                    pe.wait_ge(x_in[slot % 2], turn * (8 * 16) + 16 * (slot // 2 + 1))
                    wait(pe, normed, t - 1)
                    nc.tensor.matmul(pxc[slot % 2][:], g["cen"][:], x[:, slot % 2, :, KS // 2::KS],
                                     start=True, stop=True).then_inc(centered, 1)
                if at := locate(r, k, 1, tiles):
                    turn, slot, t = at
                    pe.wait_ge(squared, t + 1)
                    wait(pe, ln_ready, t)
                    nc.tensor.matmul(pvar[:], g["ones"][:], sq[:, slot % 2], start=True, stop=True
                                     ).then_inc(var_ready, 1)
                if at := locate(r, k, 3, tiles):
                    turn, slot, t = at
                    pe.wait_ge(normed, t + 1)
                    wait(pe, biased, 2 * t)
                    for h in range(2):
                        for c in range(2):
                            m = nc.tensor.matmul(pkv[h][:, c * 2 * C:(c + 1) * 2 * C],
                                                 xn[:, slot % 2, (2 * h + c) * 128:(2 * h + c + 1) * 128],
                                                 g["kvT"][:], start=True, stop=True)
                        m.then_inc(kv_ready, 1)
                if at := locate(r, k, 5, tiles):
                    turn, slot, t = at
                    pe.wait_ge(mapped, t + 1)
                    if slot % 8 == 0:
                        wait(pe, kept, turn * 2 + slot // 8 - 1)
                    for c in range(4):
                        m = nc.tensor.matmul(pKV[slot // 8][:, 0:C + 1], kf[:, slot % 2, c],
                                             kv[:, slot % 2, c, C:2 * C + 1],
                                             start=(slot % 8 == 0 and c == 0), stop=(slot % 8 == 7 and c == 3))
                    m.then_inc(summed, 1)
            run_steps(pe, tiles, 6, step, peel=1)

        @block.scalar
        def _(act):
            load_ln_and_exp(act)
            def step(r, k):
                if at := locate(r, k, 0, tiles):
                    turn, slot, t = at
                    act.wait_ge(centered, t + 1)
                    wait(act, var_ready, t - 1)
                    nc.scalar.activation(sq[:, slot % 2], pxc[slot % 2][:], ACT.Square).then_inc(squared, 1)
                if at := locate(r, k, 1, tiles):
                    turn, slot, t = at
                    act.wait_ge(var_ready, t + 1)
                    nc.scalar.activation(lnv[:, slot % 2], pvar[:], ACT.Ln, bias=g["eps"][:, 0:1]).then_inc(ln_ready, 1)
                    act.wait_ge(ln_ready, t + 1)
                    wait(act, normed, t - 1)
                    nc.scalar.activation(rstd[:, slot % 2], lnv[:, slot % 2], ACT.Exp, scale=-0.5
                                         ).then_inc(rstd_ready, 1)
                if at := locate(r, k, 4, tiles):
                    turn, slot, t = at
                    act.wait_ge(clipped, t + 1)
                    wait(act, mapped, t - 1)
                    nc.scalar.activation(ke[:, slot % 2], km[:, slot % 2], ACT.Exp).then_inc(exped, 1)
            run_steps(act, tiles, 5, step, peel=1)

        @block.vector
        def _(dve):
            nc.vector.memset(kv[:, :, :, 2 * C:2 * C + 1], 1.0).then_inc(ones_set, 1)

            def step(r, k):
                if at := locate(r, k, 2, tiles):
                    turn, slot, t = at
                    dve.wait_ge(rstd_ready, t + 1)
                    wait(dve, kv_ready, 2 * t - 2)
                    nc.vector.tensor_tensor(xn[:, slot % 2], pxc[slot % 2][:], rstd[:, slot % 2], ALU.mult
                                            ).then_inc(normed, 1)
                if at := locate(r, k, 5, tiles):
                    turn, slot, t = at
                    dve.wait_ge(exped, t + 1)
                    wait(dve, summed, t - 1)
                    nc.vector.scalar_tensor_tensor(kf[:, slot % 2], kv[:, slot % 2, :, 0:C], 0.0, ke[:, slot % 2],
                                                   ALU.max, ALU.add).then_inc(mapped, 1)
                if at := locate(r, k, 3, tiles):
                    turn, slot, t = at
                    wait(dve, summed, t - 1)
                    for h in range(2):
                        dve.wait_ge(kv_ready, 2 * t + 1 + h)
                        for c in range(2):
                            m = nc.vector.tensor_tensor(kv[:, slot % 2, 2 * h + c, 0:2 * C],
                                                        pkv[h][:, c * 2 * C:(c + 1) * 2 * C], g["kvb"][:], ALU.add)
                        m.then_inc(biased, 1)
                    dve.wait_ge(biased, 2 * t + 2)
                    wait(dve, exped, t - 1)
                    nc.vector.tensor_scalar(km[:, slot % 2], kv[:, slot % 2, :, 0:C], 0.0, None, ALU.min
                                            ).then_inc(clipped, 1)
                at = locate(r, k, 6, tiles)
                if at and at[1] % 8 == 7:
                    turn, slot, t = at
                    dve.wait_ge(summed, t + 1)
                    b = turn * 2 + slot // 8
                    nc.vector.tensor_tensor(g["kvden"][:, bass.ds(b * 2 * C, C)],
                                            pKV[slot // 8][:, 0:C], g["mask"][:], ALU.mult)
                    nc.vector.tensor_scalar(g["kvden"][:, bass.ds(b * 2 * C + C, C)], g["mask"][:],
                                            pKV[slot // 8][:, C:C + 1], None, ALU.mult).then_inc(kept, 1)
            run_steps(dve, tiles, 7, step, peel=1)


def attention_pass(nc, d, g):
    x_t = d["x"].rearrange("b c h w -> c b (h w)")
    x1_s, wx_s = (d[n].rearrange("w p c -> p w c") for n in ("x1s", "wxs"))
    sup_cols = SUP * RUN
    with Scope(nc, "ap") as s:
        x = s.sb("x", [128, 2, STOK])
        x1 = s.sb("x1", [128, 2, WINDOWS, SUP, RUN])
        wx = s.sb("wx", [128, 2, WINDOWS, SUP, RUN])
        two = lambda n: s.sb(n, [128, 2, TILE])
        sq, rstd, qs, qe, att, sq1, rstd1 = map(two, "sq rstd qs qe att sq1 rstd1".split())
        two_parts = lambda n: s.sb(n, [128, 2, TILE], F32R)
        sq_high, sq_low, sq1_high, sq1_low = map(two_parts, "sq_high sq_low sq1_high sq1_low".split())
        sq_high_ready, sq_low_ready, sq1_high_ready, sq1_low_ready = s.sems(
            "sq_high_ready sq_low_ready sq1_high_ready sq1_low_ready")
        four = lambda n: s.sb(n, [128, 4, TILE], F32R)
        x_high, x_low, x1_high, x1_low = map(four, "x_high x_low x1_high x1_low".split())
        high_ready, low_ready, high1_ready, low1_ready = s.sems("high_ready low_ready high1_ready low1_ready")
        kvd = s.sb("kvd", [128, 2 * C])
        pc, pvar, pq, pden, pnum, ppr, pvar1, pw = map(s.ps, "pc pvar pq pden pnum ppr pvar1 pw".split())
        centered, squared, var_ready, ln_ready, rstd_ready = s.sems("centered squared var_ready ln_ready rstd_ready")
        q_ready, q_scaled, q_exped, q_mapped, kvd_ready = s.sems("q_ready q_scaled q_exped q_mapped kvd_ready")
        den_ready, num_ready, lnd_ready, z_ready, att_ready = s.sems(
            "den_ready num_ready lnd_ready z_ready att_ready")
        proj_ready, x1_ready, centered1, squared1, var1_ready = s.sems(
            "proj_ready x1_ready centered1 squared1 var1_ready")
        ln1_ready, rstd1_ready, w_ready, wx_ready, bn_done = s.sems(
            "ln1_ready rstd1_ready w_ready wx_ready bn_done")
        x_in, x1_out, wx_out = s.sems("x_in0 x_in1"), s.sems("x1_out0 x1_out1"), s.sems("wx_out0 wx_out1")
        bn_sums, bn_sq, bn_rs = s.sb("bn_ag", [128, 2]), s.sb("bn_sq", [128, 1]), s.sb("bn_rs", [128, 1])
        fold = s.sem("fold")
        block = s.block()

        def tile_of(buf, slot):
            return buf[:, slot // SUP, :, slot % SUP, :]

        def x_line(slot):
            return x[:, slot // SUP, (slot % SUP) * TILE:(slot % SUP + 1) * TILE].rearrange(
                "p (j w i) -> p w j i", w=WINDOWS, i=WIN)

        def by_windows(buf, slot):
            return buf[:, slot % 4].rearrange("p (w i) -> p w i", i=RUN)

        def by_rows(buf, slot):
            return buf[:, slot % 4].rearrange("p (w j i) -> p w j i", w=WINDOWS, i=WIN)

        @block.sync
        def _(sp):
            def load(turn, half):
                st = turn * 2 + half
                sp.dma_start(x[:, half], d["xflat"][:, bass.ds(st // (SUPERS // B), 1),
                                                    bass.ds(st % (SUPERS // B) * STOK, STOK)]
                             ).then_inc(x_in[half], 16)

            load(0, 0)
            load(0, 1)

            def turn_body(turn, more):
                for half in range(2):
                    st = turn * 2 + half
                    sp.wait_ge(x1_ready, SUP * (st + 1))
                    if more:
                        load(turn + 1, half)
                    sp.dma_start(x1_s[:, :, bass.ds(st * sup_cols, sup_cols)],
                                 x1[:, half].rearrange("p w j i -> p w (j i)")).then_inc(x1_out[half], 16)
                    sp.wait_ge(wx_ready, SUP * (st + 1))
                    sp.dma_start(wx_s[:, :, bass.ds(st * sup_cols, sup_cols)],
                                 wx[:, half].rearrange("p w j i -> p w (j i)")).then_inc(wx_out[half], 16)
            with sp.Fori(0, PAIRS - 1) as r:
                turn_body(r, True)
            turn_body(PAIRS - 1, False)
            for out in (*x1_out, *wx_out):
                sp.wait_ge(out, 16 * PAIRS)

        @block.gpsimd
        def _(pool):
            def step(r, k):
                if at := locate(r, k, 2, TILES):
                    turn, slot, t = at
                    pool.wait_ge(sq_high_ready, t + 1)
                    wait(pool, var_ready, t - 1)
                    nc.gpsimd.tensor_tensor(sq_low[:, slot % 2], sq[:, slot % 2], sq_high[:, slot % 2], ALU.subtract
                                            ).then_inc(sq_low_ready, 1)
                if at := locate(r, k, 10, TILES):
                    turn, slot, t = at
                    pool.wait_ge(sq1_high_ready, t + 1)
                    wait(pool, var1_ready, t - 1)
                    nc.gpsimd.tensor_tensor(sq1_low[:, slot % 2], sq1[:, slot % 2], sq1_high[:, slot % 2], ALU.subtract
                                            ).then_inc(sq1_low_ready, 1)
                if at := locate(r, k, 8, TILES):
                    turn, slot, t = at
                    pool.wait_ge(high1_ready, t + 1)
                    wait(pool, w_ready, t - 3)
                    nc.gpsimd.tensor_tensor(by_windows(x1_low, slot), tile_of(x1, slot), by_windows(x1_high, slot),
                                            ALU.subtract).then_inc(low1_ready, 1)
                at = locate(r, k, 4, TILES)
                if at and at[1] == 0:
                    turn, slot, t = at
                    wait(pool, num_ready, turn * PERIOD)
                    nc.gpsimd.tensor_copy(kvd[:], g["kvden"][:, bass.ds(turn // (PAIRS // B) * (2 * C), 2 * C)]).then_inc(kvd_ready, 1)
                if at := locate(r, k, 0, TILES):
                    turn, slot, t = at
                    pool.wait_ge(high_ready, t + 1)
                    wait(pool, q_ready, t - 3)
                    nc.gpsimd.tensor_tensor(by_rows(x_low, slot), x_line(slot), by_rows(x_high, slot), ALU.subtract
                                            ).then_inc(low_ready, 1)
            run_steps(pool, TILES, 11, step)

        @block.tensor
        def _(pe):
            def step(r, k):
                mm = nc.tensor.matmul
                if at := locate(r, k, 1, TILES):
                    turn, slot, t = at
                    pe.wait_ge(low_ready, t + 1)
                    wait(pe, squared1, t - 8)
                    wait(pe, squared, t)
                    split_product(nc, pc[:], g["cen_high"][:], None, x_high[:, slot % 4], x_low[:, slot % 4]
                                  ).then_inc(centered, 1)
                if at := locate(r, k, 7, TILES):
                    turn, slot, t = at
                    pe.wait_ge(att_ready, t + 1)
                    wait(pe, x1_ready, t)
                    mm(ppr[:], g["projT"][:], att[:, slot % 2], start=True, stop=True).then_inc(proj_ready, 1)
                if at := locate(r, k, 3, TILES):
                    turn, slot, t = at
                    pe.wait_ge(sq_low_ready, t + 1)
                    wait(pe, ln_ready, t)
                    split_product(nc, pvar[:], g["ones_high"][:], None, sq_high[:, slot % 2], sq_low[:, slot % 2]
                                  ).then_inc(var_ready, 1)
                if at := locate(r, k, 11, TILES):
                    turn, slot, t = at
                    pe.wait_ge(sq1_low_ready, t + 1)
                    wait(pe, ln1_ready, t)
                    split_product(nc, pvar1[:], g["ones_high"][:], None, sq1_high[:, slot % 2], sq1_low[:, slot % 2]
                                  ).then_inc(var1_ready, 1)
                if at := locate(r, k, 9, TILES):
                    turn, slot, t = at
                    pe.wait_ge(low1_ready, t + 1)
                    if locate(r, k, 1, TILES):
                        pe.wait_ge(squared, t + 9)
                    else:
                        pe.wait_ge(squared, TILES)
                    wait(pe, squared1, t)
                    split_product(nc, pc[:], g["cen_high"][:], None, x1_high[:, slot % 4], x1_low[:, slot % 4]
                                  ).then_inc(centered1, 1)
                if at := locate(r, k, 3, TILES):
                    turn, slot, t = at
                    wait(pe, q_scaled, t)
                    split_product(nc, pq[:], g["qcWc_high"][:, 0:C], g["qcWc_low"][:, 0:C], x_high[:, slot % 4],
                                  x_low[:, slot % 4]).then_inc(q_ready, 1)
                if at := locate(r, k, 11, TILES):
                    turn, slot, t = at
                    wait(pe, wx_ready, t)
                    split_product(nc, pw[:], g["qcWc_high"][:, C:], g["qcWc_low"][:, C:], x1_high[:, slot % 4],
                                  x1_low[:, slot % 4]).then_inc(w_ready, 1)
                if at := locate(r, k, 5, TILES):
                    turn, slot, t = at
                    if slot == 0:
                        pe.wait_ge(kvd_ready, turn + 1)
                    pe.wait_ge(q_mapped, t + 1)
                    wait(pe, lnd_ready, t)
                    mm(pden[:], kvd[:, C:2 * C], qe[:, slot % 2], start=True, stop=True).then_inc(den_ready, 1)
                    wait(pe, att_ready, t)
                    mm(pnum[:], kvd[:, 0:C], qe[:, slot % 2], start=True, stop=True).then_inc(num_ready, 1)
            run_steps(pe, TILES, 12, step)

        @block.scalar
        def _(act):
            load_ln_and_exp(act)
            a = nc.scalar.activation

            def step(r, k):
                if at := locate(r, k, 6, TILES):
                    turn, slot, t = at
                    act.wait_ge(den_ready, t + 1)
                    wait(act, proj_ready, t - 1)
                    a(att[:, slot % 2], pden[:], ACT.Ln, bias=g["eps"][:, 0:1]).then_inc(lnd_ready, 1)
                    act.wait_ge(lnd_ready, t + 1)
                    a(att[:, slot % 2], att[:, slot % 2], ACT.Exp, scale=-1.0).then_inc(z_ready, 1)
                if at := locate(r, k, 1, TILES):
                    turn, slot, t = at
                    act.wait_ge(centered, t + 1)
                    wait(act, sq_low_ready, t - 1)
                    a(sq[:, slot % 2], pc[:], ACT.Square).then_inc(squared, 1)
                if at := locate(r, k, 4, TILES):
                    turn, slot, t = at
                    act.wait_ge(q_scaled, t + 1)
                    wait(act, num_ready, t - 1)
                    a(qe[:, slot % 2], qs[:, slot % 2], ACT.Exp, bias=g["cols"][:, 0:1])
                    a(qs[:, slot % 2], qs[:, slot % 2], ACT.Relu, bias=g["cols"][:, 0:1]).then_inc(q_exped, 1)
                if at := locate(r, k, 3, TILES):
                    turn, slot, t = at
                    act.wait_ge(var_ready, t + 1)
                    wait(act, q_scaled, t - 1)
                    a(rstd[:, slot % 2], pvar[:], ACT.Ln, bias=g["eps"][:, 0:1]).then_inc(ln_ready, 1)
                    act.wait_ge(ln_ready, t + 1)
                    a(rstd[:, slot % 2], rstd[:, slot % 2], ACT.Exp, scale=-0.5).then_inc(rstd_ready, 1)
                if at := locate(r, k, 9, TILES):
                    turn, slot, t = at
                    act.wait_ge(centered1, t + 1)
                    wait(act, sq1_low_ready, t - 1)
                    a(sq1[:, slot % 2], pc[:], ACT.Square).then_inc(squared1, 1)
                if at := locate(r, k, 11, TILES):
                    turn, slot, t = at
                    act.wait_ge(var1_ready, t + 1)
                    wait(act, wx_ready, t - 1)
                    a(rstd1[:, slot % 2], pvar1[:], ACT.Ln, bias=g["eps"][:, 1:2]).then_inc(ln1_ready, 1)
                    act.wait_ge(ln1_ready, t + 1)
                    a(rstd1[:, slot % 2], rstd1[:, slot % 2], ACT.Exp, scale=-0.5).then_inc(rstd1_ready, 1)
            run_steps(act, TILES, 12, step)
            act.wait_ge(fold, 1)
            a(bn_sq[:], bn_sums[:, 1:2], ACT.Ln, bias=g["eps"][:, 1:2]).then_inc(fold, 1)
            act.wait_ge(fold, 2)
            a(bn_rs[:], bn_sq[:], ACT.Exp, scale=-0.5).then_inc(fold, 1)

        @block.vector
        def _(dve):
            v = nc.vector

            def step(r, k):
                if at := locate(r, k, 2, TILES):
                    turn, slot, t = at
                    dve.wait_ge(squared, t + 1)
                    wait(dve, var_ready, t - 1)
                    high_part(v, sq_high[:, slot % 2], sq[:, slot % 2]).then_inc(sq_high_ready, 1)
                if at := locate(r, k, 10, TILES):
                    turn, slot, t = at
                    dve.wait_ge(squared1, t + 1)
                    wait(dve, var1_ready, t - 1)
                    high_part(v, sq1_high[:, slot % 2], sq1[:, slot % 2]).then_inc(sq1_high_ready, 1)
                if at := locate(r, k, 0, TILES):
                    turn, slot, t = at
                    if slot % SUP == 0:
                        dve.wait_ge(x_in[slot // SUP], 16 * (turn + 1))
                    wait(dve, q_ready, t - 3)
                    high_part(v, by_rows(x_high, slot), x_line(slot)).then_inc(high_ready, 1)
                if at := locate(r, k, 4, TILES):
                    turn, slot, t = at
                    dve.wait_ge(rstd_ready, t + 1)
                    dve.wait_ge(q_ready, t + 1)
                    wait(dve, q_mapped, t - 1)
                    v.tensor_tensor(qs[:, slot % 2], pq[:], rstd[:, slot % 2], ALU.mult).then_inc(q_scaled, 1)
                if at := locate(r, k, 5, TILES):
                    turn, slot, t = at
                    dve.wait_ge(q_exped, t + 1)
                    v.scalar_tensor_tensor(qe[:, slot % 2], qe[:, slot % 2], 1.0, qs[:, slot % 2], ALU.min, ALU.add
                                           ).then_inc(q_mapped, 1)
                if at := locate(r, k, 6, TILES):
                    turn, slot, t = at
                    dve.wait_ge(z_ready, t + 1)
                    dve.wait_ge(num_ready, t + 1)
                    v.tensor_tensor(att[:, slot % 2], pnum[:], att[:, slot % 2], ALU.mult).then_inc(att_ready, 1)
                if at := locate(r, k, 7, TILES):
                    turn, slot, t = at
                    dve.wait_ge(proj_ready, t + 1)
                    if slot % SUP == 0:
                        wait(dve, x1_out[slot // SUP], 16 * turn)
                        wait(dve, low1_ready, t - SUP)
                    for j in range(RUN // WIN):
                        m = v.scalar_tensor_tensor(
                            tile_of(x1, slot)[:, :, j * WIN:(j + 1) * WIN],
                            ppr[:].rearrange("p (w j i) -> p w j i", w=WINDOWS, i=WIN)[:, :, j], g["cols"][:, 1:2],
                            x_line(slot)[:, :, j], ALU.add, ALU.add)
                    m.then_inc(x1_ready, 1)
                if at := locate(r, k, 8, TILES):
                    turn, slot, t = at
                    dve.wait_ge(x1_ready, t + 1)
                    wait(dve, w_ready, t - 3)
                    high_part(v, by_windows(x1_high, slot), tile_of(x1, slot)).then_inc(high1_ready, 1)
                if at := locate(r, k, 12, TILES):
                    turn, slot, t = at
                    dve.wait_ge(rstd1_ready, t + 1)
                    dve.wait_ge(w_ready, t + 1)
                    if slot % SUP == 0:
                        wait(dve, wx_out[slot // SUP], 16 * turn)
                    v.tensor_tensor(tile_of(wx, slot), pw[:].rearrange("p (w i) -> p w i", i=RUN),
                                    rstd1[:, slot % 2].rearrange("p (w i) -> p w i", i=RUN), ALU.mult
                                    ).then_inc(wx_ready, 1)
                    dve.wait_ge(wx_ready, t + 1)
                    v.bn_stats(g["bn"][:, bass.ds(t * 6, 6)], tile_of(wx, slot)).then_inc(bn_done, 1)
            run_steps(dve, TILES, 13, step)
            dve.wait_ge(bn_done, TILES)
            v.bn_aggr(bn_sums[:], g["bn"][:]).then_inc(fold, 1)
            dve.wait_ge(fold, 3)
            v.tensor_tensor(g["bnss"][:, 0:1], bn_rs[:], g["cols"][:, 2:3], ALU.mult).then_inc(fold, 1)
            dve.wait_ge(fold, 4)
            v.tensor_tensor(g["bnss"][:, 2:3], bn_sums[:, 0:1], g["bnss"][:, 0:1], ALU.mult).then_inc(fold, 1)
            dve.wait_ge(fold, 5)
            v.tensor_tensor(g["bnss"][:, 1:2], g["cols"][:, 3:4], g["bnss"][:, 2:3], ALU.subtract).then_inc(fold, 1)
            dve.wait_ge(fold, 6)


def recurrence_and_norm(nc, d, g):
    with Scope(nc, "rn") as s:
        wy = s.sb("wy", [128, 2, COLS, WIN])
        xr = s.sb("xr", [128, 2, COLS, WIN])
        seed = s.sb("seed", [128, B, CHUNKS])
        gap = s.sb("gap", [128, B, CHUNKS - 1])
        gmax, gall = s.sb("gmax", [128, 1]), s.sb("gall", [128, 1])
        again = s.sb("again", [128, 1], I32)
        sq, rstd = s.sb("sq", [128, 2, TILE]), s.sb("rstd", [128, 2, TILE])
        xn = s.sb("xn", [128, 4, TILE])
        pairs = TILE // (2 * WIN)
        tiles = COLS * WIN // TILE
        ADDS = 4
        hmax, hsum = (s.sb(nm, [128, 2, pairs, WIN]) for nm in ("hmax", "hsum"))
        pmax, psum_ = (s.sb(nm, [128, 2, pairs, WIN // 2]) for nm in ("pmax", "psum"))
        yp = s.sb("yp", [128, 2, B, WIN // 2, PH])
        gcols = COLS // GROUPS
        pv_banks = [s.ps(f"pv{i}") for i in range(GROUPS)]
        pv = [bank[:, 0:gcols] for bank in pv_banks]
        pc = [s.ps(f"pc{i}") for i in range(2)] + pv_banks[0:2]
        pvar = [s.ps(f"pvar{i}") for i in range(2)]
        product_ready = s.sems(" ".join(f"product_ready{i}" for i in range(GROUPS)))
        sum_ready = s.sems(" ".join(f"sum_ready{i}" for i in range(GROUPS)))
        y_ready = s.sems(" ".join(f"y_ready{i}" for i in range(GROUPS)))
        wx_in, x1_in = s.sems("wx_in0 wx_in1"), s.sems("x1_in0 x1_in1")
        r_out, yp_out = s.sems("r_out0 r_out1"), s.sems("yp_out0 yp_out1")
        warm_in, x2_ready, seeded, gap_ready, gmax_ready, gall_ready, again_ready, passed = s.sems(
            "warm_in x2_ready seeded gap_ready gmax_ready gall_ready again_ready passed")
        centered, squared, var_ready, ln_ready, rstd_ready, normed, r_ready = s.sems(
            "centered squared var_ready ln_ready rstd_ready normed r_ready")
        rows_pooled, pooled, yp_ready = s.sems("rows_pooled pooled yp_ready")
        block = s.block()
        WARM = 2 * WIN
        half_windows = WINDOWS // 2
        seed_flat = seed[:].rearrange("p b c -> p (b c)")

        def flat(buf, half):
            return buf[:, half].rearrange("p c i -> p (c i)")

        def cols(i):
            return slice(i * gcols, (i + 1) * gcols)

        def reruns(eng, run):
            reg = eng.alloc_register("again_" + eng.engine.name)
            eng.wait_ge(again_ready, 1)
            eng.reg_load(reg, again[0:1, 0:1])
            with eng.If_ne(reg, 0):
                with eng.Fori(1, CHUNKS) as p:
                    with eng.If_ne(reg, 0):
                        run(p)
                        wait_alone(eng, again_ready, p + 1, passed)
                        eng.reg_load(reg, again[0:1, 0:1])
                    with eng.Else():
                        eng.nop()
            with eng.Else():
                eng.nop()

        def windows(eng, body):
            for q in range(2):
                for half in range(2):
                    body(q, half)
            with eng.Fori(2, half_windows) as q:
                for half in range(2):
                    body(q, half)

        def first_step(p, q, half):
            return WARM + p * CHUNK + q * (2 * WIN) + half * WIN

        def steps_and_norms(eng, p, steps, norm):
            def body(q, half):
                steps(q, half)
                if half:
                    norm(p, q, 0)
                elif not isinstance(q, int) or q:
                    norm(p, q - 1, 1)
            windows(eng, body)
            norm(p, half_windows - 1, 1)

        def tiles_before(p, q, half):
            return (p * WINDOWS + 2 * q + half) * tiles

        @block.sync
        def _(sp):
            def load(dst, src, q, half, sem):
                sp.dma_start(flat(dst, half), d[src][bass.ds(2 * q + half, 1)].rearrange("o p c -> (o p) c")
                             ).then_inc(sem, 16)

            load(wy, "wxs", half_windows - 1, 0, warm_in)
            load(wy, "wxs", half_windows - 1, 1, warm_in)

            def store(p, q, half):
                n = tiles_before(p, q, half) + tiles
                sp.wait_ge(r_ready, n)
                sp.dma_start(d["rs"][bass.ds(2 * q + half, 1)].rearrange("o p c -> (o p) c"), flat(xr, half)
                             ).then_inc(r_out[half], 16)
                sp.wait_ge(yp_ready, n)
                sp.dma_start(d["ys"][:, :, bass.ds(2 * q + half, 1)].rearrange("p b o c -> p b (o c)"),
                             yp[:, half].rearrange("p b v i -> p b (v i)")
                             ).then_inc(yp_out[half], 16)

            def run(p):
                if isinstance(p, int):
                    for half in range(2):
                        load(xr, "x1s", 0, half, x1_in[half])
                    for i in range(GROUPS):
                        sp.wait_ge(product_ready[i], WIN + 1)
                    load(wy, "wxs", 0, 0, wx_in[0])
                    sp.wait_ge(seeded, 2)
                    load(wy, "wxs", 0, 1, wx_in[1])
                else:
                    sp.wait_ge(seeded, p + 2)
                    for half in range(2):
                        load(wy, "wxs", 0, half, wx_in[half])
                        load(xr, "x1s", 0, half, x1_in[half])

                def body(q, half):
                    wait_alone(sp, x2_ready, ADDS * (p * WINDOWS + 2 * q + half + 1), passed)
                    for i in range(GROUPS):
                        sp.wait_ge(product_ready[i], first_step(p, q, half) + WIN + 1)
                    load(wy, "wxs", q + 1, half, wx_in[half])
                    store(p, q, half)
                    sp.wait_ge(r_out[half], 16 * (half_windows * p + q + 1))
                    load(xr, "x1s", q + 1, half, x1_in[half])
                for half in range(2):
                    body(0, half)
                with sp.Fori(1, half_windows - 1) as q:
                    for half in range(2):
                        body(q, half)
                for half in range(2):
                    store(p, half_windows - 1, half)
                for out in (*r_out, *yp_out):
                    wait_alone(sp, out, 16 * half_windows * (p + 1), passed)
            run(0)
            reruns(sp, run)

        @block.tensor
        def _(pe):
            mm = nc.tensor.matmul

            def step(rhs, i, n):
                wait(pe, y_ready[i], n)
                mm(pv[i], g["VT"][:], rhs, start=True, stop=True).then_inc(product_ready[i], 1)

            pe.wait_ge(seeded, 1)
            for k in range(WARM):
                for i in range(GROUPS):
                    step(wy[:, (k - 1) // WIN, cols(i), (k - 1) % WIN] if k else seed_flat[:, cols(i)], i, k)

            def norm(p, q, half):
                n = tiles_before(p, q, half)
                for u in range(tiles + 1):
                    if u < tiles:
                        pe.wait_ge(x2_ready, ADDS * (p * WINDOWS + 2 * q + half) + u // (tiles // ADDS) + 1)
                        if u in (2, 3):
                            window_after = 0 if isinstance(q, int) and q == half_windows - 1 else WIN
                            pe.wait_ge(y_ready[u - 2], first_step(p, q, half) + WIN + window_after)
                        wait(pe, normed, n + u - 3)
                        mm(pc[u % 4][:], g["cen"][:], flat(xr, half)[:, u * TILE:(u + 1) * TILE], start=True, stop=True
                           ).then_inc(centered, 1)
                    if u:
                        pe.wait_ge(squared, n + u)
                        wait(pe, ln_ready, n + u - 2)
                        mm(pvar[(u - 1) % 2][:], g["ones"][:], sq[:, (u - 1) % 2], start=True, stop=True
                           ).then_inc(var_ready, 1)

            def run(p):
                def steps(q, half):
                    for k in range(WIN):
                        for i in range(GROUPS):
                            if k:
                                rhs = wy[:, half, cols(i), k - 1]
                            elif half:
                                rhs = wy[:, 0, cols(i), WIN - 1]
                            elif isinstance(q, int) and q == 0:
                                rhs = seed_flat[:, cols(i)]
                            else:
                                rhs = wy[:, 1, cols(i), WIN - 1]
                            if k == 0 and i < 2:
                                if half:
                                    wait(pe, normed, tiles_before(p, q, 0))
                                elif isinstance(q, int) and q == 0:
                                    wait(pe, normed, tiles_before(p, 0, 0))
                                else:
                                    wait(pe, normed, tiles_before(p, q - 1, 1))
                            step(rhs, i, first_step(p, q, half) + k)
                pe.wait_ge(seeded, p + 2)
                steps_and_norms(pe, p, steps, norm)
            run(0)
            reruns(pe, run)

        @block.vector
        def _(dve):
            v = nc.vector

            def step(half, k, i, n):
                dve.wait_ge(product_ready[i], n + 1)
                v.scalar_tensor_tensor(pv[i], wy[:, half, cols(i), k], g["bnss"][:, 0:1], pv[i], ALU.mult, ALU.add
                                       ).then_inc(sum_ready[i], 1)

            v.memset(seed[:], 0.0).then_inc(seeded, 1)
            dve.wait_ge(warm_in, 32)
            for k in range(WARM):
                for i in range(GROUPS):
                    step(k // WIN, k % WIN, i, k)
            ends = wy[:, 1, :, WIN - 1].rearrange("p (b c) -> p b c", b=B)
            for i in range(GROUPS):
                dve.wait_ge(y_ready[i], WARM)
            v.tensor_copy(seed[:, :, 1:CHUNKS], ends[:, :, 0:CHUNKS - 1]).then_inc(seeded, 1)

            def norm(p, q, half):
                n = tiles_before(p, q, half)
                for u in range(tiles + 3):
                    if u < tiles:
                        dve.wait_ge(rstd_ready, n + u + 1)
                        wait(dve, r_ready, n + u - 3)
                        wait(dve, rows_pooled, n + u - 3)
                        v.tensor_tensor(xn[:, u % 4], pc[u % 4][:], rstd[:, u % 2], ALU.mult).then_inc(normed, 1)
                    if 1 <= u < tiles + 1:
                        rows = xn[:, (u - 1) % 4].rearrange("p (i two w) -> p i two w", two=2, w=WIN)
                        dve.wait_ge(normed, n + u)
                        wait(dve, pooled, n + u - 2)
                        v.tensor_tensor(hmax[:, (u - 1) % 2], rows[:, :, 0], rows[:, :, 1], ALU.max)
                        v.tensor_tensor(hsum[:, (u - 1) % 2], rows[:, :, 0], rows[:, :, 1], ALU.add
                                        ).then_inc(rows_pooled, 1)
                    if 2 <= u < tiles + 2:
                        hm, hs = hmax[:, (u - 2) % 2], hsum[:, (u - 2) % 2]
                        dve.wait_ge(rows_pooled, n + u - 1)
                        wait(dve, yp_ready, n + u - 3)
                        v.tensor_tensor(pmax[:, (u - 2) % 2], hm[:, :, 0::2], hm[:, :, 1::2], ALU.max)
                        v.tensor_tensor(psum_[:, (u - 2) % 2], hs[:, :, 0::2], hs[:, :, 1::2], ALU.add
                                        ).then_inc(pooled, 1)
                    if 3 <= u:
                        dve.wait_ge(pooled, n + u - 2)
                        if u == 3:
                            wait(dve, yp_out[half], 16 * (half_windows * p + q))
                        b, row = (u - 3) * pairs // PH, (u - 3) * pairs % PH
                        v.scalar_tensor_tensor(yp[:, half, b, :, row:row + pairs].rearrange("p v i -> p i v"),
                                               psum_[:, (u - 3) % 2], 0.25, pmax[:, (u - 3) % 2],
                                               ALU.mult, ALU.add).then_inc(yp_ready, 1)

            def run(p):
                def steps(q, half):
                    dve.wait_ge(wx_in[half], 16 * (half_windows * p + q + 1))
                    for k in range(WIN):
                        for i in range(GROUPS):
                            step(half, k, i, first_step(p, q, half) + k)
                steps_and_norms(dve, p, steps, norm)
                for i in range(GROUPS):
                    dve.wait_ge(y_ready[i], WARM + (p + 1) * CHUNK)
                dve.wait_ge(x2_ready, ADDS * WINDOWS * (p + 1))
                v.tensor_tensor(gap[:], ends[:, :, 0:CHUNKS - 1], seed[:, :, 1:CHUNKS], ALU.subtract
                                ).then_inc(gap_ready, 1)
                dve.wait_ge(gap_ready, p + 1)
                v.tensor_reduce(gmax[:], gap[:], AX.XY, ALU.max, apply_absolute_value=True).then_inc(gmax_ready, 1)
                v.tensor_copy(seed[:, :, 1:CHUNKS], ends[:, :, 0:CHUNKS - 1]).then_inc(seeded, 1)
                dve.wait_ge(gall_ready, p + 1)
                v.tensor_scalar(again[:], gall[:], SEAM_TOL, None, ALU.is_gt).then_inc(again_ready, 1)
            run(0)
            reruns(dve, run)

        @block.scalar
        def _(act):
            a = nc.scalar.activation

            def step(half, k, i, n):
                act.wait_ge(sum_ready[i], n + 1)
                a(wy[:, half, cols(i), k], pv[i], ACT.Sigmoid, bias=g["bnss"][:, 1:2]).then_inc(y_ready[i], 1)

            for k in range(WARM):
                for i in range(GROUPS):
                    step(k // WIN, k % WIN, i, k)

            def norm(p, q, half):
                n = tiles_before(p, q, half)
                load_ln_and_exp(act)
                for u in range(tiles + 2):
                    if 2 <= u:
                        act.wait_ge(var_ready, n + u - 1)
                        wait(act, normed, n + u - 3)
                        a(rstd[:, u % 2], pvar[u % 2][:], ACT.Ln, bias=g["eps"][:, 0:1]).then_inc(ln_ready, 1)
                    if u < tiles:
                        act.wait_ge(centered, n + u + 1)
                        wait(act, var_ready, n + u - 1)
                        a(sq[:, u % 2], pc[u % 4][:], ACT.Square).then_inc(squared, 1)
                    if 2 <= u:
                        act.wait_ge(ln_ready, n + u - 1)
                        a(rstd[:, u % 2], rstd[:, u % 2], ACT.Exp, scale=-0.5).then_inc(rstd_ready, 1)

            def run(p):
                act.wait_ge(seeded, p + 2)

                def steps(q, half):
                    for k in range(WIN):
                        for i in range(GROUPS):
                            step(half, k, i, first_step(p, q, half) + k)
                steps_and_norms(act, p, steps, norm)
            run(0)
            reruns(act, run)

        @block.gpsimd
        def _(pool):
            t = nc.gpsimd.tensor_tensor

            def run(p):
                def body(q, half):
                    n = tiles_before(p, q, half)
                    pool.wait_ge(x1_in[half], 16 * (half_windows * p + q + 1))
                    for i in range(GROUPS):
                        pool.wait_ge(y_ready[i], first_step(p, q, half) + WIN)
                    for j in range(ADDS):
                        c = slice(j * COLS // ADDS, (j + 1) * COLS // ADDS)
                        t(xr[:, half, c], xr[:, half, c], wy[:, half, c], ALU.add).then_inc(x2_ready, 1)
                    for u in range(tiles):
                        c = slice(u * TILE, (u + 1) * TILE)
                        pool.wait_ge(normed, n + u + 1)
                        t(flat(xr, half)[:, c], flat(xr, half)[:, c], xn[:, u % 4], ALU.add).then_inc(r_ready, 1)
                windows(pool, body)
                wait_alone(pool, gmax_ready, p + 1, passed)
                nc.gpsimd.partition_all_reduce(gall[:], gmax[:], 128, bass.bass_isa.ReduceOp.max
                                               ).then_inc(gall_ready, 1)
            run(0)
            reruns(pool, run)


def spectral(nc, d, g):
    n = PH
    last = n // 2
    fours = n // 4
    fpairs = (NK + 1) // 2
    with Scope(nc, "sg") as s:
        ya = s.sb("ya", [128, n * n])
        yb = s.sb("yb", [128, 2 * NK * n])
        q = s.sb("q", [128, n * n])
        work = s.sb("work", [128, 32 * n + 16])
        f = work[:, 0:8 * n].rearrange("p (j a) -> p j a", j=2)
        ge, gc = work[:, 8 * n:12 * n], work[:, 12 * n:16 * n]
        m1 = work[:, 16 * n + 16:24 * n + 16].rearrange("p (j u r k) -> p j u r k", j=2, u=2, r=2)
        m2 = work[:, 24 * n + 16:32 * n + 16].rearrange("p (j u r k) -> p j u r k", j=2, u=2, r=2)
        out = work[:, 8 * n:16 * n + 16].rearrange("p (j h w) -> p j h w", j=2, h=4)
        w12 = work[:, 16 * n + 16:24 * n + 16]
        dft = s.sb("dft", [128, 7 * n])
        mixm = s.sb("mixm", [128, 4 * n])
        bias = s.sb("bias", [128, 2, 2, n])
        pb = [s.ps(f"pb{i}") for i in range(8)]
        w_in, mix_ready, mix_kept, y_in = s.sems("w_in mix_ready mix_kept y_in")
        t_ready, rows_ready, f_ready, f_kept, mixed = s.sems("t_ready rows_ready f_ready f_kept mixed")
        t_kept, rows_kept, inv_kept = (s.sems(f"{x}_by_act {x}_by_dve") for x in ("t_kept", "rows_kept", "inv_kept"))
        g_done, prod_ready, z_ready, inv_ready, fin_ready, fin_kept, fin_done = s.sems(
            "g_done prod_ready z_ready inv_ready fin_ready fin_kept fin_done")
        y_out = s.sems("y_out0 y_out1")
        edge_out, passed, batch_free = s.sems("edge_out passed batch_free")
        block = s.block()
        RW, CS, SC, C_, S_, B1, B2 = (dft[:, a * n:b * n] for a, b in
                                      ((0, 1), (1, 3), (3, 5), (1, 2), (3, 4), (5, 6), (6, 7)))

        def re_slot(freq):
            return {0: 0, last: 1}.get(freq, 1 + freq)

        def im_slot(freq):
            return {0: 2 * last, last: 2 * last + 1}.get(freq, last + freq)

        @block.sync
        def _(sp):
            for dst, src in ((dft[:], d["dft"]), (w12, d["w12"])):
                sp.dma_start(dst, src).then_inc(w_in, 16)
            sp.wait_ge(mix_kept, 11)

            with sp.Fori(0, B) as b:
                sp.wait_ge(batch_free, b + 1)
                sp.dma_start(ya[:], d["ys"][:, bass.ds(b, 1)].rearrange("p o w c -> p (o w c)")).then_inc(y_in, 16)
                for i in range(2, fours + 2):
                    half = i % 2
                    sp.wait_ge(fin_done, b * fours + i - 1)
                    sp.dma_start(d["y2s"][:, bass.ds(b * (n + 2) + 4 * (i - 2) + 1, 4), :], out[:, half]
                                 ).then_inc(y_out[half], 16)
                    if i == 2:
                        sp.dma_start(d["y2s"][:, bass.ds(b * (n + 2), 1), :], out[:, 0, 0:1]
                                     ).then_inc(edge_out, 16)
                        wait_alone(sp, edge_out, b * 32 + 16, passed)
                    if i == fours + 1:
                        sp.dma_start(d["y2s"][:, bass.ds(b * (n + 2) + n + 1, 1), :], out[:, 1, 3:4]
                                     ).then_inc(edge_out, 16)
                        wait_alone(sp, edge_out, b * 32 + 32, passed)
                for half in range(2):
                    wait_alone(sp, y_out[half], b * (8 * fours) + 8 * fours, passed)

        @block.tensor
        def _(pe):
            mm = nc.tensor.matmul
            pe.wait_ge(w_in, 32)
            w1r, w1i, w2r, w2i, b1r, b1i = (w12[:, i * n:(i + 1) * n] for i in range(6))
            for j, (lr, li) in enumerate(((w1r, w1i), (b1r, b1i))):
                mm(pb[4 * j][:, 0:n], lr, w2r, start=True, stop=True)
                mm(pb[4 * j + 1][:, 0:n], li, w2i, start=True, stop=True)
                mm(pb[4 * j + 2][:, 0:n], lr, w2i, start=True, stop=False)
                mm(pb[4 * j + 2][:, 0:n], li, w2r, start=False, stop=True).then_inc(mix_ready, 1)
            pe.wait_ge(mix_kept, 11)

            with pe.Fori(0, B) as b:
                pe.wait_ge(y_in, b * 16 + 16)
                for i in range(fours):
                    if i >= 4:
                        pe.wait_ge(t_kept[i % 2], b * (fours // 2) + i // 2 - 1)
                    for h in range(4):
                        m = nc.tensor.transpose(pb[i % 4][:, h * n:(h + 1) * n], ya[:, 4 * i + h:n * n:n], g["iden"][:])
                    m.then_inc(t_ready, 1)
                for e in range(2):
                    pe.wait_ge(t_kept[e], b * (fours // 2) + fours // 2)
                for i in range(fours):
                    if i >= 4:
                        pe.wait_ge(rows_kept[i % 2], b * (fours // 2) + i // 2 - 1)
                    for c in range(4):
                        m = mm(pb[4 + i % 4][:, c * n:(c + 1) * n], yb[:, 4 * i + c:n * n:n], RW, start=True, stop=True)
                    m.then_inc(rows_ready, 1)
                for e in range(2):
                    pe.wait_ge(rows_kept[e], b * (fours // 2) + fours // 2)
                for j in range(fpairs + 1):
                    if j < fpairs:
                        if j >= 2:
                            pe.wait_ge(f_kept, b * fpairs + j - 1)
                        for u, freq in enumerate(range(2 * j, min(2 * j + 2, NK))):
                            o = pb[j % 2][:, u * 2 * n:(u + 1) * 2 * n]
                            both = 0 < freq < last
                            m = mm(o, q[:, re_slot(freq):n * n:n], CS, start=True, stop=not both)
                            if both:
                                m = mm(o, q[:, im_slot(freq):n * n:n], SC, start=False, stop=True)
                        m.then_inc(f_ready, 1)
                    if j:
                        i = j - 1
                        pe.wait_ge(f_kept, b * fpairs + i + 1)
                        if i >= 2:
                            pe.wait_ge(prod_ready, b * fpairs + i - 1)
                        live = min(2, NK - 2 * i)
                        for u in range(2 * live):
                            nc.tensor.transpose(pb[2 + i % 2][:, u * n:(u + 1) * n], f[:, i % 2, u * n:(u + 1) * n], g["iden"][:])
                        for u in range(live):
                            o = pb[4 + i % 2][:, u * 2 * n:(u + 1) * 2 * n]
                            mm(o, f[:, i % 2, 2 * u * n:(2 * u + 1) * n], mixm[:, 0:2 * n], start=True, stop=False)
                            m = mm(o, f[:, i % 2, (2 * u + 1) * n:(2 * u + 2) * n], mixm[:, 2 * n:4 * n],
                                   start=False, stop=True)
                        m.then_inc(mixed, 1)
                pe.wait_ge(z_ready, b * fpairs + fpairs)
                for i in range(fours):
                    if i >= 2:
                        for e in range(2):
                            pe.wait_ge(inv_kept[e], b * fours + i - 1)
                    for c in range(4):
                        ch = 4 * i + c
                        mm(pb[i % 2][:, c * n:(c + 1) * n], yb[:, ch:n * n:n], C_, start=True, stop=True)
                    for c in range(4):
                        ch = 4 * i + c
                        m = mm(pb[2 + i % 2][:, c * n:(c + 1) * n], yb[:, 2 * n + ch:n * n + 2 * n:n], S_,
                               start=True, stop=True)
                    m.then_inc(inv_ready, 1)
                for e in range(2):
                    pe.wait_ge(inv_kept[e], b * fours + fours)
                for i in range(fours):
                    if i >= 2:
                        pe.wait_ge(fin_kept, b * fours + i - 1)
                    for h in range(4):
                        row = 4 * i + h
                        o = pb[4 + i % 2][:, h * n:(h + 1) * n]
                        mm(o, ya[:, row:n * n:n], B1, start=True, stop=False)
                        m = mm(o, q[:, row:n * n:n], B2, start=False, stop=True)
                    m.then_inc(fin_ready, 1)

        def evacuate(eng, copy, e, b):
            for i in range(e, fours, 2):
                eng.wait_ge(t_ready, b * fours + i + 1)
                copy(yb[:, 4 * i * n:4 * (i + 1) * n], pb[i % 4][:]).then_inc(t_kept[e], 1)
            for i in range(e, fours, 2):
                eng.wait_ge(rows_ready, b * fours + i + 1)
                copy(q[:, 4 * i * n:4 * (i + 1) * n], pb[4 + i % 4][:]).then_inc(rows_kept[e], 1)

        @block.scalar
        def _(act):
            with act.Fori(0, B) as b:
                evacuate(act, nc.scalar.copy, 0, b)
                for j in range(fpairs):
                    act.wait_ge(f_ready, b * fpairs + j + 1)
                    if j >= 2:
                        act.wait_ge(mixed, b * fpairs + j - 1)
                    w = min(2, NK - 2 * j) * 2 * n
                    nc.scalar.copy(f[:, j % 2, 0:w], pb[j % 2][:, 0:w]).then_inc(f_kept, 1)
                for i in range(fours):
                    act.wait_ge(inv_ready, b * fours + i + 1)
                    nc.scalar.copy(ya[:, 4 * i * n:4 * (i + 1) * n], pb[i % 2][:]).then_inc(inv_kept[0], 1)

        @block.vector
        def _(dve):
            v = nc.vector
            kept = [0]

            def chain(ins):
                ins.then_inc(mix_kept, 1)
                kept[0] += 1
                dve.wait_ge(mix_kept, kept[0])
            dve.wait_ge(mix_ready, 2)
            chain(v.tensor_copy(gc[:, 0:n], pb[1][:, 0:n]))
            chain(v.tensor_copy(gc[:, n:2 * n], pb[5][:, 0:n]))
            chain(v.tensor_tensor(mixm[:, 0:n], pb[0][:, 0:n], gc[:, 0:n], ALU.subtract))
            chain(v.tensor_copy(mixm[:, 3 * n:4 * n], mixm[:, 0:n]))
            chain(v.tensor_copy(mixm[:, n:2 * n], pb[2][:, 0:n]))
            chain(v.tensor_scalar(mixm[:, 2 * n:3 * n], pb[2][:, 0:n], -1.0, None, ALU.mult))
            chain(v.tensor_tensor(gc[:, 2 * n:3 * n], pb[4][:, 0:n], gc[:, n:2 * n], ALU.subtract))
            chain(v.tensor_tensor(bias[:, 0, 0], gc[:, 2 * n:3 * n], w12[:, 6 * n:7 * n], ALU.add))
            chain(v.tensor_tensor(bias[:, 0, 1], pb[6][:, 0:n], w12[:, 7 * n:8 * n], ALU.add))
            chain(v.tensor_copy(bias[:, 1, 0], bias[:, 0, 0]))
            chain(v.tensor_copy(bias[:, 1, 1], bias[:, 0, 1]))

            dve.sem_inc(batch_free, 1)
            with dve.Fori(0, B) as b:
                evacuate(dve, v.tensor_copy, 1, b)
                for j in range(fpairs):
                    live = min(2, NK - 2 * j)
                    w = live * 2 * n
                    done = b * (3 * fpairs) + 3 * j
                    pT = pb[2 + j % 2][:].rearrange("p (u r k) -> p u r k", u=2, r=2)
                    gv = ge.rearrange("p (u r k) -> p u r k", u=2, r=2)
                    dve.wait_ge(mixed, b * fpairs + j + 1)
                    if j:
                        dve.wait_ge(prod_ready, b * fpairs + j)
                    v.tensor_tensor(ge[:, 0:w], pb[4 + j % 2][:, 0:w], bias[:].rearrange("p u r k -> p (u r k)")[:, 0:w],
                                    ALU.add).then_inc(g_done, 1)
                    dve.wait_ge(g_done, done + 1)
                    v.tensor_scalar(gc[:, 0:w], ge[:, 0:w], LAMBD, -LAMBD, ALU.min, ALU.max).then_inc(g_done, 1)
                    dve.wait_ge(g_done, done + 2)
                    cv = gc.rearrange("p (u r k) -> p u r k", u=2, r=2)
                    v.scalar_tensor_tensor(gv[:, 0:live, 0], gv[:, 0:live, 0], 1.0, cv[:, 0:live, 0], ALU.add, ALU.subtract)
                    v.tensor_tensor(gv[:, 0:live, 1], gv[:, 0:live, 1], cv[:, 0:live, 1], ALU.subtract
                                    ).then_inc(g_done, 1)
                    dve.wait_ge(g_done, done + 3)
                    if j >= 2:
                        dve.wait_ge(z_ready, b * fpairs + j - 1)
                    v.tensor_tensor(m1[:, j % 2, 0:live], gv[:, 0:live], pT[:, 0:live], ALU.mult)
                    v.tensor_tensor(m2[:, j % 2, 0:live, 0], gv[:, 0:live, 0], pT[:, 0:live, 1], ALU.mult)
                    m = v.tensor_tensor(m2[:, j % 2, 0:live, 1], gv[:, 0:live, 1], pT[:, 0:live, 0], ALU.mult)
                    m.then_inc(prod_ready, 1)
                for i in range(fours):
                    dve.wait_ge(inv_ready, b * fours + i + 1)
                    v.tensor_copy(q[:, 4 * i * n:4 * (i + 1) * n], pb[2 + i % 2][:]).then_inc(inv_kept[1], 1)
                for i in range(fours):
                    half = i % 2
                    dve.wait_ge(fin_ready, b * fours + i + 1)
                    if i >= 2:
                        dve.wait_ge(y_out[half], b * (8 * fours) + 16 * (i // 2))
                    if i == 2:
                        dve.wait_ge(edge_out, b * 32 + 16)
                    v.tensor_copy(out[:, half, :, 1:n + 1], pb[4 + half][:].rearrange("p (h w) -> p h w", h=4)
                                  ).then_inc(fin_kept, 1)
                    dve.wait_ge(fin_kept, b * fours + i + 1)
                    v.tensor_copy(out[:, half, :, 0:n + 2:n + 1], out[:, half, :, 1:n + 1:n - 1]).then_inc(fin_done, 1)
                wait_alone(dve, fin_done, b * fours + fours, batch_free)

        @block.gpsimd
        def _(pool):
            t = nc.gpsimd.tensor_tensor
            z = yb[:].rearrange("p (s c) -> p s c", c=n)
            with pool.Fori(0, B) as b:
                for j in range(fpairs):
                    pool.wait_ge(prod_ready, b * fpairs + j + 1)
                    runs = [(0, 1), (1, 1)] if j == 0 else [(0, min(2, NK - 2 * j))]
                    for u, k in runs:
                        freq = 2 * j + u
                        zr, zi = re_slot(freq), im_slot(freq)
                        t(z[:, zr:zr + k], m1[:, j % 2, u:u + k, 0], m1[:, j % 2, u:u + k, 1], ALU.subtract)
                        m = t(z[:, zi:zi + k], m2[:, j % 2, u:u + k, 0], m2[:, j % 2, u:u + k, 1], ALU.add)
                    m.then_inc(z_ready, 1)


def experts_scan(nc, d, g):
    n = PH
    r_s = d["rs"].rearrange("w p c -> p w c")
    with Scope(nc, "es") as s:
        rr = s.sb("rr", [128, 2, WINDOWS, SUP, RUN])
        y2 = s.sb("y2", [128, 2, SUP + 2, n + 2])
        y25 = s.sb("y25", [128, 2, SUP + 2, n + 2])
        vv, v25 = s.sb("vv", [128, 2, 2, n + 2]), s.sb("v25", [128, 2, 2, n + 2])
        up = s.sb("up", [128, 2, 2, n, 2])
        x3 = s.sb("x3", [128, 2, STOK])
        xt = s.sb("xt", [128, 2, SUP, 4, C])
        sq, lnv, rstd = (s.sb(nm, [128, 2, TILE]) for nm in ("sq", "lnv", "rstd"))
        lg = s.sb("lg", [128, 2, STOK // 2])
        le = s.sb("le", [128, STOK // 2])
        top, topi = s.sb("top", [128, 2, TOPK]), s.sb("topi", [128, 2, TOPK], U32)
        ntop, es = s.sb("ntop", [128, 2, 1]), s.sb("es", [128, 2, 1])
        junk = s.sb("junk", [128, 2])
        pc = [s.ps(f"pc{i}") for i in range(2)]
        pvar = [s.ps(f"pvar{i}") for i in range(2)]
        pg = [s.ps(f"pg{i}") for i in range(2)]
        pt = [s.ps(f"pt{i}") for i in range(2)]
        turned, xt_ready, passed = s.sems("turned xt_ready passed")
        xt_out = s.sems("xt_out0 xt_out1")
        r_in, y_in, x3_out = s.sems("r_in0 r_in1"), s.sems("y_in0 y_in1"), s.sems("x3_out0 x3_out1")
        y25_ready, v_ready, v25_ready, up_ready, x3_ready = s.sems("y25_ready v_ready v25_ready up_ready x3_ready")
        centered, squared, var_ready, ln_ready, rstd_ready, gate_ready, scaled = s.sems(
            "centered squared var_ready ln_ready rstd_ready gate_ready scaled")
        biased, top_ready, topi_ready, ntop_ready, sum_ready, exped, noted = s.sems(
            "biased top_ready topi_ready ntop_ready sum_ready exped noted")
        block = s.block()

        def line(buf, slot):
            return buf[:, slot // SUP, (slot % SUP) * TILE:(slot % SUP + 1) * TILE]

        @block.sync
        def _(sp):
            def load(st, half):
                b = st // (SUPERS // B)
                sp.dma_start(rr[:, half].rearrange("p w j i -> p w (j i)"),
                             r_s[:, :, bass.ds(st * (SUP * RUN), SUP * RUN)]).then_inc(r_in[half], 16)
                sp.dma_start(y2[:, half], d["y2s"][:, bass.ds(b * (n + 2) + st % (SUPERS // B) * SUP, SUP + 2), :]
                             ).then_inc(y_in[half], 16)
            load(0, 0)
            load(1, 1)

            def turn_body(turn, more):
                for half in range(2):
                    st = turn * 2 + half
                    sp.wait_ge(x3_ready, SUP * (st + 1))
                    if more:
                        load(st + 2, half)
                    b = st // (SUPERS // B)
                    sp.dma_start(d["outflat"][:, bass.ds(b, 1), bass.ds(st % (SUPERS // B) * STOK, STOK)],
                                 x3[:, half]).then_inc(x3_out[half], 16)
                    sp.wait_ge(xt_ready, SUP * (st + 1))
                    sp.dma_start(d["x3t"][bass.ds(st, 1)].rearrange("o (j p) c -> (o p) j c", p=128),
                                 xt[:, half].rearrange("p j q c -> p (j q) c")).then_inc(xt_out[half], 16)
            with sp.Fori(0, PAIRS - 1) as r:
                turn_body(r, True)
            turn_body(PAIRS - 1, False)
            for half in range(2):
                sp.wait_ge(x3_out[half], 16 * PAIRS)
                sp.wait_ge(xt_out[half], 16 * PAIRS)

        @block.tensor
        def _(pe):
            mm = nc.tensor.matmul

            def step(r, k):
                if at := locate(r, k, 4, TILES):
                    turn, slot, t = at
                    pe.wait_ge(x3_ready, t + 1)
                    wait(pe, squared, t - 1)
                    mm(pc[slot % 2][:], g["cen"][:], line(x3, slot), start=True, stop=True).then_inc(centered, 1)
                if at := locate(r, k, 5, TILES):
                    turn, slot, t = at
                    pe.wait_ge(squared, t + 1)
                    wait(pe, ln_ready, t - 1)
                    mm(pvar[slot % 2][:], g["ones"][:], sq[:, slot % 2], start=True, stop=True).then_inc(var_ready, 1)
                    wait(pe, xt_ready, t - 1)
                    for q in range(4):
                        m = nc.tensor.transpose(pt[slot % 2][:, q * 128:(q + 1) * 128],
                                                line(x3, slot)[:, q * 128:(q + 1) * 128], g["iden"][:])
                    m.then_inc(turned, 1)
                if at := locate(r, k, 6, TILES):
                    turn, slot, t = at
                    rows = slice(64 * (slot % SUP // 4), 64 * (slot % SUP // 4) + 64)
                    wait(pe, scaled, t - 1)
                    mm(pg[slot % 2][rows, :], g["qcWcGc"][:, 2 * C:2 * C + EXPERTS], line(x3, slot),
                       start=True, stop=True).then_inc(gate_ready, 1)
            run_steps(pe, TILES, 7, step)

        @block.scalar
        def _(act):
            load_ln_and_exp(act)
            a = nc.scalar.activation

            def step(r, k):
                at = locate(r, k, 0, TILES)
                if at and at[1] % SUP == 0:
                    turn, slot, t = at
                    st, half = turn * 2 + slot // SUP, slot // SUP
                    act.wait_ge(y_in[half], 16 * (turn + 1))
                    wait(act, v_ready, t - SUP)
                    a(y25[:, half], y2[:, half], ACT.Copy, scale=0.25).then_inc(y25_ready, 1)
                if at := locate(r, k, 6, TILES):
                    turn, slot, t = at
                    act.wait_ge(var_ready, t + 1)
                    a(lnv[:, slot % 2], pvar[slot % 2][:], ACT.Ln, bias=g["eps"][:, 1:2]).then_inc(ln_ready, 1)
                if at := locate(r, k, 4, TILES):
                    turn, slot, t = at
                    act.wait_ge(centered, t + 1)
                    wait(act, var_ready, t - 1)
                    a(sq[:, slot % 2], pc[slot % 2][:], ACT.Square).then_inc(squared, 1)
                if at := locate(r, k, 6, TILES):
                    turn, slot, t = at
                    act.wait_ge(ln_ready, t + 1)
                    wait(act, scaled, t - 1)
                    a(rstd[:, slot % 2], lnv[:, slot % 2], ACT.Exp, scale=-0.5).then_inc(rstd_ready, 1)
                if at := locate(r, k, 6, TILES):
                    turn, slot, t = at
                    act.wait_ge(turned, t + 1)
                    if slot % SUP == 0:
                        wait(act, xt_out[slot // SUP], 16 * turn)
                    a(xt[:, slot // SUP, slot % SUP].rearrange("p q c -> p (q c)"), pt[slot % 2][:], ACT.Copy
                      ).then_inc(xt_ready, 1)
                at = locate(r, k, 10, TILES)
                if at and at[1] % SUP == SUP - 1:
                    turn, slot, t = at
                    st, half = turn * 2 + slot // SUP, slot // SUP
                    act.wait_ge(ntop_ready, st + 1)
                    wait(act, sum_ready, st)
                    wait(act, exped, st)
                    a(le[:], lg[:, half], ACT.Exp, bias=ntop[:, half], accum_out=es[:, half]).then_inc(exped, 1)
            run_steps(act, TILES, 11, step)

        @block.vector
        def _(dve):
            v = nc.vector

            def step(r, k):
                if at := locate(r, k, 2, TILES):
                    turn, slot, t = at
                    dve.wait_ge(v25_ready, t + 1)
                    wait(dve, x3_ready, t - 1)
                    for odd in range(2):
                        m = v.scalar_tensor_tensor(up[:, slot % 2, :, :, odd], vv[:, slot % 2, :, 1:n + 1], 0.75,
                                                   v25[:, slot % 2, :, 2 * odd:2 * odd + n], ALU.mult, ALU.add)
                    m.then_inc(up_ready, 1)
                if at := locate(r, k, 0, TILES):
                    turn, slot, t = at
                    st, half, i = turn * 2 + slot // SUP, slot // SUP, slot % SUP
                    dve.wait_ge(y25_ready, st + 1)
                    wait(dve, up_ready, t - 1)
                    wait(dve, v25_ready, t - 1)
                    v.scalar_tensor_tensor(vv[:, slot % 2], y2[:, half, i + 1:i + 2].to_broadcast([128, 2, n + 2]),
                                           0.75, y25[:, half, i:i + 3:2], ALU.mult, ALU.add).then_inc(v_ready, 1)
                if at := locate(r, k, 7, TILES):
                    turn, slot, t = at
                    rows = slice(64 * (slot % SUP // 4), 64 * (slot % SUP // 4) + 64)
                    cols = slice((slot % 4) * TILE, (slot % 4 + 1) * TILE)
                    dve.wait_ge(rstd_ready, t + 1)
                    dve.wait_ge(gate_ready, t + 1)
                    if slot % SUP == 0:
                        wait(dve, exped, turn * 2 + slot // SUP - 1)
                    v.tensor_tensor(lg[rows, slot // SUP, cols], pg[slot % 2][rows, :], rstd[rows, slot % 2], ALU.mult
                                    ).then_inc(scaled, 1)
                at = locate(r, k, 8, TILES)
                if at and at[1] % SUP == SUP - 1:
                    turn, slot, t = at
                    st, half = turn * 2 + slot // SUP, slot // SUP
                    dve.wait_ge(scaled, t + 1)
                    v.tensor_scalar(lg[:, half], lg[:, half], g["gateb"][:], None, ALU.add).then_inc(biased, 1)
                    dve.wait_ge(biased, st + 1)
                    v.tensor_copy(junk[:, 0:1], lg[:, half, 0:1])
                    v.max(top[:, half], lg[:, half]).then_inc(top_ready, 1)
                    dve.wait_ge(top_ready, st + 1)
                    v.tensor_scalar(ntop[:, half], top[:, half, 0:1], -1.0, None, ALU.mult).then_inc(ntop_ready, 1)
                    v.max_index(topi[:, half], top[:, half], lg[:, half]).then_inc(topi_ready, 1)
                    dve.wait_ge(topi_ready, st + 1)
                    v.tensor_copy(g["cand"][:, bass.ds(st * TOPK, TOPK)], top[:, half])
                    v.tensor_copy(g["candi"][:, bass.ds(st * TOPK, TOPK)], topi[:, half]).then_inc(noted, 1)
                at = locate(r, k, 11, TILES)
                if at and at[1] % SUP == SUP - 1:
                    turn, slot, t = at
                    st, half = turn * 2 + slot // SUP, slot // SUP
                    dve.wait_ge(exped, st + 1)
                    v.tensor_copy(g["cands"][:, bass.ds(st, 1)], es[:, half]).then_inc(sum_ready, 1)
            run_steps(dve, TILES, 12, step)
            dve.wait_ge(noted, SUPERS)
            dve.wait_ge(sum_ready, SUPERS)

        @block.gpsimd
        def _(pool):
            def step(r, k):
                if at := locate(r, k, 3, TILES):
                    turn, slot, t = at
                    half = slot // SUP
                    if slot % SUP == 0:
                        pool.wait_ge(r_in[half], 16 * (turn + 1))
                        wait(pool, x3_out[half], 16 * turn)
                        wait(pool, turned, t - SUP)
                        wait(pool, gate_ready, t - SUP)
                    pool.wait_ge(up_ready, t + 1)
                    nc.gpsimd.tensor_tensor(
                        line(x3, slot).rearrange("p (j w i) -> p j w i", w=WINDOWS, i=WIN),
                        rr[:, half, :, slot % SUP].rearrange("p w (j i) -> p j w i", i=WIN),
                        up[:, slot % 2].rearrange("p a (w v) o -> p a w (v o)", w=WINDOWS), ALU.add
                        ).then_inc(x3_ready, 1)
                if at := locate(r, k, 1, TILES):
                    turn, slot, t = at
                    wait(pool, up_ready, t - 1)
                    wait_alone(pool, v_ready, t + 1, passed)
                    nc.gpsimd.tensor_scalar(v25[:, slot % 2], vv[:, slot % 2], 0.25, None, ALU.mult
                                            ).then_inc(v25_ready, 1)
            run_steps(pool, TILES, 4, step)


def experts_apply(nc, d, g):
    BK = B * TOPK
    J = BK * EXPERTS
    NCAND = SUPERS // B * 2 * TOPK
    HC = HID // 128
    EB = EXPERTS * B
    EK = EXPERTS * TOPK
    PER = 8
    TURNS = EXPERTS // (2 * PER)
    with Scope(nc, "ea") as s:
        V, TK = s.sb("V", [EXPERTS, SUPERS, 2, TOPK]), s.sb("TK", [EXPERTS, SUPERS, 2, TOPK])
        SM = s.sb("SM", [EXPERTS, SUPERS, 2])
        off, iota = s.sb("off", [EXPERTS, SUPERS * 2 * TOPK]), s.sb("iota", [EXPERTS, NCAND])
        junk = s.sb("junk", [EXPERTS, NCAND])
        tv, tok, pk = (s.sb(nm, [EXPERTS, B, TOPK]) for nm in ("tv", "tok", "pk"))
        pos, posf = s.sb("pos", [EXPERTS, B, TOPK], U32), s.sb("posf", [EXPERTS, B, TOPK])
        toki, rowi = s.sb("toki", [EXPERTS, B, TOPK], I32), s.sb("rowi", [EXPERTS, B, TOPK], U32)
        ntop, zs, rz = (s.sb(nm, [EXPERTS, B]) for nm in ("ntop", "zs", "rz"))
        em = s.sb("em", [EXPERTS, B, SUPERS // B * 2])
        tokrow = s.sb("tokrow", [1, J], I32)
        tokall = s.sb("tokall", [EXPERTS, B, TOPK, EXPERTS])
        xg, xh, sq = (s.sb(nm, [EXPERTS, BK, C]) for nm in ("xg", "xh", "sq"))
        mean, var, rstd = (s.sb(nm, [EXPERTS, BK]) for nm in ("mean", "var", "rstd"))
        pooled_e = s.sb("pooled_e", [EXPERTS, B, C])
        pooled = s.sb("pooled", [128, B, EXPERTS])
        wbuf = s.sb("wbuf", [128, 2, PER, HID])
        wb1, wb2 = s.sb("wb1", [128, EXPERTS, HC]), s.sb("wb2", [128, EXPERTS])
        hb, hh = (s.sb(nm, [128, EXPERTS * HC, B]) for nm in ("hb", "hh"))
        ob = s.sb("ob", [128, B, EXPERTS])
        oe = s.sb("oe", [EXPERTS, B, C])
        wt = s.sb("wt", [EXPERTS, 2, C])
        same = s.sb("same", [EXPERTS, 2, EK])
        new = s.sb("new", [128, B, TOPK, EXPERTS])
        ptr, pA, pB, pN = s.ps("ptr"), s.ps("pA"), s.ps("pB", (128, 2 * TILE)), s.ps("pN", (128, B * TILE))
        c_in, merged, em_ready, rows_out, rows_in, got = s.sems("c_in merged em_ready rows_out rows_in got")
        centered, squared, var_ready, ln_ready, rstd_ready, pooled_ready, turned = s.sems(
            "centered squared var_ready ln_ready rstd_ready pooled_ready turned")
        w_in = s.sems("w_in0 w_in1")
        hid_ready, hb_ready, act_ready, o_ready, out_steps, same_ready, summed, new_ready = s.sems(
            "hid_ready hb_ready act_ready o_ready out_steps same_ready summed new_ready")
        put_by_sp, put_by_act, put_by_pool, rest_by_act, rest_by_pool, passed = s.sems(
            "put_by_sp put_by_act put_by_pool rest_by_act rest_by_pool passed")
        block = s.block()
        xt = d["outflat"]
        MERGES = 4 + B * (3 + TOPK)

        def put(eng, e, b, ranks, sem):
            for k in ranks:
                t = eng.value_load(tokrow[0:1, bass.ds(e * BK + (b * TOPK + k), 1)], min_val=0, max_val=TOK - 1)
                eng.dma_start(xt[:, b, bass.ds(t, 1)], new[:, b, k, bass.ds(e, 1)], allow_slow_non_contiguous=True
                              ).then_inc(sem, 16)

        MINE = 5

        @block.sync
        def _(sp):
            for half in range(2):
                rows = slice(64 * half, 64 * half + 64)
                sp.dma_start(V[:, :, half], g["cand"][rows].rearrange("p (s k) -> p s k", k=TOPK)).then_inc(c_in, 16)
                sp.dma_start(TK[:, :, half], g["candi"][rows].rearrange("p (s k) -> p s k", k=TOPK)).then_inc(c_in, 16)
                sp.dma_start(SM[:, :, half], g["cands"][rows], allow_slow_non_contiguous=True).then_inc(c_in, 16)
            sp.dma_start(off[:], d["tokoff"].to_broadcast([EXPERTS, SUPERS * 2 * TOPK])).then_inc(c_in, 16)
            sp.dma_start(iota[:], d["iota"].to_broadcast([EXPERTS, NCAND])).then_inc(c_in, 16)
            sp.dma_start(wb1[:], d["wb1"]).then_inc(c_in, 16)
            sp.dma_start(wb2[:], d["wb2"]).then_inc(c_in, 16)

            def load1(turn, half):
                sp.dma_start(wbuf[:, half], d["w1"][bass.ds((2 * turn + half) * PER, PER), 0:C].rearrange("e c h -> c e h")
                             ).then_inc(w_in[half], 16)

            def load2(turn, half):
                for q in range(HC):
                    sp.dma_start(wbuf[:, half].rearrange("p e (q o) -> p e q o", q=HC)[:, :, q],
                                 d["w2"][bass.ds((2 * turn + half) * PER, PER), q * 128:(q + 1) * 128].rearrange(
                                     "e p o -> p e o")).then_inc(w_in[half], 16)
            for half in range(2):
                load1(0, half)
            sp.wait_ge(merged, MERGES)
            sp.dma_start(d["toks"].rearrange("o (e j) -> (o e) j", e=EXPERTS), toki[:].rearrange("p b k -> p (b k)")
                         ).then_inc(rows_out, 16)
            sp.dma_start(d["tokf"].rearrange("o (b k e) -> (o e) b k", b=B, k=TOPK), tok[:],
                         allow_slow_non_contiguous=True).then_inc(rows_out, 16)
            sp.wait_ge(rows_out, 32)
            sp.dma_start(tokrow[:], d["toks"]).then_inc(rows_in, 16)
            sp.dma_start(tokall[:].rearrange("p b k e -> p (b k e)"), d["tokf"].to_broadcast([EXPERTS, J])
                         ).then_inc(rows_in, 16)
            with sp.Fori(1, TURNS) as t:
                for half in range(2):
                    sp.wait_ge(hid_ready, 2 * t + half - 1)
                    load1(t, half)
            for half in range(2):
                sp.wait_ge(hid_ready, 2 * TURNS + half - 1)
                load2(0, half)
            with sp.Fori(1, TURNS) as t:
                for half in range(2):
                    sp.wait_ge(o_ready, 2 * t + half - 1)
                    load2(t, half)
            sp.wait_ge(new_ready, 1)
            with sp.Fori(0, EXPERTS) as e:
                put(sp, e, 0, range(TOPK), put_by_sp)
                wait_alone(sp, put_by_sp, 16 * TOPK * (e + 1), passed)

        @block.tensor
        def _(pe):
            mm = nc.tensor.matmul
            pe.wait_ge(pooled_ready, 1)
            for b in range(B):
                m = nc.tensor.transpose(ptr[:, b * EXPERTS:(b + 1) * EXPERTS], pooled_e[:, b], g["iden"][0:EXPERTS, 0:EXPERTS])
            m.then_inc(turned, 1)
            pe.wait_ge(pooled_ready, 2)

            with pe.Fori(0, TURNS) as t:
                for half in range(2):
                    pe.wait_ge(w_in[half], 16 * (t + 1))
                    for e in range(PER):
                        for q in range(HC):
                            ex = (2 * t + half) * PER + e
                            m = mm(pB[:, bass.ds((ex * HC + q) * B, B)], wbuf[:, half, e, q * 128:(q + 1) * 128],
                                   pooled[:, :, bass.ds(ex, 1)], start=True, stop=True)
                    m.then_inc(hid_ready, 1)
            pe.wait_ge(act_ready, 1)
            with pe.Fori(0, TURNS) as t:
                for half in range(2):
                    pe.wait_ge(w_in[half], 16 * (TURNS + HC * t + HC))
                    for e in range(PER):
                        ex = (2 * t + half) * PER + e
                        for q in range(HC):
                            m = mm(pA[:, bass.ds(ex * B, B)], wbuf[:, half, e, q * 128:(q + 1) * 128],
                                   hh[:, bass.ds(ex * HC + q, 1), :], start=(q == 0), stop=(q == HC - 1))
                    m.then_inc(o_ready, 1)
            pe.wait_ge(out_steps, 1)
            for b in range(B):
                m = nc.tensor.transpose(pB[0:EXPERTS, b * C:(b + 1) * C], ob[:, b], g["iden"][:])
            m.then_inc(turned, 1)
            for b in range(B):
                o = pN[:, b * TILE:(b + 1) * TILE]
                for k in range(TOPK):
                    pe.wait_ge(same_ready, b * TOPK + k + 1)
                    mm(o, wt[:, k % 2], same[:, k % 2], start=(k == 0), stop=False).then_inc(summed, 1)
                for k in range(TOPK):
                    m = mm(o[:, k * EXPERTS:(k + 1) * EXPERTS], xg[:, b * TOPK + k], g["iden"][0:EXPERTS, 0:EXPERTS],
                           start=False, stop=(k == TOPK - 1))
                m.then_inc(o_ready, 1)

        @block.scalar
        def _(act):
            load_ln_and_exp(act)
            a = nc.scalar.activation
            for b in range(B):
                act.wait_ge(merged, 2 + b * (3 + TOPK) + 3)
                heads = V[:].rearrange("p (b s) h k -> p b (s h) k", b=B)[:, b, :, 0]
                a(em[:, b], heads, ACT.Exp, bias=ntop[:, b:b + 1])
                a(pk[:, b], tv[:, b], ACT.Exp, bias=ntop[:, b:b + 1]).then_inc(em_ready, 1)
            act.wait_ge(centered, 1)
            a(sq[:], xh[:], ACT.Square).then_inc(squared, 1)
            act.wait_ge(var_ready, 1)
            a(var[:], var[:], ACT.Ln, bias=g["eps"][0:EXPERTS, 1:2], scale=1.0 / C).then_inc(ln_ready, 1)
            act.wait_ge(ln_ready, 1)
            a(rstd[:], var[:], ACT.Exp, scale=-0.5).then_inc(rstd_ready, 1)
            act.wait_ge(hb_ready, 1)
            a(hh[:], hb[:], ACT.Gelu).then_inc(act_ready, 1)
            act.wait_ge(new_ready, 3)
            put(act, 0, 1, range(TOPK), put_by_act)
            put(act, 0, 2, range(MINE), rest_by_act)
            with act.Fori(1, EXPERTS) as e:
                act.wait_ge(put_by_act, 16 * TOPK * e)
                put(act, e, 1, range(TOPK), put_by_act)
                act.wait_ge(rest_by_act, 16 * MINE * e)
                act.wait_ge(rest_by_pool, 16 * (TOPK - MINE) * e)
                put(act, e, 2, range(MINE), rest_by_act)
            act.wait_ge(put_by_act, 16 * TOPK * EXPERTS)
            act.wait_ge(rest_by_act, 16 * MINE * EXPERTS)

        @block.vector
        def _(dve):
            v = nc.vector
            n = [0]

            def chain(ins):
                ins.then_inc(merged, 1)
                n[0] += 1
                dve.wait_ge(merged, n[0])
            dve.wait_ge(c_in, 16 * 10)
            chain(v.tensor_tensor(TK[:].rearrange("p s h k -> p (s h k)"), TK[:].rearrange("p s h k -> p (s h k)"),
                                  off[:], ALU.add))
            for b in range(B):
                vb = V[:].rearrange("p (b s) h k -> p b (s h k)", b=B)[:, b]
                tb = TK[:].rearrange("p (b s) h k -> p b (s h k)", b=B)[:, b]
                chain(v.max(tv[:, b], vb))
                v.tensor_scalar(ntop[:, b:b + 1], tv[:, b, 0:1], -1.0, None, ALU.mult)
                chain(v.max_index(pos[:, b], tv[:, b], vb))
                chain(v.tensor_copy(posf[:, b], pos[:, b]))
                for k in range(TOPK):
                    chain(v.scalar_tensor_tensor(junk[:], iota[:], posf[:, b, k:k + 1], tb, ALU.is_equal, ALU.mult,
                                                 accum_out=tok[:, b, k:k + 1]))
            chain(v.tensor_copy(toki[:], tok[:]))
            chain(v.scalar_tensor_tensor(
                rowi[:], iota[:, 0:B].rearrange("p (b o) -> p b o", o=1).to_broadcast([EXPERTS, B, TOPK]), float(TOK),
                tok[:], ALU.mult, ALU.add))
            chain(v.memset(junk[:], 0.0))
            assert n[0] == MERGES
            dve.wait_ge(em_ready, B)
            chain(v.tensor_tensor(em[:], em[:], SM[:].rearrange("p (b s) h -> p b (s h)", b=B), ALU.mult))
            chain(v.tensor_reduce(zs[:], em[:], AX.X, ALU.add))
            chain(v.reciprocal(rz[:], zs[:]))
            chain(v.tensor_tensor(pk[:], pk[:], rz[:].rearrange("p (b o) -> p b o", o=1).to_broadcast([EXPERTS, B, TOPK]),
                                  ALU.mult))
            over_c = lambda x: x[:].rearrange("p (j o) -> p j o", o=1).to_broadcast([EXPERTS, BK, C])
            dve.wait_ge(got, 16 * BK)
            chain(v.tensor_reduce(mean[:], xg[:], AX.X, ALU.add))
            chain(v.tensor_scalar(mean[:], mean[:], 1.0 / C, None, ALU.mult))
            v.tensor_tensor(xh[:], xg[:], over_c(mean), ALU.subtract).then_inc(centered, 1)
            dve.wait_ge(squared, 1)
            v.tensor_reduce(var[:], sq[:], AX.X, ALU.add).then_inc(var_ready, 1)
            dve.wait_ge(rstd_ready, 1)
            chain(v.tensor_tensor(rstd[:], rstd[:], pk[:].rearrange("p b k -> p (b k)"), ALU.mult))
            chain(v.tensor_tensor(xh[:], xh[:], over_c(rstd), ALU.mult))
            v.tensor_reduce(pooled_e[:], xh[:].rearrange("p (b k) c -> p b c k", b=B), AX.X, ALU.add
                            ).then_inc(pooled_ready, 1)
            dve.wait_ge(turned, 1)
            v.tensor_copy(pooled[:].rearrange("p b e -> p (b e)"), ptr[:, 0:EB]).then_inc(pooled_ready, 1)
            dve.wait_ge(hid_ready, 2 * TURNS)
            v.tensor_tensor(hb[:], pB[:, 0:EB * HC].rearrange("p (h b) -> p h b", b=B),
                            wb1[:].rearrange("p e q -> p (e q)").rearrange("p (h o) -> p h o", o=1).to_broadcast(
                                [128, EXPERTS * HC, B]), ALU.add).then_inc(hb_ready, 1)
            dve.wait_ge(o_ready, 2 * TURNS)
            v.tensor_tensor(ob[:].rearrange("p b e -> p e b"), pA[:, 0:EB].rearrange("p (e b) -> p e b", b=B),
                            wb2[:].rearrange("p (e o) -> p e o", o=1).to_broadcast([128, EXPERTS, B]), ALU.add
                            ).then_inc(out_steps, 1)
            dve.wait_ge(turned, 2)
            v.tensor_copy(oe[:].rearrange("p b c -> p (b c)"), pB[0:EXPERTS, 0:B * C]).then_inc(out_steps, 1)
            dve.wait_ge(rows_in, 32)
            dve.wait_ge(out_steps, 2)
            for b in range(B):
                for k in range(TOPK):
                    wait(dve, summed, b * TOPK + k - 1)
                    v.tensor_scalar(same[:, k % 2], tokall[:, b].rearrange("p k e -> p (k e)"), tok[:, b, k:k + 1], None,
                                    ALU.is_equal)
                    v.tensor_scalar(wt[:, k % 2], oe[:, b], pk[:, b, k:k + 1], None, ALU.mult).then_inc(same_ready, 1)
                dve.wait_ge(o_ready, 2 * TURNS + b + 1)
                v.tensor_copy(new[:, b].rearrange("p k e -> p (k e)"), pN[:, b * TILE:(b + 1) * TILE]
                              ).then_inc(new_ready, 1)

        @block.gpsimd
        def _(pool):
            pool.wait_ge(merged, MERGES)
            for b in range(B):
                for k in range(TOPK):
                    pool.indirect_dma_start(xg[:, b * TOPK + k], None, d["x3t"].rearrange("s t c -> (s t) c"),
                                            bass.IndirectOffsetOnAxis(ap=rowi[:, b, k:k + 1], axis=0)).then_inc(got, 16)
            pool.wait_ge(rows_in, 32)
            pool.wait_ge(new_ready, B)
            put(pool, 0, 3, range(TOPK), put_by_pool)
            put(pool, 0, 2, range(MINE, TOPK), rest_by_pool)
            with pool.Fori(1, EXPERTS) as e:
                pool.wait_ge(put_by_pool, 16 * TOPK * e)
                put(pool, e, 3, range(TOPK), put_by_pool)
                pool.wait_ge(rest_by_pool, 16 * (TOPK - MINE) * e)
                pool.wait_ge(rest_by_act, 16 * MINE * e)
                put(pool, e, 2, range(MINE, TOPK), rest_by_pool)
            pool.wait_ge(put_by_pool, 16 * TOPK * EXPERTS)
            pool.wait_ge(rest_by_pool, 16 * (TOPK - MINE) * EXPERTS)


SCRATCH = {
    "x1s": ((WINDOWS, C, COLS * WIN), F32), "wxs": ((WINDOWS, C, COLS * WIN), F32),
    "rs": ((WINDOWS, C, COLS * WIN), F32), "ys": ((C, B, WINDOWS, PH * WIN // 2), F32),
    "y2s": ((C, B * (PH + 2), PH + 2), F32), "toks": ((1, B * EXPERTS * TOPK), I32),
    "tokf": ((1, B * EXPERTS * TOPK), F32), "x3t": ((SUPERS, STOK, C), F32),
}
EARLY_PARTS = {"qcWc_high": 2 * C, "qcWc_low": 2 * C, "cen_high": C, "ones_high": C}
EARLY = {"kvT": 2 * C, "kvb": 2 * C, "mask": C, "kvden": B * 2 * C, "bn": TILES * 6}
GLOBALS = {
    "cen": 128, "ones": 128, "projT": C, "VT": C, "cols": 4, "gateb": 1,
    "eps": 2, "qcWcGc": 2 * C + EXPERTS, "bnss": 3, "iden": 128,
}


def build(nc, d, phases=None):
    todo = (setup_phase, attention_sums, attention_pass, recurrence_and_norm, spectral, experts_scan, experts_apply)
    phases = phases or [f.__name__ for f in todo]
    d["xflat"] = d["x"].rearrange("b c h w -> c b (h w)")
    d["outflat"] = d["out"].rearrange("b c h w -> c b (h w)")
    with ExitStack() as ctx:
        def sb(name, cols):
            return ctx.enter_context(nc.sbuf_tensor("g_" + name, [128, cols], F32))
        g = {k: sb(k, v) for k, v in GLOBALS.items()}
        with ExitStack() as early:
            for k, v in EARLY.items():
                g[k] = early.enter_context(nc.sbuf_tensor("g_" + k, [128, v], F32))
            for k, v in EARLY_PARTS.items():
                g[k] = early.enter_context(nc.sbuf_tensor("g_" + k, [128, v], F32R))
            setup_phase(nc, d, g)
            for f in todo[1:3]:
                if f.__name__ in phases:
                    f(nc, d, g)
        for f in todo[3:5]:
            if f.__name__ in phases:
                f(nc, d, g)
        for k, v in (("cand", SUPERS * TOPK), ("candi", SUPERS * TOPK), ("cands", SUPERS)):
            g[k] = sb(k, v)
        for f in todo[5:]:
            if f.__name__ in phases:
                f(nc, d, g)


def constants():
    n = PH
    cen = np.eye(C) - 1.0 / C
    ones = np.full((C, C), 1.0 / C)
    mask = np.kron(np.eye(HEADS), np.ones((C // HEADS, C // HEADS)))
    k = np.arange(1, n // 2)
    i = np.arange(n)
    ang = 2 * np.pi * np.outer(i, i) / n
    cs, sn = np.cos(ang), np.sin(ang)
    rw = np.concatenate([cs[:, :1], cs[:, n // 2:n // 2 + 1], cs[:, k], -sn[:, k]], 1) / n
    b1 = np.concatenate([cs[:1], cs[n // 2:n // 2 + 1], 2 * cs[k], -2 * sn[k]], 0) / n
    b2 = np.concatenate([-2 * sn[k], -2 * cs[k], -cs[:1], -cs[n // 2:n // 2 + 1]], 0) / n
    dft = np.concatenate([rw, cs, -sn, sn, cs, b1, b2], 1)
    sups = SUPERS // B
    off = (np.arange(SUPERS)[:, None, None] % sups) * STOK + np.arange(2)[None, :, None] * (STOK // 2) + np.zeros((1, 1, TOPK))
    return {k: np.ascontiguousarray(v, dtype=np.float32) for k, v in dict(
        cen=cen, ones=ones, mask=mask, dft=dft, iden=np.eye(n), tokoff=off.reshape(1, -1),
        iota=np.arange(sups * 2 * TOPK)[None]).items()}


def lay_out(v):
    a = {k: np.asarray(x) for k, x in v.items()}
    w12 = np.zeros((128, 8, 128), np.float32)
    nb, bs = 8, 16
    for c in range(2):
        for k in range(nb):
            o = slice(k * bs, (k + 1) * bs)
            w12[o, c, o] = a["L1_conv_w1"][c, k].T
            w12[o, 2 + c, o] = a["L1_conv_w2"][c, k]
        w12[:, 4 + c] = a["L1_conv_b1"][c].reshape(-1)[:, None]
        w12[:, 6 + c] = a["L1_conv_b2"][c].reshape(-1)[None]
    w1, w2 = a["L1_ffn_weight1"], a["L1_ffn_weight2"]
    got = {
        "x": a["x"], "qT": a["L0_conv_q_w"].T, "kvT": a["L0_conv_kv_w"].T, "kvb": a["L0_conv_kv_b"][None],
        "projT": a["L0_conv_proj_w"].T, "WT": a["L0_ffn_W"].T, "VT": a["L0_ffn_V"].T,
        "gateT": a["L1_ffn_gate_w"].T, "gateb": np.concatenate([a["L1_ffn_gate_b"]] * 2)[:, None],
        "cols": np.stack([a["L0_conv_q_b"], a["L0_conv_proj_b"], a["L0_ffn_gamma"], a["L0_ffn_beta"]], 1),
        "w12": w12.reshape(128, -1), "w1": w1, "w2": w2,
        "wb1": w1[:, C].reshape(EXPERTS, HID // 128, 128).transpose(2, 0, 1), "wb2": w2[:, HID].T,
    }
    got = {k: np.ascontiguousarray(x) for k, x in got.items()}
    return {**got, **constants()}


def declare(nc, arrays, kinds=()):
    d = {k: nc.dram_tensor("in_" + k, list(a.shape), mybir.dt.from_np(a.dtype), kind="ExternalInput").ap()
         for k, a in arrays.items()}
    kinds = dict(kinds)
    for k, (shape, dt) in SCRATCH.items():
        d[k] = nc.dram_tensor("s_" + k, list(shape), dt, kind=kinds.get(k, "Internal")).ap()
    d["out"] = nc.dram_tensor("out_0_dram", [B, C, H, W], F32, kind=kinds.get("out", "ExternalOutput")).ap()
    return d


def kernel(**inputs):
    import concourse.bacc as bacc
    from concourse.bass_utils import run_bass_kernel_spmd

    arrays = lay_out(inputs)
    nc = bacc.Bacc("TRN2", target_bir_lowering=False, num_devices=1, dynamic_dma_scratch_size=2048)
    build(nc, declare(nc, arrays))
    r = run_bass_kernel_spmd(nc, [{"in_" + k: a for k, a in arrays.items()}], core_ids=[0])
    return r.results[0]["out_0_dram"]
```
